# Optimizing a Trainium2 kernel written in Bass

```python
import numpy as np
import jax
import jax.numpy as jnp

def _softmax(x, axis=-1):
    return jax.nn.softmax(x, axis=axis)

def _gelu(x):
    return jax.nn.gelu(x, approximate=True)

def _silu(x):
    return jax.nn.silu(x)

def _sigmoid(x):
    return jax.nn.sigmoid(x)

def _layernorm(x, axis=-1, eps=1e-05):
    m = jnp.mean(x, axis=axis, keepdims=True)
    v = jnp.var(x, axis=axis, keepdims=True)
    return (x - m) / jnp.sqrt(v + eps)

def _scatter_add(tgt, idx, src, axis=0):
    return tgt.at[idx].add(src)

def _segment_sum(src, seg, n):
    return jax.ops.segment_sum(src, seg, n)
kernel_name = 'mk_adaln_d1_jaxref_r4_cea15e'

def setup_inputs(seed: int=0):
    np.random.seed(seed)
    _w = jnp.asarray

    def _L0_attn_setup():
        import math
        import jax, jax.numpy as jnp
        import numpy as np
        B, T, D_MODEL = (4, 256, 256)
        N_HEADS = 16
        HEAD_DIM = D_MODEL // N_HEADS
        TOP_K = 64

        def _scatter_last(base, idx, vals):
            d = base.shape[-1]
            k = idx.shape[-1]
            fb = base.reshape(-1, d)
            fi = idx.reshape(-1, k)
            fv = vals.reshape(-1, k)
            rows = jnp.arange(fb.shape[0])[:, None]
            return fb.at[rows, fi].set(fv).reshape(base.shape)

        def _sparsify_last_dim_topk(x, keep_k):
            if keep_k >= x.shape[-1]:
                return x
            _, idx = jax.lax.top_k(jnp.abs(x), keep_k)
            vals = jnp.take_along_axis(x, idx, axis=-1)
            return _scatter_last(jnp.zeros_like(x), idx, vals)

        def _forward(x, wq, wk, wv, wo):
            Bx, Tx, C = x.shape
            k_keep = min(TOP_K, Tx)
            feature_keep = min(HEAD_DIM, max(1, math.ceil(HEAD_DIM * (k_keep / Tx))))

            def proj(w):
                y = jnp.einsum('btc,dc->btd', x, w)
                return y.reshape(Bx, Tx, N_HEADS, HEAD_DIM).transpose(0, 2, 1, 3)
            q = _sparsify_last_dim_topk(proj(wq), feature_keep)
            k = _sparsify_last_dim_topk(proj(wk), feature_keep)
            v = _sparsify_last_dim_topk(proj(wv), feature_keep)
            scores = jnp.einsum('bhqd,bhkd->bhqk', q, k) / math.sqrt(HEAD_DIM)
            causal = jnp.triu(jnp.ones((Tx, Tx), dtype=bool), k=1)
            neg_inf = jnp.float32(-jnp.inf)
            scores = jnp.where(causal[None, None], neg_inf, scores)
            topk_vals, topk_idx = jax.lax.top_k(scores, k_keep)
            sparse_scores = _scatter_last(jnp.full_like(scores, neg_inf), topk_idx, topk_vals)
            attn = jax.nn.softmax(sparse_scores, axis=-1)
            out = jnp.einsum('bhqk,bhkd->bhqd', attn, v)
            out = out.transpose(0, 2, 1, 3).reshape(Bx, Tx, C)
            return jnp.einsum('btc,dc->btd', out, wo)
        key = jax.random.key(seed)
        kx, kq, kk, kv, ko = jax.random.split(key, 5)
        scale = 0.02
        x = jax.random.normal(kx, (B, T, D_MODEL), dtype=jnp.float32)
        wq = jax.random.normal(kq, (D_MODEL, D_MODEL), dtype=jnp.float32) * scale
        wk = jax.random.normal(kk, (D_MODEL, D_MODEL), dtype=jnp.float32) * scale
        wv = jax.random.normal(kv, (D_MODEL, D_MODEL), dtype=jnp.float32) * scale
        wo = jax.random.normal(ko, (D_MODEL, D_MODEL), dtype=jnp.float32) * scale
        return {'x': x, 'wq': wq, 'wk': wk, 'wv': wv, 'wo': wo}
    _L0_attn_in = _L0_attn_setup()

    def _L0_ffn_setup():
        import jax, jax.numpy as jnp
        import numpy as np
        B, S, HID, DFF, E, K = (4, 512, 256, 1024, 8, 512)
        key = jax.random.key(seed)
        ks = jax.random.split(key, 4)
        sc_h = 1.0 / np.sqrt(HID)
        sc_f = 1.0 / np.sqrt(DFF)
        return {'x': jax.random.normal(ks[0], (B, S, HID), jnp.float32), 'router_w': jax.random.normal(ks[1], (HID, E), jnp.float32) * sc_h, 'router_b': jnp.zeros((E,), jnp.float32), 'w1': jax.random.normal(ks[2], (E, HID, DFF), jnp.float32) * sc_h, 'b1': jnp.zeros((E, DFF), jnp.float32), 'w2': jax.random.normal(ks[3], (E, DFF, HID), jnp.float32) * sc_f, 'b2': jnp.zeros((E, HID), jnp.float32)}
    _L0_ffn_in = _L0_ffn_setup()
    _L0_c = _w((lambda *s: np.random.randn(*s).astype(np.float32) * 0.05)(4, 256))
    _L0_wmod = _w((lambda *s: np.random.randn(*s).astype(np.float32) * 0.05)(256, 6 * 256) * 256 ** (-0.5))
    _d = {'L0_attn_x': _L0_attn_in['x'], 'L0_attn_wq': _L0_attn_in['wq'], 'L0_attn_wk': _L0_attn_in['wk'], 'L0_attn_wv': _L0_attn_in['wv'], 'L0_attn_wo': _L0_attn_in['wo'], 'L0_ffn_router_w': _L0_ffn_in['router_w'], 'L0_ffn_router_b': _L0_ffn_in['router_b'], 'L0_ffn_w1': _L0_ffn_in['w1'], 'L0_ffn_b1': _L0_ffn_in['b1'], 'L0_ffn_w2': _L0_ffn_in['w2'], 'L0_ffn_b2': _L0_ffn_in['b2'], 'L0_c': _L0_c, 'L0_wmod': _L0_wmod}
    _x0 = _d['L0_attn_x']
    _d['L0_attn_x'] = jax.random.normal(jax.random.fold_in(jax.random.key(seed), 1), (4, 1024, 256), dtype=_x0.dtype)
    del _x0
    return _d

def reference(L0_attn_x, L0_attn_wq, L0_attn_wk, L0_attn_wv, L0_attn_wo, L0_ffn_router_w, L0_ffn_router_b, L0_ffn_w1, L0_ffn_b1, L0_ffn_w2, L0_ffn_b2, L0_c, L0_wmod):

    def _L0_attn_ref(x, wq, wk, wv, wo):
        import math
        import jax, jax.numpy as jnp
        import numpy as np
        B, T, D_MODEL = (4, 256, 256)
        N_HEADS = 16
        HEAD_DIM = D_MODEL // N_HEADS
        TOP_K = 64

        def _scatter_last(base, idx, vals):
            d = base.shape[-1]
            k = idx.shape[-1]
            fb = base.reshape(-1, d)
            fi = idx.reshape(-1, k)
            fv = vals.reshape(-1, k)
            rows = jnp.arange(fb.shape[0])[:, None]
            return fb.at[rows, fi].set(fv).reshape(base.shape)

        def _sparsify_last_dim_topk(x, keep_k):
            if keep_k >= x.shape[-1]:
                return x
            _, idx = jax.lax.top_k(jnp.abs(x), keep_k)
            vals = jnp.take_along_axis(x, idx, axis=-1)
            return _scatter_last(jnp.zeros_like(x), idx, vals)

        def _forward(x, wq, wk, wv, wo):
            Bx, Tx, C = x.shape
            k_keep = min(TOP_K, Tx)
            feature_keep = min(HEAD_DIM, max(1, math.ceil(HEAD_DIM * (k_keep / Tx))))

            def proj(w):
                y = jnp.einsum('btc,dc->btd', x, w)
                return y.reshape(Bx, Tx, N_HEADS, HEAD_DIM).transpose(0, 2, 1, 3)
            q = _sparsify_last_dim_topk(proj(wq), feature_keep)
            k = _sparsify_last_dim_topk(proj(wk), feature_keep)
            v = _sparsify_last_dim_topk(proj(wv), feature_keep)
            scores = jnp.einsum('bhqd,bhkd->bhqk', q, k) / math.sqrt(HEAD_DIM)
            causal = jnp.triu(jnp.ones((Tx, Tx), dtype=bool), k=1)
            neg_inf = jnp.float32(-jnp.inf)
            scores = jnp.where(causal[None, None], neg_inf, scores)
            topk_vals, topk_idx = jax.lax.top_k(scores, k_keep)
            sparse_scores = _scatter_last(jnp.full_like(scores, neg_inf), topk_idx, topk_vals)
            attn = jax.nn.softmax(sparse_scores, axis=-1)
            out = jnp.einsum('bhqk,bhkd->bhqd', attn, v)
            out = out.transpose(0, 2, 1, 3).reshape(Bx, Tx, C)
            return jnp.einsum('btc,dc->btd', out, wo)
        return _forward(x, wq, wk, wv, wo)

    def _L0_ffn_ref(x, router_w, router_b, w1, b1, w2, b2):
        import jax, jax.numpy as jnp
        import numpy as np
        B, S, HID, DFF, E, K = (4, 512, 256, 1024, 8, 512)
        b, s, h = x.shape
        xf = x.reshape(-1, h)
        logits = xf @ router_w + router_b
        scores = jax.nn.softmax(logits, axis=-1)
        G, idx = jax.lax.top_k(scores.T, K)
        toks = xf[idx]
        h1 = jax.nn.relu(jnp.einsum('ekh,ehf->ekf', toks, w1) + b1[:, None, :])
        eo = jnp.einsum('ekf,efh->ekh', h1, w2) + b2[:, None, :]
        contrib = (eo * G[..., None]).reshape(-1, h)
        y = jnp.zeros_like(xf).at[idx.reshape(-1)].add(contrib)
        return y.reshape(b, s, h)
    x = L0_attn_x
    mod = (_silu(L0_c) @ L0_wmod).reshape(L0_c.shape[0], 6, 1, -1)
    sa, ca, ga, sb, cb, gb = (mod[:, 0], mod[:, 1], mod[:, 2], mod[:, 3], mod[:, 4], mod[:, 5])
    ga = (2 * (ga >= 0) - 1) * jnp.maximum(jnp.abs(ga), 0.25)
    gb = (2 * (gb >= 0) - 1) * jnp.maximum(jnp.abs(gb), 0.25)
    h = _layernorm(x, axis=-1) * (1 + ca) + sa
    x = x + ga * _L0_attn_ref(h, L0_attn_wq, L0_attn_wk, L0_attn_wv, L0_attn_wo)
    h = _layernorm(x, axis=-1) * (1 + cb) + sb
    x = x + gb * _L0_ffn_ref(h, L0_ffn_router_w, L0_ffn_router_b, L0_ffn_w1, L0_ffn_b1, L0_ffn_w2, L0_ffn_b2)
    return x

_drawn_inputs = setup_inputs


def setup_inputs(seed=0):
    import zlib

    import numpy as np

    out = dict(_drawn_inputs(seed))
    spreads = {'L0_ffn_router_b': (0.0, 0.8), 'L0_ffn_b1': (0.0, 0.8), 'L0_ffn_b2': (0.0, 0.8)}
    factors = {'L0_attn_wq': 8.0, 'L0_attn_wk': 8.0, 'L0_attn_wv': 8.0, 'L0_attn_wo': 8.0}
    for name, (base, spread) in spreads.items():
        noise = np.random.default_rng([zlib.crc32(name.encode()), seed]).standard_normal(out[name].shape)
        drawn = base * np.exp(spread * noise) if base else spread * noise
        out[name] = jnp.asarray(drawn.astype(out[name].dtype))
    for name, factor in factors.items():
        out[name] = (out[name] * factor).astype(out[name].dtype)
    return out
```

```python
from contextlib import ExitStack

import concourse.bass as bass
from concourse import mybir

ALU = mybir.AluOpType
ACT = mybir.ActivationFunctionType
AX = mybir.AxisListType
F32 = mybir.dt.float32
BF16 = mybir.dt.bfloat16
I32 = mybir.dt.int32
U32 = mybir.dt.uint32

P = 128
B, T, D = 4, 1024, 256
N = B * T
NT = T // P
NTALL = N // P
KD = D // P
NH, HD = 16, 16
HG = 4
NG = NH // HG
TOPK = 64
E, DFF, CAP = 8, 1024, 512
FO = DFF // P
CC = CAP // P
ROW = D + E
BIG = 1.0e30
TAKEN = -3.0e38
EPS = 1e-5


def build_kernel(nc, x, wq, wk, wv, wo, router_w, router_b, w1, b1, w2, b2, c, wmod, out):
    with ExitStack() as ctx:
        def sb(name, shape, dt=F32):
            return ctx.enter_context(nc.sbuf_tensor(name, shape, dt))

        def sem(name):
            return ctx.enter_context(nc.semaphore(name))

        out_rows = out.rearrange("b t d -> (b t) d")
        h_table = nc.dram_tensor("h_table", [N, ROW], F32, kind="Internal").ap()
        gb_table = nc.dram_tensor("gb_table", [B, D], F32, kind="Internal").ap()

        ps = ctx.enter_context(nc.psum_tensor("ps", [P, 8, 512], F32))

        stand = sb("stand", [P, 1])
        stand_p = sb("stand_p", [P, 1])
        ident = sb("ident", [P, P])
        ones_f = sb("ones_f", [P, P])
        first_of = sb("first_of", [P, NH * 3, HD], BF16)
        causal = sb("causal", [P, 15 * P])
        same_e = sb("same_e", [P, P])
        before_e = sb("before_e", [P, P])
        e_of_q = sb("e_of_q", [P, E])
        iota_lo = sb("iota_lo", [P, 32])
        iota_hi = sb("iota_hi", [P, 16])
        p_col = sb("p_col", [P, 1])
        tile_no = sb("tile_no", [P, NTALL], BF16)
        bit_u = sb("bit_u", [P, 30], U32)
        bit_f = sb("bit_f", [P, 30])

        probs = sb("probs", [P, NTALL, E])
        ids = sb("ids", [P, E, CC], U32)
        bat = sb("bat", [P, E, CC], U32)
        b1_t = sb("b1_t", [P, E * FO])
        b2_sb = sb("b2_sb", [1, E, D])
        att = ExitStack()

        def sba(name, shape, dt=F32):
            return att.enter_context(nc.sbuf_tensor(name, shape, dt))

        w_nat = sba("w_nat", [P, 4, KD, D])
        w_t = sba("w_t", [P, KD, 3 * D])
        wo_t = sba("wo_t", [P, KD, D])
        wo_ga = sba("wo_ga", [P, KD, D])
        wmod_sb = sba("wmod_sb", [P, KD, 6 * D])
        c_sb = sba("c_sb", [B, D])
        c_sig = sba("c_sig", [B, D])
        c_t = sba("c_t", [P, KD, B])
        mod_t = sba("mod_t", [P, 6, KD, B])
        mod_b = sba("mod_b", [P, 6, KD])
        mod_rows = sba("mod_rows", [B, 3 * D])
        g_abs = sba("g_abs", [P, 2 * KD * B])
        g_row = sba("g_row", [B, D])
        g_row2 = sba("g_row2", [B, D])
        pick_b = sba("pick_b", [B, P])
        rw_sb = sba("rw_sb", [P, KD, E])
        rb_sb = sba("rb_sb", [1, E])

        x_in = sba("x_in", [P, NT, D])
        x_res = sba("x_res", [P, NT, D])
        st = sba("st", [P, NT, 6])
        mv = sba("mv", [P, NT, 2])
        var_e = sba("var_e", [P, NT])
        half_neg = sba("half_neg", [P, NT])
        rstd = sba("rstd", [P, NT])
        h_t = sba("h_t", [P, 2, KD, P])
        y_abs = sba("y_abs", [P, 2, 3 * NH, HD])
        y_val = sba("y_val", [P, 2, 3 * NH, HD])
        y_max = sba("y_max", [P, 3 * NH])
        y_eq = sba("y_eq", [P, 3 * NH, HD], BF16)
        y_ord = sba("y_ord", [P, 3 * NH, HD], BF16)
        y_first = sba("y_first", [P, 3 * NH], BF16)
        y_one = sba("y_one", [P, 2, 3 * NH, HD], BF16)
        qkv = sba("qkv", [P, NT, 3, NH, HD])
        q_st = sba("q_st", [P, NT, HG, 2, HD])
        k_st = sba("k_st", [P, NT, HG, 2, HD])
        v_st = sba("v_st", [P, NT, HG, HD + 1])
        q_rows = sba("q_rows", [P, T])
        k_rows = sba("k_rows", [P, T])
        q_tile = sba("q_tile", [P, P])
        sc = sba("sc", [P, T])
        work = sba("work", [P, T])
        top8 = sba("top8", [P, TOPK])
        neg_m = sba("neg_m", [P, 1])
        prob = sba("prob", [P, T])
        prob_t = sba("prob_t", [P, NT, P])
        z_inv = sba("z_inv", [P, 1])
        o_tok = sba("o_tok", [P, NT, NH, HD])
        o_t = sba("o_t", [P, 2, KD, P])
        x2 = sba("x2", [P, NT, D])
        bc = sba("bc", [P, 2 * D])
        h2p = sba("h2p", [P, NT, ROW])
        logit = sba("logit", [P, NT, E])
        l_max = sba("l_max", [P, NT])

        s_const, s_w, s_wload = sem("s_const"), sem("s_w"), sem("s_wload")
        s_pe_pro, s_ev_pro, s_tab = sem("s_pe_pro"), sem("s_ev_pro"), sem("s_tab")

        with nc.Block() as blk:
            @blk.sync
            def _(sp):
                for i, w in enumerate((wq, wk, wv, wo)):
                    sp.dma_start(w_nat[:, i, :, :], w.rearrange("(k p) c -> p k c", p=P)).then_inc(s_wload, 16)
                sp.dma_start(c_sb[:, :], c).then_inc(s_wload, 16)
                sp.dma_start(wmod_sb[:, :, :], wmod.rearrange("(k p) m -> p k m", p=P)).then_inc(s_wload, 16)
                sp.dma_start(rw_sb[:, :, :], router_w.rearrange("(k p) e -> p k e", p=P)).then_inc(s_wload, 16)
                sp.dma_start(rb_sb[:, :], router_b.rearrange("(o e) -> o e", o=1)).then_inc(s_wload, 16)
                sp.wait_ge(s_wload, 16 * 8)
                sp.wait_ge(s_w, 3)
                sp.dma_start(gb_table, mod_rows[:, 2 * D:3 * D]).then_inc(s_tab, 16)
                sp.wait_ge(s_tab, 16)

            @blk.gpsimd
            def _(pool):
                pool.memset(ones_f[:, :], 1.0)
                pool.memset(ident[:, :], 0.0)
                pool.memset(causal[:, :], 0.0)
                pool.memset(half_neg[:, :], -0.5)
                pool.memset(v_st[:, :, :, :], 1.0)
                pool.iota(first_of[:, :, :], [[0, 3 * NH], [-1, HD]], base=HD, channel_multiplier=0,
                          allow_small_or_imprecise_dtypes=True)
                pool.iota(iota_lo[:, :], [[1, 32]], base=0, channel_multiplier=0,
                          allow_small_or_imprecise_dtypes=True)
                pool.iota(iota_hi[:, :], [[1, 16]], base=0, channel_multiplier=0,
                          allow_small_or_imprecise_dtypes=True)
                pool.iota(p_col[:, :], [[0, 1]], base=0, channel_multiplier=1,
                          allow_small_or_imprecise_dtypes=True)
                pool.iota(tile_no[:, :], [[P, NTALL]], base=0, channel_multiplier=0,
                          allow_small_or_imprecise_dtypes=True)
                for k in range(30):
                    pool.memset(bit_u[:, k:k + 1], 1 << (29 - k))
                    pool.memset(bit_f[:, k:k + 1], float(1 << (29 - k)))
                pool.drain()
                pool.affine_select(ident[:, :], ident[:, :], [[-1, P]], ALU.not_equal, 1.0, base=0,
                                   channel_multiplier=1)
                pool.affine_select(causal[:, :], causal[:, :], [[-1, 15 * P]], ALU.is_ge, -BIG, base=7 * P,
                                   channel_multiplier=1)
                pool.drain().then_inc(s_const, 1)
                pool.wait_ge(s_const, 2)
                pool.affine_select(before_e[:, :], same_e[:, :], [[1, P]], ALU.is_gt, 0.0, base=0,
                                   channel_multiplier=-1)
                pool.drain().then_inc(s_const, 1)

            @blk.vector
            def _(dve):
                dve.wait_ge(s_const, 1)
                dve.tensor_reduce(e_of_q[:, :], ident[:, :].rearrange("p (a e) -> p e a", e=E), AX.X, ALU.add)
                dve.drain()
                dve.tensor_copy(same_e[:, :].rearrange("p (a e) -> p a e", e=E),
                                e_of_q[:, :].unsqueeze(1).to_broadcast([P, P // E, E]))
                dve.drain().then_inc(s_const, 1)
                dve.wait_ge(s_ev_pro, 1)
                dve.tensor_scalar(c_sig[:, :], c_sig[:, :], 1.0, None, ALU.add)
                dve.drain()
                dve.reciprocal(c_sig[:, :], c_sig[:, :])
                dve.drain()
                dve.tensor_tensor(c_sig[:, :], c_sig[:, :], c_sb[:, :], ALU.mult)
                dve.drain().then_inc(s_w, 1)
                dve.wait_ge(s_pe_pro, 1)
                dve.tensor_copy(c_t[:, :, :], ps[:, 0, 0:KD * B].rearrange("p (k b) -> p k b", k=KD))
                dve.drain().then_inc(s_w, 1)
                for w in range(3):
                    dve.wait_ge(s_pe_pro, 2 + w)
                    dve.tensor_copy(w_t[:, :, w * D:(w + 1) * D], ps[:, 1 + w, :].rearrange("p (k d) -> p k d", k=KD))
                dve.wait_ge(s_pe_pro, 5)
                dve.tensor_copy(mod_t[:, :, :, :], ps[:, 4, 0:6 * KD * B].rearrange("p (j k b) -> p j k b", j=6, k=KD))
                dve.tensor_copy(mod_rows[:, 0:2 * D], ps[0:B, 5, :])
                dve.tensor_copy(g_row[:, :], ps[0:B, 6, 0:D])
                dve.drain()
                for g, out_g, tmp in ((mod_t[:, 2, :, :].rearrange("p k b -> p (k b)"), None, g_abs),
                                      (g_row[:, :], mod_rows[:, 2 * D:3 * D], g_row2)):
                    n = KD * B if out_g is None else D
                    a = tmp[:, 0:n]
                    dve.scalar_tensor_tensor(a, g, -1.0, g, ALU.mult, ALU.max)
                    dve.drain()
                    s = tmp[:, n:2 * n] if out_g is None else c_sig[:, :]
                    dve.tensor_scalar(s, g, 0.0, 2.0, ALU.is_ge, ALU.mult)
                    dve.tensor_scalar(a, a, 0.25, None, ALU.max)
                    dve.drain()
                    dve.scalar_tensor_tensor(g if out_g is None else out_g, s, -1.0, a, ALU.add, ALU.mult)
                for j in (1, 4):
                    v = mod_t[:, j, :, :].rearrange("p k b -> p (k b)")
                    dve.tensor_scalar(v, v, 1.0, None, ALU.add)
                dve.tensor_scalar(mod_rows[:, D:2 * D], mod_rows[:, D:2 * D], 1.0, None, ALU.add)
                dve.drain().then_inc(s_w, 1)

            @blk.scalar
            def _(act):
                act.wait_ge(s_wload, 16 * 8)
                act.activation(c_sig[:, :], c_sb[:, :], ACT.Exp, scale=-1.0)
                act.drain().then_inc(s_ev_pro, 1)

            @blk.tensor
            def _(pe):
                pe.wait_ge(s_const, 1)
                pe.wait_ge(s_w, 1)
                for k in range(KD):
                    m = pe.transpose(ps[:, 0, k * B:(k + 1) * B], c_sig[:, k * P:(k + 1) * P], ident[0:B, 0:B])
                m.then_inc(s_pe_pro, 1)
                pe.wait_ge(s_wload, 16 * 8)
                for w in range(3):
                    for k in range(KD):
                        for h in range(KD):
                            m = pe.transpose(ps[:, 1 + w, k * D + h * P:k * D + (h + 1) * P],
                                             w_nat[:, w, h, k * P:(k + 1) * P], ident[:, :])
                    m.then_inc(s_pe_pro, 1)
                pe.wait_ge(s_w, 2)
                for m6 in range(6 * KD):
                    for k in range(KD):
                        pe.matmul(ps[:, 4, m6 * B:(m6 + 1) * B], wmod_sb[:, k, m6 * P:(m6 + 1) * P], c_t[:, k, :],
                                  start=k == 0, stop=k == KD - 1)
                for bank, lo, n in ((5, 3 * D, 2 * D), (6, 5 * D, D)):
                    for k in range(KD):
                        m = pe.matmul(ps[0:B, bank, 0:n], c_t[:, k, :], wmod_sb[:, k, lo:lo + n],
                                      start=k == 0, stop=k == KD - 1)
                m.then_inc(s_pe_pro, 1)

        s_x, s_xr = sem("s_x"), sem("s_xr")
        s_x_free, s_xr_free = sem("s_x_free"), sem("s_xr_free")
        s_var, s_rstd = sem("s_var"), sem("s_rstd")
        s_xhat, s_xT, s_hT, s_qkv = sem("s_xhat"), sem("s_xT"), sem("s_hT"), sem("s_qkv")
        s_yev, s_one, s_keep = sem("s_yev"), sem("s_one"), sem("s_keep")
        s_stage, s_rT, s_rows, s_qt = sem("s_stage"), sem("s_rT"), sem("s_rows"), sem("s_qt")
        s_S, s_m, s_p, s_pk, s_pT, s_pts, s_O = (sem(n) for n in
                                                ("s_S", "s_m", "s_p", "s_pk", "s_pT", "s_pts", "s_O"))
        s_otok, s_oT, s_oev, s_Y, s_x2 = (sem(n) for n in ("s_otok", "s_oT", "s_oev", "s_Y", "s_x2"))
        s_modb, s_woga, s_woT, s_wot, s_bc = (sem(n) for n in ("s_modb", "s_woga", "s_woT", "s_wot", "s_bc"))
        s_h2, s_h2T, s_h2ev, s_log, s_lm, s_lexp = (sem(n) for n in
                                                    ("s_h2", "s_h2T", "s_h2ev", "s_log", "s_lm", "s_lexp"))
        s_pr, s_out, s_bcev, s_var2, s_rstd2 = (sem(n) for n in ("s_pr", "s_out", "s_bcev", "s_var2", "s_rstd2"))

        x_v = x.rearrange("b (n p) d -> b p n d", p=P)
        out_v = out.rearrange("b (n p) d -> b p n d", p=P)
        h_v = h_table.rearrange("(b n p) d -> b p n d", b=B, p=P)

        def row(t, n):
            return t.rearrange("b p n d -> (b p) n d")

        with nc.Block() as blk:
            @blk.sync
            def _(sp):
                with sp.Fori(0, B) as b:
                    sp.wait_ge(s_x_free, b + 1)
                    sp.dma_start(x_in[:, :, :], x_v[bass.ds(b, 1)].rearrange("o p n d -> (o p) n d")).then_inc(s_x, 16)
                    sp.wait_ge(s_xr_free, NT * b + 1)
                    sp.dma_start(x_res[:, :, :], x_v[bass.ds(b, 1)].rearrange("o p n d -> (o p) n d")).then_inc(s_xr, 16)
                    sp.wait_ge(s_x2, b + 1)
                    sp.dma_start(out_v[bass.ds(b, 1)].rearrange("o p n d -> (o p) n d"), x2[:, :, :]).then_inc(s_out, 16)
                    sp.wait_ge(s_pr, b + 1)
                    sp.dma_start(h_v[bass.ds(b, 1)].rearrange("o p n d -> (o p) n d"), h2p[:, :, :]).then_inc(s_out, 16)
                sp.wait_ge(s_out, 32 * B)

            @blk.gpsimd
            def _(pool):
                with pool.Fori(0, B) as b:
                    pool.wait_ge(s_var, b + 1)
                    pool.tensor_tensor(rstd[:, :], var_e[:, :], half_neg[:, :], ALU.pow)
                    pool.drain().then_inc(s_rstd, 1)
                    for t in range(NT):
                        pool.wait_ge(s_one, NT * b + t + 1)
                        if t == 0:
                            pool.wait_ge(s_otok, b + 1)
                        pool.tensor_tensor(qkv[:, t].rearrange("p j h d -> p (j h) d"), y_val[:, t % 2],
                                           y_one[:, t % 2], ALU.mult).then_inc(s_keep, 1)
                    pool.wait_ge(s_var2, b + 1)
                    pool.tensor_tensor(rstd[:, :], var_e[:, :], half_neg[:, :], ALU.pow)
                    pool.drain().then_inc(s_rstd2, 1)

            @blk.scalar
            def _(act):
                with act.Fori(0, B) as b:
                    for t in range(NT):
                        act.wait_ge(s_qkv, NT * b + t + 1)
                        y = ps[:, 2 + 2 * (t % 2):4 + 2 * (t % 2), :].rearrange("p a b -> p (a b)")[:, 0:3 * D]
                        if t >= 2:
                            act.wait_ge(s_keep, NT * b + t - 1)
                        act.activation(y_abs[:, t % 2].rearrange("p h d -> p (h d)"), y, ACT.Abs)
                        act.activation(y_val[:, t % 2].rearrange("p h d -> p (h d)"), y, ACT.Copy).then_inc(s_yev, 1)
                    with act.Fori(0, NG) as g:
                        gi = b * NG + g
                        act.wait_ge(s_rT, gi + 1)
                        act.activation(q_rows[:, :], ps[:, 0:2, :].rearrange("p a b -> p (a b)"), ACT.Copy)
                        act.activation(k_rows[:, :], ps[:, 2:4, :].rearrange("p a b -> p (a b)"),
                                       ACT.Copy).then_inc(s_rows, 1)
                        with act.Fori(0, NT) as i:
                            for j in range(HG):
                                u = (gi * NT + i) * HG + j
                                act.wait_ge(s_m, u + 1)
                                act.activation(prob[:, :], sc[:, :], ACT.Exp, scale=0.25,
                                               bias=neg_m[:, :]).then_inc(s_p, 1)
                                act.wait_ge(s_pT, u + 1)
                                act.activation(prob_t[:, :, :].rearrange("p a b -> p (a b)"),
                                               ps[:, 6:8, :].rearrange("p a b -> p (a b)"), ACT.Copy).then_inc(s_pts, 1)
                    for t in range(NT):
                        act.wait_ge(s_oT, NT * b + t + 1)
                        act.activation(o_t[:, t % 2].rearrange("p k t -> p (k t)"), ps[:, t % 2, 0:KD * P],
                                       ACT.Copy).then_inc(s_oev, 1)
                    for t in range(NT):
                        act.wait_ge(s_h2T, NT * b + t + 1)
                        act.activation(h_t[:, t % 2].rearrange("p k t -> p (k t)"), ps[:, 4 + t % 2, 0:KD * P],
                                       ACT.Copy).then_inc(s_h2ev, 1)
                    act.wait_ge(s_lm, b + 1)
                    act.activation(logit[:, :, :], logit[:, :, :], ACT.Exp).then_inc(s_lexp, 1)

            @blk.tensor
            def _(pe):
                with pe.Fori(0, B) as b:
                    pe.wait_ge(s_woga, b + 1)
                    for k in range(KD):
                        for h in range(KD):
                            m = pe.transpose(ps[:, 6, k * D + h * P:k * D + (h + 1) * P],
                                             wo_ga[:, h, k * P:(k + 1) * P], ident[:, :])
                    m.then_inc(s_woT, 1)
                    pe.matmul(ps[:, 7, :], pick_b[:, :], mod_rows[:, 0:2 * D], start=True, stop=True).then_inc(s_bc, 1)

                    def turn(t):
                        pe.wait_ge(s_xhat, NT * b + t + 1)
                        for k in range(KD):
                            m = pe.transpose(ps[:, t % 2, k * P:(k + 1) * P], x_in[:, t, k * P:(k + 1) * P], ident[:, :])
                        m.then_inc(s_xT, 1)

                    turn(0)
                    for t in range(NT):
                        if t + 1 < NT:
                            turn(t + 1)
                        pe.wait_ge(s_hT, NT * b + t + 1)
                        if t >= 2:
                            pe.wait_ge(s_yev, NT * b + t - 1)
                        for bank, lo, n in ((0, 0, 2 * D), (1, 2 * D, D)):
                            for k in range(KD):
                                m = pe.matmul(ps[:, 2 + 2 * (t % 2) + bank, 0:n], h_t[:, t % 2, k, :],
                                              w_t[:, k, lo:lo + n], start=k == 0, stop=k == KD - 1)
                        m.then_inc(s_qkv, 1)
                    with pe.Fori(0, NG) as g:
                        gi = b * NG + g
                        pe.wait_ge(s_stage, gi + 1)
                        for bank, src in ((0, q_st), (2, k_st)):
                            for t in range(NT):
                                m = pe.transpose(ps[:, bank + t // 4, (t % 4) * P:(t % 4 + 1) * P],
                                                 src[:, t].rearrange("p h s d -> p (h s d)"), ident[:, :])
                        m.then_inc(s_rT, 1)
                        with pe.Fori(0, NT) as i:
                            pe.wait_ge(s_qt, gi * NT + i + 1)
                            for j in range(HG):
                                u = (gi * NT + i) * HG + j
                                r = slice(32 * j, 32 * j + 32)
                                for half in range(2):
                                    m = pe.matmul(ps[:, 4 + half, :], q_tile[r, :], k_rows[r, 512 * half:512 * half + 512],
                                                  start=True, stop=True)
                                m.then_inc(s_S, 1)
                                pe.wait_ge(s_pk, u + 1)
                                for t in range(NT):
                                    m = pe.transpose(ps[:, 6 + t // 4, (t % 4) * P:(t % 4 + 1) * P],
                                                     prob[:, t * P:(t + 1) * P], ident[:, :])
                                m.then_inc(s_pT, 1)
                                pe.wait_ge(s_pts, u + 1)
                                for t in range(NT):
                                    m = pe.matmul(ps[:, 0, 0:HD + 1], prob_t[:, t, :], v_st[:, t, j, :],
                                                  start=t == 0, stop=t == NT - 1)
                                m.then_inc(s_O, 1)

                    def turn_o(t):
                        if t == 0:
                            pe.wait_ge(s_otok, b + 2)
                        if t >= 2:
                            pe.wait_ge(s_oev, NT * b + t - 1)
                        for k in range(KD):
                            m = pe.transpose(ps[:, t % 2, k * P:(k + 1) * P],
                                             o_tok[:, t].rearrange("p h d -> p (h d)")[:, k * P:(k + 1) * P], ident[:, :])
                        m.then_inc(s_oT, 1)

                    turn_o(0)
                    for t in range(NT):
                        if t + 1 < NT:
                            turn_o(t + 1)
                        pe.wait_ge(s_oev, NT * b + t + 1)
                        if t >= 2:
                            pe.wait_ge(s_xr_free, NT * b + t)
                        for k in range(KD):
                            m = pe.matmul(ps[:, 2 + t % 2, 0:D], o_t[:, t % 2, k, :], wo_t[:, k, :],
                                          start=k == 0, stop=k == KD - 1)
                        m.then_inc(s_Y, 1)

                    def turn_h(t):
                        pe.wait_ge(s_h2, NT * b + t + 1)
                        if t >= 2:
                            pe.wait_ge(s_h2ev, NT * b + t - 1)
                        for k in range(KD):
                            m = pe.transpose(ps[:, 4 + t % 2, k * P:(k + 1) * P], h2p[:, t, k * P:(k + 1) * P], ident[:, :])
                        m.then_inc(s_h2T, 1)

                    turn_h(0)
                    for t in range(NT):
                        if t + 1 < NT:
                            turn_h(t + 1)
                        pe.wait_ge(s_h2ev, NT * b + t + 1)
                        lo = ps[:, 6, t * E:(t + 1) * E]
                        for k in range(KD):
                            pe.matmul(lo, h_t[:, t % 2, k, :], rw_sb[:, k, :], start=k == 0, stop=False)
                        m = pe.matmul(lo, ones_f[0:1, :], rb_sb[:, :], start=False, stop=True)
                    m.then_inc(s_log, 1)

            @blk.vector
            def _(dve):
                dve.sem_inc(s_x_free, 1)
                dve.sem_inc(s_xr_free, 1)
                dve.sem_inc(s_otok, 1)
                with dve.Fori(0, B) as b:
                    dve.tensor_copy(mod_b[:, :, :], mod_t[:, :, :, bass.ds(b, 1)].rearrange("p j k o -> p j (k o)"))
                    dve.tensor_copy(pick_b[:, :], ident[0:B, bass.ds(b, 1)].to_broadcast([B, P]))
                    dve.drain()
                    for k in range(KD):
                        dve.tensor_scalar(wo_ga[:, k, :], w_nat[:, 3, k, :], mod_b[:, 2, k:k + 1], None, ALU.mult)
                    dve.drain().then_inc(s_woga, 1)
                    dve.wait_ge(s_x, 16 * (b + 1))
                    for t in range(NT):
                        dve.bn_stats(st[:, t, :], x_in[:, t, :])
                    dve.drain()
                    for t in range(NT):
                        dve.bn_aggr(mv[:, t, :], st[:, t, :])
                    dve.drain()
                    dve.tensor_scalar(var_e[:, :], mv[:, :, 1], EPS, None, ALU.add)
                    dve.drain().then_inc(s_var, 1)
                    dve.wait_ge(s_woT, b + 1)
                    dve.tensor_copy(wo_t[:, :, :], ps[:, 6, :].rearrange("p (k d) -> p k d", k=KD))
                    dve.wait_ge(s_bc, b + 1)
                    dve.tensor_copy(bc[:, :], ps[:, 7, :])
                    dve.wait_ge(s_rstd, b + 1)
                    for t in range(NT):
                        dve.tensor_scalar(x_in[:, t, :], x_in[:, t, :], mv[:, t, 0:1], rstd[:, t:t + 1],
                                          ALU.subtract, ALU.mult).then_inc(s_xhat, 1)
                    for t in range(NT):
                        dve.wait_ge(s_xT, NT * b + t + 1)
                        if t >= 2:
                            dve.wait_ge(s_qkv, NT * b + t - 1)
                        for k in range(KD):
                            m = dve.tensor_scalar(h_t[:, t % 2, k, :], ps[:, t % 2, k * P:(k + 1) * P],
                                                  mod_b[:, 1, k:k + 1], mod_b[:, 0, k:k + 1], ALU.mult, ALU.add)
                        m.then_inc(s_hT, 1)
                        dve.wait_ge(s_yev, NT * b + t + 1)
                        a = y_abs[:, t % 2]
                        dve.tensor_reduce(y_max[:, :], a, AX.X, ALU.max)
                        dve.drain()
                        dve.tensor_tensor(y_eq[:, :, :], a, y_max[:, :].unsqueeze(2).to_broadcast([P, 3 * NH, HD]),
                                          ALU.is_equal)
                        dve.drain()
                        dve.tensor_tensor(y_ord[:, :, :], y_eq[:, :, :], first_of[:, :, :], ALU.mult)
                        dve.drain()
                        dve.tensor_reduce(y_first[:, :], y_ord[:, :, :], AX.X, ALU.max)
                        dve.drain()
                        dve.tensor_tensor(y_one[:, t % 2], y_ord[:, :, :],
                                          y_first[:, :].unsqueeze(2).to_broadcast([P, 3 * NH, HD]),
                                          ALU.is_equal)
                        dve.drain().then_inc(s_one, 1)
                    dve.drain().then_inc(s_x_free, 1)
                    dve.wait_ge(s_keep, NT * (b + 1))
                    dve.memset(stand[:, :], 0.0)
                    with dve.Fori(0, NG) as g:
                        gi = b * NG + g
                        hs = bass.ds(g * HG, HG)
                        dve.tensor_copy(q_st[:, :, :, 0, :], qkv[:, :, 0, hs, :])
                        dve.tensor_scalar(q_st[:, :, :, 1, :], qkv[:, :, 0, hs, :], -1.0, None, ALU.mult)
                        dve.tensor_scalar(k_st[:, :, :, 0, :], qkv[:, :, 1, hs, :], 0.0, None, ALU.max)
                        dve.tensor_scalar(k_st[:, :, :, 1, :], qkv[:, :, 1, hs, :], -1.0, 0.0, ALU.mult, ALU.max)
                        dve.tensor_copy(v_st[:, :, :, 0:HD], qkv[:, :, 2, hs, :])
                        dve.drain().then_inc(s_stage, 1)
                        with dve.Fori(0, NT) as i:
                            dve.wait_ge(s_rows, gi + 1)
                            dve.tensor_copy(q_tile[:, :], q_rows[:, bass.ds(i * P, P)])
                            dve.drain().then_inc(s_qt, 1)
                            for j in range(HG):
                                u = (gi * NT + i) * HG + j
                                dve.wait_ge(s_S, u + 1)
                                dve.memset(stand[:, :], 0.0)
                                dve.tensor_tensor(sc[:, :], ps[:, 4:6, :].rearrange("p a b -> p (a b)"),
                                                  causal[:, bass.ds((7 - i) * P, T)], ALU.add)
                                dve.drain()
                                for r in range(TOPK // 8):
                                    src = sc if r == 0 else work
                                    dve.max(top8[:, 8 * r:8 * r + 8], src[:, :])
                                    dve.drain()
                                    if r == 0:
                                        dve.tensor_scalar(neg_m[:, :], top8[:, 0:1], -0.25, None, ALU.mult)
                                        dve.drain().then_inc(s_m, 1)
                                    dve.match_replace(work[:, :], top8[:, 8 * r:8 * r + 8], src[:, :], TAKEN)
                                    dve.drain()
                                dve.wait_ge(s_p, u + 1)
                                dve.scalar_tensor_tensor(prob[:, :], work[:, :], TAKEN, prob[:, :], ALU.is_equal,
                                                         ALU.mult)
                                dve.drain().then_inc(s_pk, 1)
                                dve.wait_ge(s_O, u + 1)
                                dve.reciprocal(z_inv[:, :], ps[:, 0, HD:HD + 1])
                                dve.drain()
                                dve.tensor_scalar(o_tok[:, bass.ds(i, 1), bass.ds(g * HG + j, 1), :].rearrange(
                                    "p a b d -> p (a b d)"), ps[:, 0, 0:HD], z_inv[:, :], None, ALU.mult)
                    dve.drain().then_inc(s_otok, 1)
                    dve.wait_ge(s_xr, 16 * (b + 1))
                    for t in range(NT):
                        dve.wait_ge(s_Y, NT * b + t + 1)
                        dve.tensor_tensor(x2[:, t, :], ps[:, 2 + t % 2, 0:D], x_res[:, t, :],
                                          ALU.add).then_inc(s_xr_free, 1)
                    dve.drain().then_inc(s_x2, 1)
                    for t in range(NT):
                        dve.bn_stats(st[:, t, :], x2[:, t, :])
                    dve.drain()
                    for t in range(NT):
                        dve.bn_aggr(mv[:, t, :], st[:, t, :])
                    dve.drain()
                    dve.tensor_scalar(var_e[:, :], mv[:, :, 1], EPS, None, ALU.add)
                    dve.drain().then_inc(s_var2, 1)
                    dve.wait_ge(s_rstd2, b + 1)
                    for t in range(NT):
                        h = h2p[:, t, 0:D]
                        dve.tensor_scalar(h, x2[:, t, :], mv[:, t, 0:1], rstd[:, t:t + 1], ALU.subtract, ALU.mult)
                        dve.drain()
                        dve.tensor_tensor(h, h, bc[:, D:2 * D], ALU.mult)
                        dve.drain()
                        dve.tensor_tensor(h, h, bc[:, 0:D], ALU.add)
                        dve.drain().then_inc(s_h2, 1)
                    dve.wait_ge(s_log, b + 1)
                    lg = ps[:, 6, 0:NT * E].rearrange("p (n e) -> p n e", e=E)
                    dve.tensor_reduce(l_max[:, :], lg, AX.X, ALU.max)
                    dve.drain()
                    dve.tensor_tensor(logit[:, :, :], lg, l_max[:, :].unsqueeze(2).to_broadcast([P, NT, E]), ALU.subtract)
                    dve.drain().then_inc(s_lm, 1)
                    dve.wait_ge(s_lexp, b + 1)
                    dve.tensor_reduce(l_max[:, :], logit[:, :, :], AX.X, ALU.add)
                    dve.drain()
                    dve.reciprocal(l_max[:, :], l_max[:, :])
                    dve.drain()
                    dve.tensor_tensor(h2p[:, :, D:ROW], logit[:, :, :], l_max[:, :].unsqueeze(2).to_broadcast([P, NT, E]),
                                      ALU.mult)
                    dve.drain()
                    dve.tensor_copy(probs[:, bass.ds(b * NT, NT), :], h2p[:, :, D:ROW])
                    dve.drain().then_inc(s_pr, 1)
                    dve.wait_ge(s_out, 32 * (b + 1))

        att.close()
        w1_sb = sb("w1_sb", [P, 2, KD, DFF])
        w2_sb = sb("w2_sb", [P, 2, FO, D])
        sel = ExitStack()

        def sbs(name, shape, dt=F32):
            return sel.enter_context(nc.sbuf_tensor(name, shape, dt))

        gate_q = sbs("gate_q", [P, 2, P])
        junk = sbs("junk", [P, 2 * P], BF16)
        zeros = sbs("zeros", [P, P])
        thr = sbs("thr", [P, 1], U32)
        cand = sbs("cand", [P, 1], U32)
        step_u = sbs("step_u", [P, 1], U32)
        cnt = sbs("cnt", [P, 1])
        cnt2 = sbs("cnt2", [P, 2])
        need = sbs("need", [P, 1])
        start2 = sbs("start2", [P, 2])
        above = sbs("above", [P, 2, P])
        equal = sbs("equal", [P, 2, P])
        rank = sbs("rank", [P, 2, P])
        slot = sbs("slot", [P, NTALL, E])
        slot_i = sbs("slot_i", [P, 2, NTALL, E], I32)
        slot_f = sbs("slot_f", [P, 2, NTALL, E])
        oh_lo = sbs("oh_lo", [P, NTALL, E, 32], BF16)
        oh_hi = sbs("oh_hi", [P, NTALL, E, 2, 16], BF16)
        ids_f = sbs("ids_f", [32, E, 2, 16])
        b1_nat = sbs("b1_nat", [E * FO, P])
        s_gT, s_gq, s_cnt, s_tot = sem("s_gT"), sem("s_gq"), sem("s_cnt"), sem("s_tot")
        s_c2, s_off, s_sel, s_slT, s_oh, s_ids, s_idx = (sem(n) for n in
                                                        ("s_c2", "s_off", "s_sel", "s_slT", "s_oh", "s_ids", "s_idx"))
        s_b, s_b1T, s_b1 = sem("s_b"), sem("s_b1T"), sem("s_b1")

        with nc.Block() as blk:
            @blk.sync
            def _(sp):
                sp.dma_start(b1_nat[:, :], b1.rearrange("e (o p) -> (e o) p", p=P)).then_inc(s_b, 16)
                sp.dma_start(b2_sb[:, :, :], b2.rearrange("(o e) d -> o e d", o=1)).then_inc(s_b, 16)
                sp.wait_ge(s_b, 32)

            @blk.scalar
            def _(act):
                act.wait_ge(s_gT, 1)
                act.activation(gate_q[:, :, :], ps[:, 0, 0:2 * P].rearrange("p (a b) -> p a b", a=2),
                               ACT.Copy).then_inc(s_gq, 1)
                act.wait_ge(s_b1T, 1)
                act.activation(b1_t[:, :], ps[:, 1, 0:E * FO], ACT.Copy).then_inc(s_b1, 1)

            @blk.tensor
            def _(pe):
                flat = probs[:, :, :].rearrange("p n e -> p (n e)")
                for a in range(2):
                    m = pe.transpose(ps[:, 0, a * P:(a + 1) * P], flat[:, a * P:(a + 1) * P], ident[:, :])
                m.then_inc(s_gT, 1)
                pe.wait_ge(s_b, 32)
                pe.transpose(ps[:, 1, 0:E * FO], b1_nat[:, :], ident[0:E * FO, 0:E * FO]).then_inc(s_b1T, 1)
                with pe.Fori(0, 30) as k:
                    pe.wait_ge(s_cnt, k + 1)
                    pe.matmul(ps[:, 2, 0:1], same_e[:, :], cnt[:, :], start=True, stop=True).then_inc(s_tot, 1)
                for r in range(2):
                    pe.wait_ge(s_c2, r + 1)
                    pe.matmul(ps[:, 3, 0:1], same_e[:, :], cnt[:, :], start=True, stop=True)
                    pe.matmul(ps[:, 3, 1:3], before_e[:, :], cnt2[:, :], start=True, stop=True)
                    pe.matmul(ps[:, 3, 3:4], same_e[:, :], cnt2[:, 0:1], start=True, stop=True).then_inc(s_off, 1)
                pe.wait_ge(s_sel, 1)
                for a in range(2):
                    m = pe.transpose(ps[:, 4, a * P:(a + 1) * P], rank[:, a, :], ident[:, :])
                m.then_inc(s_slT, 1)
                pe.wait_ge(s_oh, 1)
                for e in range(E):
                    for n in range(NTALL):
                        m = pe.matmul(ps[0:32, 5, e * 32:(e + 1) * 32], oh_lo[:, n, e, :],
                                      oh_hi[:, n, e].rearrange("p a h -> p (a h)"), start=n == 0, stop=n == NTALL - 1)
                m.then_inc(s_ids, 1)

            @blk.vector
            def _(dve):
                dve.memset(thr[:, :], 0)
                dve.memset(zeros[:, :], 0.0)
                dve.wait_ge(s_gq, 1)
                gates = gate_q[:, :, :].rearrange("p a b -> p (a b)")
                dve.drain()
                with dve.Fori(0, 30) as k:
                    dve.tensor_tensor(cand[:, :], thr[:, :], bit_u[:, bass.ds(k, 1)], ALU.bitwise_or)
                    dve.drain()
                    dve.tensor_scalar(junk[:, :], gates, cand[:, :].bitcast(F32), None, ALU.is_ge, ALU.add,
                                      accum_out=cnt[:, :])
                    dve.drain().then_inc(s_cnt, 1)
                    dve.wait_ge(s_tot, k + 1)
                    dve.tensor_scalar(step_u[:, :], ps[:, 2, 0:1], float(CAP), bit_f[:, bass.ds(k, 1)], ALU.is_ge,
                                      ALU.mult)
                    dve.drain()
                    dve.tensor_tensor(thr[:, :], thr[:, :], step_u[:, :], ALU.bitwise_or)
                    dve.drain()
                t = thr[:, :].bitcast(F32)
                dve.tensor_scalar(above[:, :, :].rearrange("p a b -> p (a b)"), gates, t, None, ALU.is_gt)
                dve.tensor_scalar(equal[:, :, :].rearrange("p a b -> p (a b)"), gates, t, None, ALU.is_equal)
                dve.drain()
                for r, src in ((0, equal), (1, above)):
                    if r == 0:
                        dve.tensor_reduce(cnt[:, :], above[:, :, :], AX.XY, ALU.add)
                    dve.tensor_reduce(cnt2[:, :], src[:, :, :], AX.X, ALU.add)
                    dve.drain().then_inc(s_c2, 1)
                    dve.wait_ge(s_off, r + 1)
                    dve.tensor_copy(start2[:, :], ps[:, 3, 1:3])
                    dve.tensor_scalar(need[:, :], ps[:, 3, 0:1], -1.0, float(CAP), ALU.mult, ALU.add)
                    dve.drain()
                    dve.tensor_tensor(start2[:, 1:2], start2[:, 1:2], ps[:, 3, 3:4], ALU.add)
                    dve.drain()
                    for a in range(2):
                        dve.tensor_tensor_scan(rank[:, a, :], src[:, a, :], zeros[:, :], start2[:, a:a + 1], ALU.add,
                                               ALU.max)
                    dve.drain()
                    if r == 0:
                        dve.scalar_tensor_tensor(equal[:, :, :], rank[:, :, :], need[:, :], equal[:, :, :], ALU.is_le,
                                                 ALU.mult)
                        dve.drain()
                        dve.tensor_tensor(above[:, :, :], above[:, :, :], equal[:, :, :], ALU.add)
                        dve.drain()
                dve.scalar_tensor_tensor(rank[:, :, :], rank[:, :, :], -1025.0, above[:, :, :], ALU.add, ALU.mult)
                dve.drain()
                dve.tensor_scalar(rank[:, :, :], rank[:, :, :], 1024.0, None, ALU.add)
                dve.drain().then_inc(s_sel, 1)
                dve.wait_ge(s_slT, 1)
                dve.tensor_copy(slot_i[:, 0].rearrange("p n e -> p (n e)"), ps[:, 4, 0:2 * P])
                dve.drain()
                dve.tensor_scalar(slot_i[:, 1], slot_i[:, 0], 31, None, ALU.bitwise_and)
                dve.drain()
                dve.tensor_scalar(slot_i[:, 0], slot_i[:, 0], 5, None, ALU.logical_shift_right)
                dve.drain()
                dve.tensor_copy(slot_f[:, :, :, :], slot_i[:, :, :, :])
                dve.drain()
                for e in range(E):
                    dve.tensor_tensor(oh_lo[:, :, e, :], slot_f[:, 1, :, e].unsqueeze(2).to_broadcast([P, NTALL, 32]),
                                      iota_lo[:, :].unsqueeze(1).to_broadcast([P, NTALL, 32]), ALU.is_equal)
                    dve.tensor_tensor(oh_hi[:, :, e, 0, :], slot_f[:, 0, :, e].unsqueeze(2).to_broadcast([P, NTALL, 16]),
                                      iota_hi[:, :].unsqueeze(1).to_broadcast([P, NTALL, 16]), ALU.is_equal)
                dve.drain()
                for e in range(E):
                    dve.tensor_tensor(oh_hi[:, :, e, 1, :], oh_hi[:, :, e, 0, :],
                                      tile_no[:, :].unsqueeze(2).to_broadcast([P, NTALL, 16]), ALU.mult)
                dve.drain()
                for e in range(E):
                    dve.tensor_scalar(oh_hi[:, :, e, 0, :], oh_hi[:, :, e, 0, :], p_col[:, :], None, ALU.mult)
                dve.drain().then_inc(s_oh, 1)
                dve.wait_ge(s_ids, 1)
                dve.tensor_copy(ids_f[:, :, :, :].rearrange("p e a h -> p (e a h)"), ps[0:32, 5, 0:E * 32])
                dve.drain()
                dve.tensor_tensor(ids_f[:, :, 0, :], ids_f[:, :, 0, :], ids_f[:, :, 1, :], ALU.add)
                dve.drain()
                for q in range(CC):
                    dve.tensor_copy(ids[32 * q:32 * q + 32, :, :],
                                    ids_f[:, :, 0, :].rearrange("p e (c q) -> p e c q", q=4)[:, :, :, q])
                dve.drain()
                dve.tensor_scalar(bat[:, :, :], ids[:, :, :], 10, None, ALU.logical_shift_right)
                dve.drain().then_inc(s_idx, 1)

        sel.close()
        idx_e = sb("idx_e", [P, 2, CC], U32)
        bat_e = sb("bat_e", [P, 2, CC], U32)
        tok = sb("tok", [P, 2, CC, ROW])
        gbk = sb("gbk", [P, 2, CC, D])
        tok_t = sb("tok_t", [P, KD, CAP])
        gate = sb("gate", [P, 2, CC])
        b1_e = sb("b1_e", [P, FO])
        b2_e = sb("b2_e", [1, D])
        h1_t = sb("h1_t", [P, FO, CAP])
        ctr = sb("ctr", [P, 2, CC, D])
        s_w12 = [sem("s_w12_0"), sem("s_w12_1")]
        s_ie, s_g0, s_g1, s_tT, s_tt = (sem(n) for n in ("s_ie", "s_g0", "s_g1", "s_tT", "s_tt"))
        s_g = [s_g0, s_g1]
        s_L1, s_h1, s_L2, s_ctr, s_sc, s_be = (sem(n) for n in ("s_L1", "s_h1", "s_L2", "s_ctr", "s_sc", "s_be"))

        with nc.Block() as blk:
            @blk.sync
            def _(sp):
                with sp.Fori(0, E // 2) as ep:
                    for a in range(2):
                        e = 2 * ep + a
                        sp.wait_ge(s_L2, CC * e + 1)
                        sp.dma_start(w1_sb[:, a], w1[bass.ds(e, 1)].rearrange("o (k p) f -> p (o k) f", p=P)).then_inc(s_w12[a], 16)
                        sp.dma_start(w2_sb[:, a], w2[bass.ds(e, 1)].rearrange("o (k p) f -> p (o k) f", p=P)).then_inc(s_w12[a], 16)

            @blk.gpsimd
            def _(pool):
                with pool.Fori(0, E // 2) as ep:
                    for a in range(2):
                        e = 2 * ep + a
                        pool.tensor_copy(idx_e[:, a, :], ids[:, bass.ds(e, 1), :].rearrange("p o c -> p (o c)"))
                        pool.tensor_copy(bat_e[:, a, :], bat[:, bass.ds(e, 1), :].rearrange("p o c -> p (o c)"))
                        pool.drain()
                        for k in range(CC):
                            pool.indirect_dma_start(tok[:, a, k, :], None, h_table,
                                                    bass.IndirectOffsetOnAxis(idx_e[:, a, k:k + 1], 0)).then_inc(s_g[a], 16)
                            pool.indirect_dma_start(gbk[:, a, k, :], None, gb_table,
                                                    bass.IndirectOffsetOnAxis(bat_e[:, a, k:k + 1], 0)).then_inc(s_g[a], 16)
                        for k in range(CC):
                            pool.wait_ge(s_ctr, CC * e + k + 1)
                            pool.tensor_tensor(stand_p[:, :], ones_f[:, 0:1], ones_f[:, 0:1], ALU.add)
                            pool.drain()
                            pool.indirect_dma_start(out_rows, bass.IndirectOffsetOnAxis(idx_e[:, a, k:k + 1], 0),
                                                    ctr[:, a, k, :], None, compute_op=ALU.add).then_inc(s_sc, 16)
                        pool.wait_ge(s_sc, 16 * CC * (e + 1))
                        pool.tensor_tensor(stand_p[:, :], ones_f[:, 0:1], ones_f[:, 0:1], ALU.add)
                        pool.drain()

            @blk.tensor
            def _(pe):
                with pe.Fori(0, E // 2) as ep:
                    for a in range(2):
                        e = 2 * ep + a
                        pe.wait_ge(s_g[a], 32 * CC * (ep + 1))
                        for k in range(KD):
                            for q in range(CC):
                                m = pe.transpose(ps[:, k, q * P:(q + 1) * P], tok[:, a, q, k * P:(k + 1) * P], ident[:, :])
                        m.then_inc(s_tT, 1)
                        pe.wait_ge(s_tt, e + 1)
                        pe.wait_ge(s_w12[a], 32 * (ep + 1))
                        for f in range(FO):
                            if f >= 2:
                                pe.wait_ge(s_h1, FO * e + f - 1)
                            for k in range(KD):
                                m = pe.matmul(ps[:, 2 + f % 2, :], w1_sb[:, a, k, f * P:(f + 1) * P], tok_t[:, k, :],
                                              start=k == 0, stop=k == KD - 1)
                            m.then_inc(s_L1, 1)
                        pe.wait_ge(s_h1, FO * (e + 1))
                        for q in range(CC):
                            if q >= 2:
                                pe.wait_ge(s_ctr, CC * e + q - 1)
                            for f in range(FO):
                                pe.matmul(ps[:, 4 + q % 2, 0:D], h1_t[:, f, q * P:(q + 1) * P], w2_sb[:, a, f, :],
                                          start=f == 0, stop=False)
                            pe.matmul(ps[:, 4 + q % 2, 0:D], ones_f[0:1, :], b2_e[:, :], start=False,
                                      stop=True).then_inc(s_L2, 1)

            @blk.scalar
            def _(act):
                with act.Fori(0, E // 2) as ep:
                    for a in range(2):
                        e = 2 * ep + a
                        act.wait_ge(s_be, e + 1)
                        for f in range(FO):
                            act.wait_ge(s_L1, FO * e + f + 1)
                            act.activation(h1_t[:, f, :], ps[:, 2 + f % 2, :], ACT.Relu,
                                           bias=b1_e[:, f:f + 1]).then_inc(s_h1, 1)

            @blk.vector
            def _(dve):
                dve.drain().then_inc(s_L2, 1)
                with dve.Fori(0, E // 2) as ep:
                    for a in range(2):
                        e = 2 * ep + a
                        dve.wait_ge(s_tT, e + 1)
                        dve.tensor_copy(tok_t[:, :, :], ps[:, 0:2, :]).then_inc(s_tt, 1)
                        dve.tensor_copy(b1_e[:, :], b1_t[:, bass.ds(e * FO, FO)])
                        dve.tensor_copy(b2_e[:, :], b2_sb[:, bass.ds(e, 1), :].rearrange("p o d -> p (o d)"))
                        dve.tensor_copy(gate[:, a, :], tok[:, a, :, bass.ds(D + e, 1)].rearrange("p c o -> p (c o)"))
                        dve.drain().then_inc(s_be, 1)
                        for q in range(CC):
                            dve.wait_ge(s_L2, CC * e + q + 2)
                            dve.scalar_tensor_tensor(ctr[:, a, q, :], ps[:, 4 + q % 2, 0:D], gate[:, a, q:q + 1],
                                                     gbk[:, a, q, :], ALU.mult, ALU.mult).then_inc(s_ctr, 1)


_INS = ["L0_attn_x", "L0_attn_wq", "L0_attn_wk", "L0_attn_wv", "L0_attn_wo", "L0_ffn_router_w", "L0_ffn_router_b",
        "L0_ffn_w1", "L0_ffn_b1", "L0_ffn_w2", "L0_ffn_b2", "L0_c", "L0_wmod"]
_OUTS = [((B, T, D), "float32")]


def kernel(**inputs):
    import numpy as _np
    import concourse.bacc as _bacc
    from concourse import mybir as _mybir
    from concourse.bass_utils import run_bass_kernel_spmd as _run

    nc = _bacc.Bacc("TRN2", target_bir_lowering=False, num_devices=1)
    arrays, args = {}, []
    for name in _INS:
        a = _np.ascontiguousarray(inputs[name])
        arrays[f"in_{name}_dram"] = a
        args.append(nc.dram_tensor(f"in_{name}_dram", a.shape, _mybir.dt.from_np(a.dtype), kind="ExternalInput").ap())
    for i, (shape, dtype) in enumerate(_OUTS):
        dt = _mybir.dt.from_np(_np.dtype(dtype))
        args.append(nc.dram_tensor(f"out_{i}_dram", shape, dt, kind="ExternalOutput").ap())
    build_kernel(nc, *args)
    r = _run(nc, [arrays], core_ids=[0])
    return r.results[0]["out_0_dram"]
```

```python
from contextlib import ExitStack

import concourse.bass as bass
from concourse import mybir

ALU = mybir.AluOpType
ACT = mybir.ActivationFunctionType
AX = mybir.AxisListType
F32 = mybir.dt.float32
BF16 = mybir.dt.bfloat16
I32 = mybir.dt.int32
U32 = mybir.dt.uint32

P = 128
B, T, D = 4, 1024, 256
N = B * T
NT = T // P
NTALL = N // P
KD = D // P
NH, HD = 16, 16
HG = 4
NG = NH // HG
TOPK = 64
E, DFF, CAP = 8, 1024, 512
FO = DFF // P
CC = CAP // P
ROW = D + E
BIG = 1.0e30
TAKEN = -3.0e38
EPS = 1e-5


def build_kernel(nc, x, wq, wk, wv, wo, router_w, router_b, w1, b1, w2, b2, c, wmod, out):
    with ExitStack() as ctx:
        def sb(name, shape, dt=F32):
            return ctx.enter_context(nc.sbuf_tensor(name, shape, dt))

        def sem(name):
            return ctx.enter_context(nc.semaphore(name))

        out_rows = out.rearrange("b t d -> (b t) d")
        h_table = nc.dram_tensor("h_table", [N, ROW], F32, kind="Internal").ap()
        gb_table = nc.dram_tensor("gb_table", [B, D], F32, kind="Internal").ap()

        ps = ctx.enter_context(nc.psum_tensor("ps", [P, 8, 512], F32))

        stand = sb("stand", [P, 1])
        stand_p = sb("stand_p", [P, 1])
        ident = sb("ident", [P, P])
        ones_f = sb("ones_f", [P, P])
        first_of = sb("first_of", [P, HD], BF16)
        same_e = sb("same_e", [P, P])
        before_e = sb("before_e", [P, P])
        e_of_q = sb("e_of_q", [P, E])
        iota_lo = sb("iota_lo", [P, 32])
        iota_hi = sb("iota_hi", [P, 16])
        p_col = sb("p_col", [P, 1])
        tile_no = sb("tile_no", [P, NTALL], BF16)
        bit_u = sb("bit_u", [P, 30], U32)
        bit_f = sb("bit_f", [P, 30])

        bad_f = sb("bad_f", [1, 1], I32)
        probs = sb("probs", [P, NTALL, E])
        ids = sb("ids", [P, E, CC], U32)
        bat = sb("bat", [P, E, CC], U32)
        b1_t = sb("b1_t", [P, E * FO])
        att = ExitStack()

        def sba(name, shape, dt=F32):
            return att.enter_context(nc.sbuf_tensor(name, shape, dt))

        wo_nat = sba("wo_nat", [P, KD, D])
        half_neg = sba("half_neg", [P, NT])
        w_t = sba("w_t", [P, KD, 3 * D])
        wo_t = sba("wo_t", [P, KD, D])
        mod_t = sba("mod_t", [P, 6, KD, B])
        mod_b = sba("mod_b", [P, 6, KD])
        mod_rows = sba("mod_rows", [B, 3 * D])
        pick_b = sba("pick_b", [B, P])
        rw_sb = sba("rw_sb", [P, KD, E])
        rb_sb = sba("rb_sb", [1, E])

        pro = ExitStack()

        def spr(name, shape, dt=F32):
            return pro.enter_context(nc.sbuf_tensor(name, shape, dt))

        w_nat = spr("w_nat", [P, 3, KD, D])
        wmod_sb = spr("wmod_sb", [P, KD, 6 * D])
        c_sb = spr("c_sb", [B, D])
        c_sig = spr("c_sig", [B, D])
        c_t = spr("c_t", [P, KD, B])
        g_abs = spr("g_abs", [P, 2 * KD * B])
        g_row = spr("g_row", [B, D])
        g_row2 = spr("g_row2", [B, D])

        s_const, s_w, s_wload = sem("s_const"), sem("s_w"), sem("s_wload")
        s_pe_pro, s_ev_pro, s_tab = sem("s_pe_pro"), sem("s_ev_pro"), sem("s_tab")

        with nc.Block() as blk:
            @blk.sync
            def _(sp):
                for i, w in enumerate((wq, wk, wv)):
                    sp.dma_start(w_nat[:, i, :, :], w.rearrange("(k p) c -> p k c", p=P)).then_inc(s_wload, 16)
                sp.dma_start(wo_nat[:, :, :], wo.rearrange("(k p) c -> p k c", p=P)).then_inc(s_wload, 16)
                sp.dma_start(c_sb[:, :], c).then_inc(s_wload, 16)
                sp.dma_start(wmod_sb[:, :, :], wmod.rearrange("(k p) m -> p k m", p=P)).then_inc(s_wload, 16)
                sp.dma_start(rw_sb[:, :, :], router_w.rearrange("(k p) e -> p k e", p=P)).then_inc(s_wload, 16)
                sp.dma_start(rb_sb[:, :], router_b.rearrange("(o e) -> o e", o=1)).then_inc(s_wload, 16)
                sp.wait_ge(s_wload, 16 * 8)
                sp.wait_ge(s_w, 3)
                sp.dma_start(gb_table, mod_rows[:, 2 * D:3 * D]).then_inc(s_tab, 16)
                sp.wait_ge(s_tab, 16)

            @blk.gpsimd
            def _(pool):
                pool.memset(ones_f[:, :], 1.0)
                pool.memset(ident[:, :], 0.0)
                pool.memset(half_neg[:, :], -0.5)
                pool.iota(first_of[:, :], [[-1, HD]], base=HD, channel_multiplier=0,
                          allow_small_or_imprecise_dtypes=True)
                pool.iota(iota_lo[:, :], [[1, 32]], base=0, channel_multiplier=0,
                          allow_small_or_imprecise_dtypes=True)
                pool.iota(iota_hi[:, :], [[1, 16]], base=0, channel_multiplier=0,
                          allow_small_or_imprecise_dtypes=True)
                pool.iota(p_col[:, :], [[0, 1]], base=0, channel_multiplier=1,
                          allow_small_or_imprecise_dtypes=True)
                pool.iota(tile_no[:, :], [[P, NTALL]], base=0, channel_multiplier=0,
                          allow_small_or_imprecise_dtypes=True)
                for k in range(30):
                    pool.memset(bit_u[:, k:k + 1], 1 << (29 - k))
                    pool.memset(bit_f[:, k:k + 1], float(1 << (29 - k)))
                pool.drain()
                pool.affine_select(ident[:, :], ident[:, :], [[-1, P]], ALU.not_equal, 1.0, base=0,
                                   channel_multiplier=1)
                pool.drain().then_inc(s_const, 1)
                pool.wait_ge(s_const, 2)
                pool.affine_select(before_e[:, :], same_e[:, :], [[1, P]], ALU.is_gt, 0.0, base=0,
                                   channel_multiplier=-1)
                pool.drain().then_inc(s_const, 1)

            @blk.vector
            def _(dve):
                dve.wait_ge(s_const, 1)
                dve.tensor_reduce(e_of_q[:, :], ident[:, :].rearrange("p (a e) -> p e a", e=E), AX.X, ALU.add)
                dve.drain()
                dve.tensor_copy(same_e[:, :].rearrange("p (a e) -> p a e", e=E),
                                e_of_q[:, :].unsqueeze(1).to_broadcast([P, P // E, E]))
                dve.drain().then_inc(s_const, 1)
                dve.wait_ge(s_ev_pro, 1)
                dve.tensor_scalar(c_sig[:, :], c_sig[:, :], 1.0, None, ALU.add)
                dve.drain()
                dve.reciprocal(c_sig[:, :], c_sig[:, :])
                dve.drain()
                dve.tensor_tensor(c_sig[:, :], c_sig[:, :], c_sb[:, :], ALU.mult)
                dve.drain().then_inc(s_w, 1)
                dve.wait_ge(s_pe_pro, 1)
                dve.tensor_copy(c_t[:, :, :], ps[:, 0, 0:KD * B].rearrange("p (k b) -> p k b", k=KD))
                dve.drain().then_inc(s_w, 1)
                for w in range(3):
                    dve.wait_ge(s_pe_pro, 2 + w)
                    dve.tensor_copy(w_t[:, :, w * D:(w + 1) * D], ps[:, 1 + w, :].rearrange("p (k d) -> p k d", k=KD))
                dve.wait_ge(s_pe_pro, 5)
                dve.tensor_copy(mod_t[:, :, :, :], ps[:, 4, 0:6 * KD * B].rearrange("p (j k b) -> p j k b", j=6, k=KD))
                dve.tensor_copy(mod_rows[:, 0:2 * D], ps[0:B, 5, :])
                dve.tensor_copy(g_row[:, :], ps[0:B, 6, 0:D])
                dve.drain()
                for g, out_g, tmp in ((mod_t[:, 2, :, :].rearrange("p k b -> p (k b)"), None, g_abs),
                                      (g_row[:, :], mod_rows[:, 2 * D:3 * D], g_row2)):
                    n = KD * B if out_g is None else D
                    a = tmp[:, 0:n]
                    dve.scalar_tensor_tensor(a, g, -1.0, g, ALU.mult, ALU.max)
                    dve.drain()
                    s = tmp[:, n:2 * n] if out_g is None else c_sig[:, :]
                    dve.tensor_scalar(s, g, 0.0, 2.0, ALU.is_ge, ALU.mult)
                    dve.tensor_scalar(a, a, 0.25, None, ALU.max)
                    dve.drain()
                    dve.scalar_tensor_tensor(g if out_g is None else out_g, s, -1.0, a, ALU.add, ALU.mult)
                for j in (1, 4):
                    v = mod_t[:, j, :, :].rearrange("p k b -> p (k b)")
                    dve.tensor_scalar(v, v, 1.0, None, ALU.add)
                dve.tensor_scalar(mod_rows[:, D:2 * D], mod_rows[:, D:2 * D], 1.0, None, ALU.add)
                dve.drain().then_inc(s_w, 1)

            @blk.scalar
            def _(act):
                act.wait_ge(s_wload, 16 * 8)
                act.activation(c_sig[:, :], c_sb[:, :], ACT.Exp, scale=-1.0)
                act.drain().then_inc(s_ev_pro, 1)

            @blk.tensor
            def _(pe):
                pe.wait_ge(s_const, 1)
                pe.wait_ge(s_w, 1)
                for k in range(KD):
                    m = pe.transpose(ps[:, 0, k * B:(k + 1) * B], c_sig[:, k * P:(k + 1) * P], ident[0:B, 0:B])
                m.then_inc(s_pe_pro, 1)
                pe.wait_ge(s_wload, 16 * 8)
                for w in range(3):
                    for k in range(KD):
                        for h in range(KD):
                            m = pe.transpose(ps[:, 1 + w, k * D + h * P:k * D + (h + 1) * P],
                                             w_nat[:, w, h, k * P:(k + 1) * P], ident[:, :])
                    m.then_inc(s_pe_pro, 1)
                pe.wait_ge(s_w, 2)
                for m6 in range(6 * KD):
                    for k in range(KD):
                        pe.matmul(ps[:, 4, m6 * B:(m6 + 1) * B], wmod_sb[:, k, m6 * P:(m6 + 1) * P], c_t[:, k, :],
                                  start=k == 0, stop=k == KD - 1)
                for bank, lo, n in ((5, 3 * D, 2 * D), (6, 5 * D, D)):
                    for k in range(KD):
                        m = pe.matmul(ps[0:B, bank, 0:n], c_t[:, k, :], wmod_sb[:, k, lo:lo + n],
                                      start=k == 0, stop=k == KD - 1)
                m.then_inc(s_pe_pro, 1)
        pro.close()

        x_v = x.rearrange("b (n p) d -> b p n d", p=P)
        out_v = out.rearrange("b (n p) d -> b p n d", p=P)
        h_v = h_table.rearrange("(b n p) d -> b p n d", b=B, p=P)

        fst = ExitStack()

        def sf(name, shape, dt=F32):
            return fst.enter_context(nc.sbuf_tensor(name, shape, dt))

        st = sf("st", [P, NT, 6])
        mv = sf("mv", [P, NT, 2])
        var_e = sf("var_e", [P, NT])
        rstd = sf("rstd", [P, NT])
        y_max = sf("y_max", [P, 3 * NH])
        y_hi = sf("y_hi", [P, 3 * NH])
        y_lo = sf("y_lo", [P, 3 * NH])
        qkv = sf("qkv", [P, NT, 3, NH, HD])
        q_st = sf("q_st", [P, NT, HG, 2, HD])
        k_st = sf("k_st", [P, NT, HG, 2, HD])
        kn_st = sf("kn_st", [P, HG, 2, HD])
        v_st = sf("v_st", [P, 2, NT, HG, 32])
        vz_r = sf("vz_r", [P, HG, 32])
        vz = sf("vz", [P, 2, 3, HG, 32], BF16)
        kx = sf("kx", [P, T])
        qx = kx
        cn = sf("cn", [P, T], BF16)
        x_in = sf("x_in", [P, NT, D])
        mx = x_in[:, 0:NT // 2, :].rearrange("p n d -> p (n d)")
        q1 = x_in[:, NT // 2:NT, :].rearrange("p n d -> p (n d)").bitcast(BF16).rearrange("p (a t) -> p a t", a=2)
        qn = sf("qn", [P, 2, T], BF16)
        parts = sf("parts", [P, 8, T], BF16)
        A1 = sf("A1", [P, 2, HG, T], BF16)
        A2 = sf("A2", [P, 2, HG, T], BF16)
        R1 = sf("R1", [P, 2, HG, T], BF16)
        R2 = sf("R2", [P, 2, HG, T], BF16)
        p_buf = sf("p_buf", [P, 2, HG, 512])
        p_flat = p_buf[:, :, :, :].rearrange("p a h t -> p (a h t)")
        YN = 3 * NH * HD
        y_abs = p_flat[:, 0:YN].rearrange("p (j d) -> p j d", d=HD)
        y_val = p_flat[:, YN:3 * YN].rearrange("p (a j d) -> p a j d", a=2, d=HD)
        y_one = p_flat[:, 3 * YN:4 * YN].bitcast(BF16).rearrange("p (a j d) -> p a j d", a=2, d=HD)
        y_eq = p_flat[:, 4 * YN:4 * YN + YN // 2].bitcast(BF16).rearrange("p (j d) -> p j d", d=HD)
        y_first = sf("y_first", [P, 3 * NH], BF16)
        h2p = sf("h2p", [P, NT, ROW])
        h_flat = h2p[:, :, :].rearrange("p n r -> p (n r)")
        zm = h_flat[:, 0:2 * 512].bitcast(BF16).rearrange("p (h t) -> p h t", h=HG)
        k1zf = h_flat[:, 1024:1536].rearrange("p (h t) -> p h t", h=HG)
        k0swz = h_flat[:, 1536:1792].bitcast(BF16).rearrange("p (h t) -> p h t", h=HG)
        lw = h_flat[:, 1792:2048].bitcast(BF16).rearrange("p (h t) -> p h t", h=HG)
        em = sf("em", [P, 2, NT, HG])
        gz = sf("gz", [P, 2, HG, P], BF16)
        g_a = sf("g_a", [P, P], BF16)
        k128 = sf("k128", [P, P])
        q128 = sf("q128", [P, P])
        kxz = sf("kxz", [P, HG, P])
        k1zb = sf("k1zb", [P, HG, P], BF16)
        nk1f = sf("nk1f", [P, P])
        kb0 = sf("kb0", [P, P], BF16)
        knz = sf("knz", [P, HG, P])
        pn = sf("pn", [P, HG, P])
        wo_ga = pn[:, :, :].rearrange("p h t -> p (h t)").rearrange("p (k d) -> p k d", k=KD)
        o_sb = sf("o_sb", [P, 2, 512])
        h_t = o_sb[:, 0, :].rearrange("p (a k t) -> p a k t", a=2, k=KD)
        o_cmb = sf("o_cmb", [P, 4, HG, HD + 1])
        o_inv = sf("o_inv", [P, 4, HG])
        o_tok = qkv[:, :, 0]
        bc = sf("bc", [P, 2 * D])
        logit = sf("logit", [P, NT, E])
        l_max = sf("l_max", [P, NT])
        n_hi = sf("n_hi", [P, 1])
        z_lo = sf("z_lo", [P, 4, HG])
        good = sf("good", [P, 4])
        onesz = sf("onesz", [P, HG, P], BF16)
        headsel = sf("headsel", [P, HG], BF16)
        identb = sf("identb", [P, P], BF16)
        later_b = sf("later_b", [P, P], BF16)
        late256 = sf("late256", [P, P], BF16)
        upto = sf("upto", [P, P], BF16)
        tie = sf("tie", [P, P])
        partner = sf("partner", [P, P], BF16)
        part_r = nk1f
        t_less = sf("t_less", [P, P])
        z_thr = sf("z_thr", [P, 1])
        TINY = 1e-30
        UP = -(1.0 + 2.0 ** -7)

        f_const = sem("f_const")
        f_x, f_xr, f_xfree, f_xrfree = (sem(n) for n in ("f_x", "f_xr", "f_xfree", "f_xrfree"))
        f_var, f_rstd, f_xhat, f_hT, f_yev, f_one, f_keep = (sem(n) for n in (
            "f_var", "f_rstd", "f_xhat", "f_hT", "f_yev", "f_one", "f_keep"))
        f_full = [sem(f"f_full{i}") for i in range(3)]
        f_free = [sem(f"f_free{i}") for i in range(3)]
        f_stage, f_kx, f_kp, f_kdma, f_qx, f_qp, f_qdma = (sem(n) for n in (
            "f_stage", "f_kx", "f_kp", "f_kdma", "f_qx", "f_qp", "f_qdma"))
        f_pool, f_pq, f_neg, f_gz, f_em, f_lw, f_nexp, f_pn = (sem(n) for n in (
            "f_pool", "f_pq", "f_neg", "f_gz", "f_em", "f_lw", "f_nexp", "f_pn"))
        f_zm, f_pz, f_p, f_pv, f_O, f_osb = (sem(n) for n in (
            "f_zm", "f_pz", "f_p", "f_pv", "f_O", "f_osb"))
        f_otok, f_oev, f_x2, f_woga, f_h2, f_hev, f_log, f_lm, f_lexp = (sem(n) for n in (
            "f_otok", "f_oev", "f_x2", "f_woga", "f_h2", "f_hev", "f_log", "f_lm", "f_lexp"))
        f_good, f_goods, f_flag = (sem(n) for n in ("f_good", "f_goods", "f_flag"))
        f_pr, f_out, f_var2, f_rstd2 = (sem(n) for n in ("f_pr", "f_out", "f_var2", "f_rstd2"))

        def units(c):
            return [(i, c) for i in range(4 * (c + 1))]

        def span(i, c):
            t0 = max(P * i, 512 * c)
            return t0, 512 * (c + 1) - t0

        def prep_steps(n):
            return [(k, n) for k in ("stage", "K", "Kd", "Q", "G", "Qd", "D2", "M", "NS", "W")]

        def group_steps(g):
            n = g + 1
            body = [("stage", n), ("Z", g, 0), ("K", n), ("S", g, 0, 0), ("Kd", n), ("S", g, 1, 0), ("PZ", g, 0),
                    ("Q", n), ("S", g, 2, 0), ("PN", g), ("G", n), ("S", g, 3, 0), ("PV", g, 3, 0), ("Z", g, 1),
                    ("O", g, 0), ("S", g, 0, 1), ("Qd", n), ("S", g, 1, 1), ("PZ", g, 1), ("S", g, 2, 1), ("S", g, 3, 1),
                    ("D2", n), ("S", g, 4, 1), ("M", n), ("NS", n), ("S", g, 5, 1), ("W", n), ("S", g, 6, 1),
                    ("S", g, 7, 1), ("PV", g, 7, 1), ("O", g, 1)]
            own = ("stage", "K", "Kd", "Q", "G", "Qd", "D2", "M", "NS", "W")
            return [s for s in body if n < NG or s[0] not in own]

        uses = [("WO",), ("BC",)]
        for t in range(NT):
            if t == 0:
                uses.append(("T", 0))
            if t + 1 < NT:
                uses.append(("T", t + 1))
            uses.append(("Y", t))
        attn = prep_steps(0) + [s for g in range(NG) for s in group_steps(g)]
        for s in attn:
            if s[0] in ("K", "Q", "G", "D2", "M", "NS", "W", "O"):
                uses.append(s)
            elif s[0] == "Z":
                uses += [s + (0,), s + (1,)]
            elif s[0] == "S":
                uses += [s + (0,), s + (1,)] if span(s[2], s[3])[1] > 256 else [s + (0,)]
        for t in range(NT):
            if t == 0:
                uses.append(("OT", 0))
            if t + 1 < NT:
                uses.append(("OT", t + 1))
            uses.append(("P", t))
        uses += [("HT", t) for t in range(NT)]
        place = {u: (i % 3, i // 3) for i, u in enumerate(uses)}
        per = [sum(i % 3 == q for i in range(len(uses))) for q in range(3)]

        def buf(u):
            return ps[:, 2 * place[u][0]:2 * place[u][0] + 2, :]

        def buf_of(u):
            return place[u][0]

        def nth(u, b):
            return per[place[u][0]] * b + place[u][1]

        with nc.Block() as blk:
            @blk.sync
            def _(sp):
                with sp.Fori(0, B) as b:
                    sp.wait_ge(f_xfree, b + 1)
                    sp.dma_start(x_in[:, :, :], x_v[bass.ds(b, 1)].rearrange("o p n d -> (o p) n d")).then_inc(f_x, 16)
                    for s in attn:
                        if s[0] == "Kd":
                            n = s[1]
                            sp.wait_ge(f_kp, NG * b + n + 1)
                            if n:
                                sp.wait_ge(f_pv, 12 * (NG * b + n - 1) + 2)
                            for h in range(HG):
                                for dst, lo in ((A1, 0), (A2, 2)):
                                    sp.dma_start(dst[:, n % 2, h, :], parts[32 * h:32 * h + 32, lo:lo + 4, :]).then_inc(f_kdma, 16)
                        if s[0] == "Qd":
                            n = s[1]
                            sp.wait_ge(f_qp, NG * b + n + 1)
                            for h in range(HG):
                                for dst, lo in ((R1, 0), (R2, 4)):
                                    sp.dma_start(dst[:, n % 2, h, :], parts[32 * h:32 * h + 32, lo:lo + 4, :]).then_inc(f_qdma, 16)
                    sp.wait_ge(f_xrfree, b + 1)
                    sp.dma_start(x_in[:, :, :], x_v[bass.ds(b, 1)].rearrange("o p n d -> (o p) n d")).then_inc(f_xr, 16)
                    sp.wait_ge(f_x2, b + 1)
                    sp.dma_start(out_v[bass.ds(b, 1)].rearrange("o p n d -> (o p) n d"), x_in[:, :, :]).then_inc(f_out, 16)
                    sp.wait_ge(f_pr, b + 1)
                    sp.dma_start(h_v[bass.ds(b, 1)].rearrange("o p n d -> (o p) n d"), h2p[:, :, :]).then_inc(f_out, 16)
                sp.wait_ge(f_out, 32 * B)

            @blk.gpsimd
            def _(pool):
                pool.memset(v_st[:, :, :, :, :], 0.0)
                pool.memset(vz_r[:, :, :], 0.0)
                pool.memset(gz[:, :, :, :], 0.0)
                pool.memset(kxz[:, :, :], 0.0)
                pool.memset(knz[:, :, :], 0.0)
                pool.memset(onesz[:, :, :], 0.0)
                pool.memset(headsel[:, :], 0.0)
                pool.memset(later_b[:, :], 0.0)
                pool.memset(late256[:, :], 0.0)
                pool.memset(upto[:, :], 1.0)
                pool.memset(tie[:, :], 0.0)
                pool.memset(part_r[:, :], 0.0)
                pool.memset(half_neg[:, :], -0.5)
                pool.memset(y_hi[:, :], 0.0)
                pool.memset(y_lo[:, :], 1.0)
                pool.memset(n_hi[:, :], 0.0)
                pool.memset(z_lo[:, :, :], 1.0)
                pool.iota(t_less[:, :], [[1, P]], base=1 - TOPK, channel_multiplier=0,
                          allow_small_or_imprecise_dtypes=True)
                pool.iota(z_thr[:, :], [[0, 1]], base=TOPK, channel_multiplier=-1,
                          allow_small_or_imprecise_dtypes=True)
                pool.tensor_copy(identb[:, :], ident[:, :])
                pool.drain()
                pool.memset(v_st[:, :, :, :, HD:HD + 1], 1.0)
                pool.drain()
                for h in range(HG):
                    pool.memset(onesz[32 * h:32 * h + 32, h, :], 1.0)
                    pool.drain()
                    pool.memset(headsel[32 * h:32 * h + 32, h:h + 1], 1.0)
                    pool.drain()
                pool.affine_select(later_b[:, :], later_b[:, :], [[1, P]], ALU.is_ge, -BIG, base=0, channel_multiplier=-1)
                pool.affine_select(late256[:, :], late256[:, :], [[1, P]], ALU.is_ge, 256.0, base=0, channel_multiplier=-1)
                pool.affine_select(upto[:, :], upto[:, :], [[1, P]], ALU.is_ge, 0.0, base=0, channel_multiplier=-1)
                pool.affine_select(tie[:, :], tie[:, :], [[1, P]], ALU.is_ge, TINY, base=0, channel_multiplier=-1)
                for h in range(HG):
                    lo = 32 * h
                    pool.affine_select(part_r[:, lo + HD:lo + 32], part_r[:, lo + HD:lo + 32], [[-1, HD]],
                                       ALU.not_equal, 1.0, base=-lo, channel_multiplier=1)
                    pool.affine_select(part_r[:, lo:lo + HD], part_r[:, lo:lo + HD], [[-1, HD]],
                                       ALU.not_equal, 1.0, base=-lo - HD, channel_multiplier=1)
                pool.drain()
                pool.tensor_tensor(partner[:, :], part_r[:, :], ident[:, :], ALU.add)
                pool.drain().then_inc(f_const, 1)
                with pool.Fori(0, B) as b:
                    pool.wait_ge(f_var, b + 1)
                    pool.tensor_tensor(rstd[:, :], var_e[:, :], half_neg[:, :], ALU.pow)
                    pool.drain().then_inc(f_rstd, 1)
                    for t in range(NT):
                        pool.wait_ge(f_one, NT * b + t + 1)
                        pool.tensor_tensor(qkv[:, t].rearrange("p j h d -> p (j h) d"), y_val[:, t % 2],
                                           y_one[:, t % 2], ALU.mult).then_inc(f_keep, 1)
                    for s in attn:
                        if s[0] == "Qd":
                            pool.wait_ge(f_pool, NG * b + s[1] + 1)
                            pool.tensor_tensor(qn[:, s[1] % 2, :], q1[:, s[1] % 2, :], cn[:, :], ALU.mult)
                            pool.drain().then_inc(f_pq, 1)
                    pool.wait_ge(f_var2, b + 1)
                    pool.tensor_tensor(rstd[:, :], var_e[:, :], half_neg[:, :], ALU.pow)
                    pool.drain().then_inc(f_rstd2, 1)

            @blk.scalar
            def _(act):
                with act.Fori(0, B) as b:
                    for t in range(NT):
                        u = ("Y", t)
                        act.wait_ge(f_full[buf_of(u)], nth(u, b) + 1)
                        y = buf(u).rearrange("p a b -> p (a b)")[:, 0:3 * D]
                        if t >= 1:
                            act.wait_ge(f_one, NT * b + t)
                        if t >= 2:
                            act.wait_ge(f_keep, NT * b + t - 1)
                        act.activation(y_abs[:, :, :].rearrange("p h d -> p (h d)"), y, ACT.Abs)
                        act.activation(y_val[:, t % 2].rearrange("p h d -> p (h d)"), y, ACT.Copy)
                        act.drain().then_inc(f_free[buf_of(u)], 1)
                        act.nop().then_inc(f_yev, 1)
                    for s in attn:
                        kind = s[0]
                        gi = NG * b + s[1]
                        if kind in ("K", "Q", "M", "NS"):
                            u = s
                            act.wait_ge(f_full[buf_of(u)], nth(u, b) + 1)
                        if kind == "K":
                            if s[1]:
                                act.wait_ge(f_qdma, 128 * gi)
                            flat = buf(u).rearrange("p a b -> p (a b)")
                            act.activation(kx[:, :], flat, ACT.Copy)
                            act.activation(parts[:, 2, :], flat, ACT.Copy)
                            act.activation(parts[:, 4, :], flat, ACT.Copy)
                            act.drain().then_inc(f_free[buf_of(u)], 1)
                            act.nop().then_inc(f_kx, 1)
                        if kind == "Q":
                            act.wait_ge(f_kdma, 128 * (gi + 1))
                            flat = buf(u).rearrange("p a b -> p (a b)")
                            act.activation(qx[:, :], flat, ACT.Copy)
                            act.activation(parts[:, 0, :], flat, ACT.Copy)
                            act.activation(parts[:, 2, :], flat, ACT.Copy)
                            act.activation(parts[:, 3, :], flat, ACT.Copy)
                            act.drain().then_inc(f_free[buf_of(u)], 1)
                            act.nop().then_inc(f_qx, 1)
                        if kind == "M":
                            act.activation(em[:, s[1] % 2, :, :].rearrange("p n h -> p (n h)"), buf(u)[:, 0, 0:NT * HG],
                                           ACT.Exp, scale=0.25)
                            act.drain().then_inc(f_free[buf_of(u)], 1)
                            act.nop().then_inc(f_em, 1)
                        if kind == "NS":
                            act.activation(pn[:, :, :].rearrange("p h t -> p (h t)"), buf(u)[:, 0, :], ACT.Exp,
                                           scale=0.25)
                            act.drain().then_inc(f_free[buf_of(u)], 1)
                            act.nop().then_inc(f_nexp, 1)
                        if kind == "S":
                            _, g, i, c = s
                            w = span(i, c)[1]
                            k = (12 * gi + (i if c == 0 else 4 + i))
                            act.wait_ge(f_pv, k + 1)
                            pb = p_buf[:, (i if c == 0 else 4 + i) % 2]
                            if w > 256:
                                for a in range(2):
                                    u = s + (a,)
                                    act.wait_ge(f_full[buf_of(u)], nth(u, b) + 1)
                                    act.activation(pb[:, 2 * a:2 * a + 2, 0:w], buf(u)[:, :, 0:w], ACT.Exp, scale=0.25)
                                    act.drain().then_inc(f_free[buf_of(u)], 1)
                            else:
                                u = s + (0,)
                                act.wait_ge(f_full[buf_of(u)], nth(u, b) + 1)
                                act.activation(pb[:, :, 0:w], buf(u).rearrange("p a (h t) -> p (a h) t", h=2)[:, :, 0:w],
                                               ACT.Exp, scale=0.25)
                                act.drain().then_inc(f_free[buf_of(u)], 1)
                            act.nop().then_inc(f_p, 1)
                        if kind == "O":
                            c = s[2]
                            act.wait_ge(f_O, 2 * gi + c + 1)
                            act.activation(o_sb[:, :, :], ps[:, 6:8, :], ACT.Copy)
                            act.drain().then_inc(f_osb, 1)
                    for t in range(NT):
                        u = ("OT", t)
                        act.wait_ge(f_full[buf_of(u)], nth(u, b) + 1)
                        act.activation(h_t[:, t % 2].rearrange("p k t -> p (k t)"), buf(u)[:, 0, 0:KD * P], ACT.Copy)
                        act.drain().then_inc(f_free[buf_of(u)], 1)
                        act.nop().then_inc(f_oev, 1)
                    for t in range(NT):
                        u = ("HT", t)
                        act.wait_ge(f_full[buf_of(u)], nth(u, b) + 1)
                        if t >= 2:
                            act.wait_ge(f_log, NT * b + t - 1)
                        act.activation(h_t[:, t % 2].rearrange("p k t -> p (k t)"), buf(u)[:, 0, 0:KD * P], ACT.Copy)
                        act.drain().then_inc(f_free[buf_of(u)], 1)
                        act.nop().then_inc(f_hev, 1)
                    act.wait_ge(f_lm, b + 1)
                    act.activation(logit[:, :, :], logit[:, :, :], ACT.Exp)
                    act.drain().then_inc(f_lexp, 1)

            @blk.tensor
            def _(pe):
                for q in range(3):
                    pe.drain().then_inc(f_free[q], 1)
                pe.drain().then_inc(f_pv, 2)
                pe.drain().then_inc(f_pz, 1)
                pe.wait_ge(f_const, 1)
                with pe.Fori(0, B) as b:
                    def begin(u):
                        pe.wait_ge(f_free[buf_of(u)], nth(u, b) + 1)

                    u = ("WO",)
                    begin(u)
                    pe.wait_ge(f_woga, b + 1)
                    for k in range(KD):
                        for h in range(KD):
                            m = pe.transpose(buf(u)[:, 0, k * D + h * P:k * D + (h + 1) * P],
                                             wo_ga[:, h, k * P:(k + 1) * P], ident[:, :])
                    m.then_inc(f_full[buf_of(u)], 1)
                    u = ("BC",)
                    begin(u)
                    pe.matmul(buf(u)[:, 0, :], pick_b[:, :], mod_rows[:, 0:2 * D], start=True,
                              stop=True).then_inc(f_full[buf_of(u)], 1)

                    def turn(t):
                        u = ("T", t)
                        begin(u)
                        pe.wait_ge(f_xhat, NT * b + t + 1)
                        for k in range(KD):
                            m = pe.transpose(buf(u)[:, 0, k * P:(k + 1) * P], x_in[:, t, k * P:(k + 1) * P], ident[:, :])
                        m.then_inc(f_full[buf_of(u)], 1)

                    turn(0)
                    for t in range(NT):
                        if t + 1 < NT:
                            turn(t + 1)
                        u = ("Y", t)
                        begin(u)
                        pe.wait_ge(f_hT, NT * b + t + 1)
                        for bank, lo, n in ((0, 0, 2 * D), (1, 2 * D, D)):
                            for k in range(KD):
                                m = pe.matmul(buf(u)[:, bank, 0:n], h_t[:, t % 2, k, :], w_t[:, k, lo:lo + n],
                                              start=k == 0, stop=k == KD - 1)
                        m.then_inc(f_full[buf_of(u)], 1)

                    def pv(g, i, c):
                        gi = NG * b + g
                        k = i if c == 0 else 4 + i
                        pe.wait_ge(f_p, 12 * gi + k + 1)
                        t0, w = span(i, c)
                        o = t0 - 512 * c
                        if i == 0:
                            pe.wait_ge(f_osb, 2 * gi + c + 1)
                        for h in range(HG):
                            m = pe.matmul(ps[32 * h:32 * h + 32, 6, o:o + w], v_st[:, g % 2, i, h, :],
                                          p_buf[:, k % 2, h, 0:w], start=i == 0, stop=False, skip_group_check=True)
                        m.then_inc(f_pv, 1)

                    for s in attn:
                        kind = s[0]
                        n = s[1]
                        gi = NG * b + n
                        par = n % 2
                        if kind in ("K", "Q", "G", "D2", "M", "NS", "W", "O"):
                            u = s
                            if kind != "O":
                                begin(u)
                        if kind in ("K", "Q"):
                            pe.wait_ge(f_stage, gi + 1)
                            src = k_st if kind == "K" else q_st
                            for t in range(NT):
                                m = pe.transpose(buf(u)[:, t // 4, (t % 4) * P:(t % 4 + 1) * P],
                                                 src[:, t].rearrange("p h s d -> p (h s d)"), ident[:, :])
                            m.then_inc(f_full[buf_of(u)], 1)
                        if kind == "G":
                            pe.wait_ge(f_neg, gi + 1)
                            pe.matmul(buf(u)[:, 0, 0:P], partner[:, :], g_a[:, :], start=True, stop=True)
                            pe.transpose(buf(u)[:, 1, 0:P], kn_st[:, :, :, :].rearrange("p h s d -> p (h s d)"),
                                         ident[:, :]).then_inc(f_full[buf_of(u)], 1)
                        if kind == "D2":
                            pe.wait_ge(f_gz, gi + 1)
                            for h in range(HG):
                                o = buf(u)[:, 0, h * P:(h + 1) * P]
                                pe.matmul(o, k1zb[:, h, :], kb0[:, :], start=True, stop=False)
                                pe.matmul(o, k1zf[:, h, :], k128[:, :], start=False, stop=False)
                                m = pe.matmul(o, kxz[:, h, :], nk1f[:, :], start=False, stop=True)
                            m.then_inc(f_full[buf_of(u)], 1)
                        if kind == "M":
                            pe.wait_ge(f_qp, gi + 1)
                            for t in range(NT):
                                m = pe.matmul(buf(u)[:, 0, t * HG:(t + 1) * HG], parts[:, 1, t * P:(t + 1) * P],
                                              headsel[:, :], start=True, stop=True)
                            m.then_inc(f_full[buf_of(u)], 1)
                        if kind == "NS":
                            for h in range(HG):
                                o = buf(u)[:, 0, h * P:(h + 1) * P]
                                pe.matmul(o, k0swz[:, h, :], parts[:, 7, 0:P], start=True, stop=False)
                                pe.matmul(o, identb[:, :], later_b[:, :], start=False, stop=False)
                                pe.matmul(o, onesz[:, h, :], parts[:, 1, 0:P], start=False, stop=False)
                                m = pe.matmul(o, knz[:, h, :], q128[:, :], start=False, stop=True)
                            m.then_inc(f_full[buf_of(u)], 1)
                        if kind == "W":
                            pe.wait_ge(f_lw, gi + 1)
                            for h in range(HG):
                                m = pe.matmul(buf(u)[:, 0, h * P:(h + 1) * P], lw[:, h, :], upto[:, :], start=True, stop=True)
                            m.then_inc(f_full[buf_of(u)], 1)
                        if kind == "Z":
                            c = s[2]
                            if c == 0:
                                pe.wait_ge(f_gz, gi + 1)
                                pe.wait_ge(f_pq, gi + 1)
                            for a in range(2):
                                u = s + (a,)
                                begin(u)
                                for h in (2 * a, 2 * a + 1):
                                    o = buf(u)[:, h % 2, :]
                                    pe.matmul(o, gz[:, par, h, :], q1[:, par, 512 * c:512 * c + 512], start=True, stop=False)
                                    m = pe.matmul(o, onesz[:, h, :], qn[:, par, 512 * c:512 * c + 512], start=False,
                                                  stop=c == 1)
                                    if c == 0:
                                        m = pe.matmul(o[:, 0:P], identb[:, :], late256[:, :], start=False, stop=True)
                                m.then_inc(f_full[buf_of(u)], 1)
                        if kind == "PZ":
                            c = s[2]
                            pe.wait_ge(f_zm, 2 * gi + c + 1)
                            pe.wait_ge(f_osb, 2 * gi + c + 1)
                            for q in range(3):
                                for h in range(HG):
                                    m = pe.matmul(ps[32 * h:32 * h + 32, 7, :], vz[:, par, q, h, :], zm[:, h, :],
                                                  start=q == 0, stop=q == 2, skip_group_check=True)
                            m.then_inc(f_pz, 1)
                        if kind == "PN":
                            pe.wait_ge(f_pn, gi + 1)
                            for h in range(HG):
                                m = pe.matmul(ps[32 * h:32 * h + 32, 6, 0:P], v_st[:, par, 0, h, :], pn[:, h, :],
                                              start=False, stop=False, skip_group_check=True)
                        if kind == "S":
                            _, g, i, c = s
                            t0, w = span(i, c)
                            if i == 0 and c == 0:
                                pe.wait_ge(f_kdma, 128 * (gi + 1))
                                pe.wait_ge(f_qdma, 128 * (gi + 1))
                            for a in range(2 if w > 256 else 1):
                                u = s + (a,)
                                begin(u)
                                for h in ((2 * a, 2 * a + 1) if w > 256 else range(HG)):
                                    o = buf(u)[:, h % 2, 0:w] if w > 256 else buf(u)[:, h // 2, 256 * (h % 2):256 * (h % 2) + w]
                                    ks, ts = slice(P * i, P * i + P), slice(t0, t0 + w)
                                    pe.matmul(o, A1[:, par, h, ks], R1[:, par, h, ts], start=True, stop=False)
                                    m = pe.matmul(o, A2[:, par, h, ks], R2[:, par, h, ts], start=False, stop=t0 != P * i)
                                    if t0 == P * i:
                                        m = pe.matmul(o[:, 0:P], identb[:, :], later_b[:, :], start=False, stop=True)
                                m.then_inc(f_full[buf_of(u)], 1)
                            if i:
                                pv(g, i - 1, c)
                        if kind == "PV":
                            _, g, i, c = s
                            pv(g, i, c)
                            pe.drain().then_inc(f_O, 1)
                        if kind == "O":
                            c = s[2]
                            begin(u)
                            pe.wait_ge(f_osb, 2 * gi + c + 2)
                            for q in range(4):
                                for a in range(2):
                                    m = pe.transpose(buf(u)[:, a, q * P:(q + 1) * P], o_sb[:, a, q * P:(q + 1) * P], ident[:, :])
                            m.then_inc(f_full[buf_of(u)], 1)

                    def turn_o(t):
                        u = ("OT", t)
                        begin(u)
                        if t == 0:
                            pe.wait_ge(f_otok, b + 1)
                        for k in range(KD):
                            m = pe.transpose(buf(u)[:, 0, k * P:(k + 1) * P],
                                             o_tok[:, t].rearrange("p h d -> p (h d)")[:, k * P:(k + 1) * P], ident[:, :])
                        m.then_inc(f_full[buf_of(u)], 1)

                    turn_o(0)
                    for t in range(NT):
                        if t + 1 < NT:
                            turn_o(t + 1)
                        u = ("P", t)
                        begin(u)
                        pe.wait_ge(f_oev, NT * b + t + 1)
                        for k in range(KD):
                            m = pe.matmul(buf(u)[:, 0, 0:D], h_t[:, t % 2, k, :], wo_t[:, k, :],
                                          start=k == 0, stop=k == KD - 1)
                        m.then_inc(f_full[buf_of(u)], 1)

                    def turn_h(t):
                        u = ("HT", t)
                        begin(u)
                        pe.wait_ge(f_h2, NT * b + t + 1)
                        for k in range(KD):
                            m = pe.transpose(buf(u)[:, 0, k * P:(k + 1) * P], h2p[:, t, k * P:(k + 1) * P], ident[:, :])
                        m.then_inc(f_full[buf_of(u)], 1)

                    turn_h(0)
                    for t in range(NT):
                        if t + 1 < NT:
                            turn_h(t + 1)
                        pe.wait_ge(f_hev, NT * b + t + 1)
                        lo = ps[:, 6, t * E:(t + 1) * E]
                        for k in range(KD):
                            pe.matmul(lo, h_t[:, t % 2, k, :], rw_sb[:, k, :], start=k == 0, stop=False)
                        pe.matmul(lo, ones_f[0:1, :], rb_sb[:, :], start=False, stop=True).then_inc(f_log, 1)
                pe.wait_ge(f_good, 1)
                pe.matmul(ps[0:1, 7, 0:4], ones_f[:, 0:1], good[:, :], start=True, stop=True).then_inc(f_goods, 1)

            @blk.vector
            def _(dve):
                dve.wait_ge(f_const, 1)
                dve.drain().then_inc(f_xfree, 1)
                dve.drain().then_inc(f_osb, 1)
                with dve.Fori(0, B) as b:
                    def full(u):
                        dve.wait_ge(f_full[buf_of(u)], nth(u, b) + 1)

                    def release(u):
                        dve.drain().then_inc(f_free[buf_of(u)], 1)

                    dve.tensor_copy(mod_b[:, :, :], mod_t[:, :, :, bass.ds(b, 1)].rearrange("p j k o -> p j (k o)"))
                    dve.tensor_copy(pick_b[:, :], ident[0:B, bass.ds(b, 1)].to_broadcast([B, P]))
                    dve.drain()
                    for k in range(KD):
                        dve.tensor_scalar(wo_ga[:, k, :], wo_nat[:, k, :], mod_b[:, 2, k:k + 1], None, ALU.mult)
                    dve.drain().then_inc(f_woga, 1)
                    dve.wait_ge(f_x, 16 * (b + 1))
                    for t in range(NT):
                        dve.bn_stats(st[:, t, :], x_in[:, t, :])
                    dve.drain()
                    for t in range(NT):
                        dve.bn_aggr(mv[:, t, :], st[:, t, :])
                    dve.drain()
                    dve.tensor_scalar(var_e[:, :], mv[:, :, 1], EPS, None, ALU.add)
                    dve.drain().then_inc(f_var, 1)
                    full(("WO",))
                    dve.tensor_copy(wo_t[:, :, :], buf(("WO",))[:, 0, :].rearrange("p (k d) -> p k d", k=KD))
                    release(("WO",))
                    full(("BC",))
                    dve.tensor_copy(bc[:, :], buf(("BC",))[:, 0, :])
                    release(("BC",))
                    dve.wait_ge(f_rstd, b + 1)
                    for t in range(NT):
                        dve.tensor_scalar(x_in[:, t, :], x_in[:, t, :], mv[:, t, 0:1], rstd[:, t:t + 1],
                                          ALU.subtract, ALU.mult).then_inc(f_xhat, 1)

                    def modulate(t):
                        u = ("T", t)
                        full(u)
                        if t >= 2:
                            v = ("Y", t - 2)
                            dve.wait_ge(f_full[buf_of(v)], nth(v, b) + 1)
                        for k in range(KD):
                            dve.tensor_scalar(h_t[:, t % 2, k, :], buf(u)[:, 0, k * P:(k + 1) * P],
                                              mod_b[:, 1, k:k + 1], mod_b[:, 0, k:k + 1], ALU.mult, ALU.add)
                        release(u)
                        dve.nop().then_inc(f_hT, 1)

                    modulate(0)
                    for t in range(NT):
                        if t + 1 < NT:
                            modulate(t + 1)
                        dve.wait_ge(f_yev, NT * b + t + 1)
                        one = y_one[:, t % 2]
                        if t >= 2:
                            dve.wait_ge(f_keep, NT * b + t - 1)
                        dve.tensor_reduce(y_max[:, :], y_abs[:, :, :], AX.X, ALU.max)
                        dve.drain()
                        dve.tensor_tensor(y_eq[:, :, :], y_abs[:, :, :],
                                          y_max[:, :].unsqueeze(2).to_broadcast([P, 3 * NH, HD]), ALU.is_equal)
                        dve.tensor_tensor(y_hi[:, :], y_hi[:, :], y_max[:, :], ALU.max)
                        dve.tensor_tensor(y_lo[:, :], y_lo[:, :], y_max[:, :], ALU.min)
                        dve.drain()
                        dve.tensor_tensor(y_eq[:, :, :], y_eq[:, :, :], first_of[:, :].unsqueeze(1).to_broadcast([P, 3 * NH, HD]), ALU.mult)
                        dve.drain()
                        dve.tensor_reduce(y_first[:, :], y_eq[:, :, :], AX.X, ALU.max)
                        dve.drain()
                        dve.tensor_tensor(one, y_eq[:, :, :], y_first[:, :].unsqueeze(2).to_broadcast([P, 3 * NH, HD]),
                                          ALU.is_equal)
                        dve.drain().then_inc(f_one, 1)

                    for s in attn:
                        kind = s[0]
                        n = s[1]
                        gi = NG * b + n
                        par = n % 2
                        hs = slice(HG * n, HG * n + HG)
                        if kind == "stage":
                            if n == 0:
                                dve.wait_ge(f_keep, NT * (b + 1))
                            else:
                                dve.wait_ge(f_pv, 12 * (gi - 1) + 2)
                            for sg, mul in ((0, 1.0), (1, -1.0)):
                                dve.tensor_scalar(k_st[:, :, :, sg, :], qkv[:, :, 1, hs, :], mul, 0.0, ALU.mult, ALU.max)
                                dve.tensor_scalar(q_st[:, :, :, sg, :], qkv[:, :, 0, hs, :], mul, 0.0, ALU.mult, ALU.max)
                                dve.tensor_scalar(kn_st[:, :, sg, :], qkv[:, 0, 1, hs, :], mul, 0.0, ALU.mult, ALU.min)
                            dve.tensor_copy(v_st[:, par, :, :, 0:HD], qkv[:, :, 2, hs, :])
                            dve.drain().then_inc(f_stage, 1)
                            v0 = v_st[:, par, 0, :, :]
                            dve.tensor_copy(vz[:, par, 0], v0)
                            dve.drain()
                            dve.tensor_tensor(vz_r[:, :, :], v0, vz[:, par, 0], ALU.subtract)
                            dve.drain()
                            dve.tensor_copy(vz[:, par, 1], vz_r[:, :, :])
                            dve.drain()
                            dve.tensor_tensor(vz[:, par, 2], vz_r[:, :, :], vz[:, par, 1], ALU.subtract)
                        if kind == "Kd":
                            dve.wait_ge(f_kx, gi + 1)
                            dve.tensor_scalar(parts[:, 1, :], kx[:, :], 0.0, None, ALU.is_gt)
                            dve.tensor_scalar(parts[:, 5, :], kx[:, :], 0.0, None, ALU.is_le)
                            dve.drain()
                            dve.tensor_tensor_scan(mx[:, :], kx[:, :], kx[:, :], 0.0, ALU.max, ALU.max)
                            dve.tensor_tensor_scan(cn[:, :], parts[:, 1, :], parts[:, 1, :], 0.0, ALU.add, ALU.max)
                            dve.tensor_copy(k128[:, :], kx[:, 0:P])
                            for h in range(HG):
                                r = slice(32 * h, 32 * h + 32)
                                dve.tensor_copy(kxz[r, h, :], kx[r, 0:P])
                            dve.drain()
                            dve.tensor_tensor(kx[:, :], kx[:, :], parts[:, 2, :], ALU.subtract)
                            dve.tensor_scalar(k1zf[:, :, :], kxz[:, :, :], 0.0, None, ALU.is_gt)
                            dve.tensor_scalar(k1zb[:, :, :], kxz[:, :, :], 0.0, None, ALU.is_gt)
                            dve.tensor_scalar(nk1f[:, :], k128[:, :], 0.0, -1.0, ALU.is_gt, ALU.mult)
                            dve.tensor_scalar(kb0[:, :], k128[:, :], 0.0, BIG, ALU.is_le, ALU.mult)
                            dve.scalar_tensor_tensor(g_a[:, :], parts[:, 1, 0:P], 257.0, cn[:, 0:P], ALU.mult, ALU.subtract)
                            dve.tensor_tensor(n_hi[:, :], n_hi[:, :], cn[:, T - 1:T], ALU.max)
                            dve.drain().then_inc(f_neg, 1)
                            dve.tensor_copy(parts[:, 3, :], kx[:, :])
                            dve.drain()
                            dve.tensor_tensor(parts[:, 0, :], kx[:, :], parts[:, 3, :], ALU.subtract)
                            dve.drain().then_inc(f_kp, 1)
                        if kind == "G":
                            full(s)
                            for h in range(HG):
                                r = slice(32 * h, 32 * h + 32)
                                dve.tensor_copy(gz[r, par, h, :], buf(s)[r, 0, 0:P])
                                dve.tensor_copy(knz[r, h, :], buf(s)[r, 1, 0:P])
                            release(s)
                            dve.scalar_tensor_tensor(k0swz[:, :, :], knz[:, :, :], 0.0, onesz[:, :, :], ALU.is_ge, ALU.mult)
                            dve.drain().then_inc(f_gz, 1)
                        if kind == "Qd":
                            dve.wait_ge(f_qx, gi + 1)
                            dve.tensor_scalar(q1[:, par, :], qx[:, :], 0.0, None, ALU.is_gt)
                            dve.drain().then_inc(f_pool, 1)
                            dve.tensor_scalar(parts[:, 7, :], qx[:, :], 0.0, -BIG, ALU.is_gt, ALU.mult)
                            dve.scalar_tensor_tensor(parts[:, 1, :], qx[:, :], UP, mx[:, :], ALU.mult, ALU.mult)
                            dve.tensor_copy(q128[:, :], qx[:, 0:P])
                            dve.drain()
                            dve.tensor_tensor(qx[:, :], qx[:, :], parts[:, 0, :], ALU.subtract)
                            dve.drain()
                            dve.tensor_copy(parts[:, 4, :], qx[:, :])
                            dve.tensor_copy(parts[:, 5, :], qx[:, :])
                            dve.drain()
                            dve.tensor_tensor(parts[:, 6, :], qx[:, :], parts[:, 4, :], ALU.subtract)
                            dve.drain().then_inc(f_qp, 1)
                        if kind == "D2":
                            full(s)
                            dve.tensor_tensor(lw[:, :, :], buf(s)[:, 0, :].rearrange("p (h t) -> p h t", h=HG),
                                              tie[:, :].unsqueeze(1).to_broadcast([P, HG, P]), ALU.is_lt)
                            release(s)
                            dve.nop().then_inc(f_lw, 1)
                        if kind == "W":
                            full(s)
                            dve.tensor_tensor(k1zf[:, :, :], buf(s)[:, 0, :].rearrange("p (h t) -> p h t", h=HG),
                                              t_less[:, :].unsqueeze(1).to_broadcast([P, HG, P]), ALU.is_ge)
                            release(s)
                            dve.wait_ge(f_nexp, gi + 1)
                            dve.tensor_tensor(pn[:, :, :], pn[:, :, :], k1zf[:, :, :], ALU.mult)
                            dve.drain().then_inc(f_pn, 1)
                        if kind == "Z":
                            c = s[2]
                            for a in range(2):
                                u = s + (a,)
                                full(u)
                                if a == 0:
                                    dve.wait_ge(f_pz, 2 * gi + c + 1)
                                dve.tensor_scalar(zm[:, 2 * a:2 * a + 2, :], buf(u), z_thr[:, :], None, ALU.is_lt)
                                release(u)
                            dve.nop().then_inc(f_zm, 1)
                            if n == NG - 1 and c == 1:
                                dve.drain().then_inc(f_xrfree, 1)
                        if kind == "O":
                            c = s[2]
                            full(s)
                            if c == 0:
                                dve.wait_ge(f_em, gi + 1)
                            o4 = buf(s)[:, 1, :].rearrange("p (q h d) -> p q h d", q=4, h=HG)[:, :, :, 0:HD + 1]
                            p4 = buf(s)[:, 0, :].rearrange("p (q h d) -> p q h d", q=4, h=HG)[:, :, :, 0:HD + 1]
                            dve.tensor_tensor(o_cmb[:, :, :, :], o4,
                                              em[:, par, 4 * c:4 * c + 4, :].unsqueeze(3).to_broadcast([P, 4, HG, HD + 1]),
                                              ALU.mult)
                            dve.drain()
                            dve.tensor_tensor(o_cmb[:, :, :, :], o_cmb[:, :, :, :], p4, ALU.add)
                            release(s)
                            dve.drain()
                            dve.tensor_tensor(z_lo[:, :, :], z_lo[:, :, :], o_cmb[:, :, :, HD], ALU.min)
                            dve.reciprocal(o_inv[:, :, :], o_cmb[:, :, :, HD])
                            dve.drain()
                            dve.tensor_tensor(o_tok[:, 4 * c:4 * c + 4, hs, :], o_cmb[:, :, :, 0:HD],
                                              o_inv[:, :, :].unsqueeze(3).to_broadcast([P, 4, HG, HD]), ALU.mult)
                            dve.drain()
                    dve.drain().then_inc(f_otok, 1)
                    dve.wait_ge(f_xr, 16 * (b + 1))
                    for t in range(NT):
                        u = ("P", t)
                        full(u)
                        dve.tensor_tensor(x_in[:, t, :], buf(u)[:, 0, 0:D], x_in[:, t, :], ALU.add)
                        release(u)
                        dve.bn_stats(st[:, t, :], x_in[:, t, :])
                    dve.drain().then_inc(f_x2, 1)
                    for t in range(NT):
                        dve.bn_aggr(mv[:, t, :], st[:, t, :])
                    dve.drain()
                    dve.tensor_scalar(var_e[:, :], mv[:, :, 1], EPS, None, ALU.add)
                    dve.drain().then_inc(f_var2, 1)
                    dve.wait_ge(f_rstd2, b + 1)
                    for t in range(NT):
                        h = h2p[:, t, 0:D]
                        dve.tensor_scalar(h, x_in[:, t, :], mv[:, t, 0:1], rstd[:, t:t + 1], ALU.subtract, ALU.mult)
                        dve.drain()
                        dve.tensor_tensor(h, h, bc[:, D:2 * D], ALU.mult)
                        dve.drain()
                        dve.tensor_tensor(h, h, bc[:, 0:D], ALU.add)
                        dve.drain().then_inc(f_h2, 1)
                    dve.wait_ge(f_log, NT * (b + 1))
                    lg = ps[:, 6, 0:NT * E].rearrange("p (n e) -> p n e", e=E)
                    dve.tensor_reduce(l_max[:, :], lg, AX.X, ALU.max)
                    dve.drain()
                    dve.tensor_tensor(logit[:, :, :], lg, l_max[:, :].unsqueeze(2).to_broadcast([P, NT, E]), ALU.subtract)
                    dve.drain().then_inc(f_lm, 1)
                    dve.wait_ge(f_lexp, b + 1)
                    dve.tensor_reduce(l_max[:, :], logit[:, :, :], AX.X, ALU.add)
                    dve.drain()
                    dve.reciprocal(l_max[:, :], l_max[:, :])
                    dve.drain()
                    dve.tensor_tensor(h2p[:, :, D:ROW], logit[:, :, :], l_max[:, :].unsqueeze(2).to_broadcast([P, NT, E]),
                                      ALU.mult)
                    dve.drain()
                    dve.tensor_copy(probs[:, bass.ds(b * NT, NT), :], h2p[:, :, D:ROW])
                    dve.drain().then_inc(f_pr, 1)
                    dve.wait_ge(f_out, 32 * (b + 1))
                    dve.memset(stand[:, :], 0.0)
                    dve.drain().then_inc(f_xfree, 1)
                dve.tensor_reduce(y_max[:, 0:1], y_hi[:, 0:2 * NH], AX.X, ALU.max)
                dve.tensor_reduce(y_max[:, 1:2], y_lo[:, 0:2 * NH], AX.X, ALU.min)
                dve.tensor_reduce(y_max[:, 2:3], z_lo[:, :, :], AX.XY, ALU.min)
                dve.drain()
                dve.tensor_scalar(good[:, 0:1], n_hi[:, :], float(TOPK), None, ALU.is_le)
                dve.tensor_scalar(good[:, 1:2], y_max[:, 0:1], 1e12, None, ALU.is_le)
                dve.tensor_scalar(good[:, 2:3], y_max[:, 1:2], 1e-12, None, ALU.is_ge)
                dve.tensor_scalar(good[:, 3:4], y_max[:, 2:3], 1e-30, None, ALU.is_ge)
                dve.drain().then_inc(f_good, 1)
                dve.wait_ge(f_goods, 1)
                dve.tensor_reduce(good[0:1, 0:1], ps[0:1, 7, 0:4], AX.X, ALU.add)
                dve.drain()
                dve.tensor_scalar(bad_f[:, :], good[0:1, 0:1], 4.0 * P, None, ALU.is_lt)
                dve.drain().then_inc(f_flag, 1)
        fst.close()

        gen = ExitStack()

        def sg(name, shape, dt=F32):
            return gen.enter_context(nc.sbuf_tensor("gen_" + name, shape, dt))

        x_in = sg("x_in", [P, NT, D])
        x_res = sg("x_res", [P, NT, D])
        st = sg("st", [P, NT, 6])
        mv = sg("mv", [P, NT, 2])
        var_e = sg("var_e", [P, NT])
        rstd = sg("rstd", [P, NT])
        h_t = sg("h_t", [P, 2, KD, P])
        y_abs = sg("y_abs", [P, 2, 3 * NH, HD])
        y_val = sg("y_val", [P, 2, 3 * NH, HD])
        y_max = sg("y_max", [P, 3 * NH])
        y_eq = sg("y_eq", [P, 3 * NH, HD], BF16)
        y_ord = sg("y_ord", [P, 3 * NH, HD], BF16)
        y_first = sg("y_first", [P, 3 * NH], BF16)
        y_one = sg("y_one", [P, 2, 3 * NH, HD], BF16)
        qkv = sg("qkv", [P, NT, 3, NH, HD])
        q_st = sg("q_st", [P, NT, HG, 2, HD])
        k_st = sg("k_st", [P, NT, HG, 2, HD])
        v_st = sg("v_st", [P, NT, HG, HD + 1])
        q_rows = sg("q_rows", [P, T])
        k_rows = sg("k_rows", [P, T])
        q_tile = sg("q_tile", [P, P])
        sc = sg("sc", [P, T])
        work = sg("work", [P, T])
        top8 = sg("top8", [P, TOPK])
        neg_m = sg("neg_m", [P, 1])
        prob = sg("prob", [P, T])
        prob_t = sg("prob_t", [P, NT, P])
        z_inv = sg("z_inv", [P, 1])
        o_tok = sg("o_tok", [P, NT, NH, HD])
        o_t = sg("o_t", [P, 2, KD, P])
        x2 = sg("x2", [P, NT, D])
        bc = sg("bc", [P, 2 * D])
        h2p = sg("h2p", [P, NT, ROW])
        logit = sg("logit", [P, NT, E])
        l_max = sg("l_max", [P, NT])
        wo_ga = sg("wo_ga", [P, KD, D])
        causal = sg("causal", [P, 15 * P])
        s_causal = sem("s_causal")
        s_x, s_xr = sem("s_x"), sem("s_xr")
        s_x_free, s_xr_free = sem("s_x_free"), sem("s_xr_free")
        s_var, s_rstd = sem("s_var"), sem("s_rstd")
        s_xhat, s_xT, s_hT, s_qkv = sem("s_xhat"), sem("s_xT"), sem("s_hT"), sem("s_qkv")
        s_yev, s_one, s_keep = sem("s_yev"), sem("s_one"), sem("s_keep")
        s_stage, s_rT, s_rows, s_qt = sem("s_stage"), sem("s_rT"), sem("s_rows"), sem("s_qt")
        s_S, s_m, s_p, s_pk, s_pT, s_pts, s_O = (sem(n) for n in
                                                ("s_S", "s_m", "s_p", "s_pk", "s_pT", "s_pts", "s_O"))
        s_otok, s_oT, s_oev, s_Y, s_x2 = (sem(n) for n in ("s_otok", "s_oT", "s_oev", "s_Y", "s_x2"))
        s_modb, s_woga, s_woT, s_wot, s_bc = (sem(n) for n in ("s_modb", "s_woga", "s_woT", "s_wot", "s_bc"))
        s_h2, s_h2T, s_h2ev, s_log, s_lm, s_lexp = (sem(n) for n in
                                                    ("s_h2", "s_h2T", "s_h2ev", "s_log", "s_lm", "s_lexp"))
        s_pr, s_out, s_bcev, s_var2, s_rstd2 = (sem(n) for n in ("s_pr", "s_out", "s_bcev", "s_var2", "s_rstd2"))

        with nc.Block() as blk:
            @blk.sync
            def _(sp):
                general = sp.value_load(bad_f[0:1, 0:1])
                with sp.If(general == 1):
                    with sp.Fori(0, B) as b:
                        sp.wait_ge(s_x_free, b + 1)
                        sp.dma_start(x_in[:, :, :], x_v[bass.ds(b, 1)].rearrange("o p n d -> (o p) n d")).then_inc(s_x, 16)
                        sp.wait_ge(s_xr_free, NT * b + 1)
                        sp.dma_start(x_res[:, :, :], x_v[bass.ds(b, 1)].rearrange("o p n d -> (o p) n d")).then_inc(s_xr, 16)
                        sp.wait_ge(s_x2, b + 1)
                        sp.dma_start(out_v[bass.ds(b, 1)].rearrange("o p n d -> (o p) n d"), x2[:, :, :]).then_inc(s_out, 16)
                        sp.wait_ge(s_pr, b + 1)
                        sp.dma_start(h_v[bass.ds(b, 1)].rearrange("o p n d -> (o p) n d"), h2p[:, :, :]).then_inc(s_out, 16)
                    sp.wait_ge(s_out, 32 * B)
                sp.nop()

            @blk.gpsimd
            def _(pool):
                general = pool.value_load(bad_f[0:1, 0:1])
                with pool.If(general == 1):
                    pool.memset(causal[:, :], 0.0)
                    pool.memset(v_st[:, :, :, :], 1.0)
                    pool.drain()
                    pool.affine_select(causal[:, :], causal[:, :], [[-1, 15 * P]], ALU.is_ge, -BIG, base=7 * P,
                                       channel_multiplier=1)
                    pool.drain().then_inc(s_causal, 1)
                    with pool.Fori(0, B) as b:
                        pool.wait_ge(s_var, b + 1)
                        pool.tensor_tensor(rstd[:, :], var_e[:, :], half_neg[:, :], ALU.pow)
                        pool.drain().then_inc(s_rstd, 1)
                        for t in range(NT):
                            pool.wait_ge(s_one, NT * b + t + 1)
                            if t == 0:
                                pool.wait_ge(s_otok, b + 1)
                            pool.tensor_tensor(qkv[:, t].rearrange("p j h d -> p (j h) d"), y_val[:, t % 2],
                                               y_one[:, t % 2], ALU.mult).then_inc(s_keep, 1)
                        pool.wait_ge(s_var2, b + 1)
                        pool.tensor_tensor(rstd[:, :], var_e[:, :], half_neg[:, :], ALU.pow)
                        pool.drain().then_inc(s_rstd2, 1)
                pool.nop()

            @blk.scalar
            def _(act):
                general = act.value_load(bad_f[0:1, 0:1])
                with act.If(general == 1):
                    with act.Fori(0, B) as b:
                        for t in range(NT):
                            act.wait_ge(s_qkv, NT * b + t + 1)
                            y = ps[:, 2 + 2 * (t % 2):4 + 2 * (t % 2), :].rearrange("p a b -> p (a b)")[:, 0:3 * D]
                            if t >= 2:
                                act.wait_ge(s_keep, NT * b + t - 1)
                            act.activation(y_abs[:, t % 2].rearrange("p h d -> p (h d)"), y, ACT.Abs)
                            act.activation(y_val[:, t % 2].rearrange("p h d -> p (h d)"), y, ACT.Copy).then_inc(s_yev, 1)
                        with act.Fori(0, NG) as g:
                            gi = b * NG + g
                            act.wait_ge(s_rT, gi + 1)
                            act.activation(q_rows[:, :], ps[:, 0:2, :].rearrange("p a b -> p (a b)"), ACT.Copy)
                            act.activation(k_rows[:, :], ps[:, 2:4, :].rearrange("p a b -> p (a b)"),
                                           ACT.Copy).then_inc(s_rows, 1)
                            with act.Fori(0, NT) as i:
                                for j in range(HG):
                                    u = (gi * NT + i) * HG + j
                                    act.wait_ge(s_m, u + 1)
                                    act.activation(prob[:, :], sc[:, :], ACT.Exp, scale=0.25,
                                                   bias=neg_m[:, :]).then_inc(s_p, 1)
                                    act.wait_ge(s_pT, u + 1)
                                    act.activation(prob_t[:, :, :].rearrange("p a b -> p (a b)"),
                                                   ps[:, 6:8, :].rearrange("p a b -> p (a b)"), ACT.Copy).then_inc(s_pts, 1)
                        for t in range(NT):
                            act.wait_ge(s_oT, NT * b + t + 1)
                            act.activation(o_t[:, t % 2].rearrange("p k t -> p (k t)"), ps[:, t % 2, 0:KD * P],
                                           ACT.Copy).then_inc(s_oev, 1)
                        for t in range(NT):
                            act.wait_ge(s_h2T, NT * b + t + 1)
                            act.activation(h_t[:, t % 2].rearrange("p k t -> p (k t)"), ps[:, 4 + t % 2, 0:KD * P],
                                           ACT.Copy).then_inc(s_h2ev, 1)
                        act.wait_ge(s_lm, b + 1)
                        act.activation(logit[:, :, :], logit[:, :, :], ACT.Exp).then_inc(s_lexp, 1)
                act.nop()

            @blk.tensor
            def _(pe):
                general = pe.value_load(bad_f[0:1, 0:1])
                with pe.If(general == 1):
                    with pe.Fori(0, B) as b:
                        pe.wait_ge(s_woga, b + 1)
                        for k in range(KD):
                            for h in range(KD):
                                m = pe.transpose(ps[:, 6, k * D + h * P:k * D + (h + 1) * P],
                                                 wo_ga[:, h, k * P:(k + 1) * P], ident[:, :])
                        m.then_inc(s_woT, 1)
                        pe.matmul(ps[:, 7, :], pick_b[:, :], mod_rows[:, 0:2 * D], start=True, stop=True).then_inc(s_bc, 1)

                        def turn(t):
                            pe.wait_ge(s_xhat, NT * b + t + 1)
                            for k in range(KD):
                                m = pe.transpose(ps[:, t % 2, k * P:(k + 1) * P], x_in[:, t, k * P:(k + 1) * P], ident[:, :])
                            m.then_inc(s_xT, 1)

                        turn(0)
                        for t in range(NT):
                            if t + 1 < NT:
                                turn(t + 1)
                            pe.wait_ge(s_hT, NT * b + t + 1)
                            if t >= 2:
                                pe.wait_ge(s_yev, NT * b + t - 1)
                            for bank, lo, n in ((0, 0, 2 * D), (1, 2 * D, D)):
                                for k in range(KD):
                                    m = pe.matmul(ps[:, 2 + 2 * (t % 2) + bank, 0:n], h_t[:, t % 2, k, :],
                                                  w_t[:, k, lo:lo + n], start=k == 0, stop=k == KD - 1)
                            m.then_inc(s_qkv, 1)
                        with pe.Fori(0, NG) as g:
                            gi = b * NG + g
                            pe.wait_ge(s_stage, gi + 1)
                            for bank, src in ((0, q_st), (2, k_st)):
                                for t in range(NT):
                                    m = pe.transpose(ps[:, bank + t // 4, (t % 4) * P:(t % 4 + 1) * P],
                                                     src[:, t].rearrange("p h s d -> p (h s d)"), ident[:, :])
                            m.then_inc(s_rT, 1)
                            with pe.Fori(0, NT) as i:
                                pe.wait_ge(s_qt, gi * NT + i + 1)
                                for j in range(HG):
                                    u = (gi * NT + i) * HG + j
                                    r = slice(32 * j, 32 * j + 32)
                                    for half in range(2):
                                        m = pe.matmul(ps[:, 4 + half, :], q_tile[r, :], k_rows[r, 512 * half:512 * half + 512],
                                                      start=True, stop=True)
                                    m.then_inc(s_S, 1)
                                    pe.wait_ge(s_pk, u + 1)
                                    for t in range(NT):
                                        m = pe.transpose(ps[:, 6 + t // 4, (t % 4) * P:(t % 4 + 1) * P],
                                                         prob[:, t * P:(t + 1) * P], ident[:, :])
                                    m.then_inc(s_pT, 1)
                                    pe.wait_ge(s_pts, u + 1)
                                    for t in range(NT):
                                        m = pe.matmul(ps[:, 0, 0:HD + 1], prob_t[:, t, :], v_st[:, t, j, :],
                                                      start=t == 0, stop=t == NT - 1)
                                    m.then_inc(s_O, 1)

                        def turn_o(t):
                            if t == 0:
                                pe.wait_ge(s_otok, b + 2)
                            if t >= 2:
                                pe.wait_ge(s_oev, NT * b + t - 1)
                            for k in range(KD):
                                m = pe.transpose(ps[:, t % 2, k * P:(k + 1) * P],
                                                 o_tok[:, t].rearrange("p h d -> p (h d)")[:, k * P:(k + 1) * P], ident[:, :])
                            m.then_inc(s_oT, 1)

                        turn_o(0)
                        for t in range(NT):
                            if t + 1 < NT:
                                turn_o(t + 1)
                            pe.wait_ge(s_oev, NT * b + t + 1)
                            if t >= 2:
                                pe.wait_ge(s_xr_free, NT * b + t)
                            for k in range(KD):
                                m = pe.matmul(ps[:, 2 + t % 2, 0:D], o_t[:, t % 2, k, :], wo_t[:, k, :],
                                              start=k == 0, stop=k == KD - 1)
                            m.then_inc(s_Y, 1)

                        def turn_h(t):
                            pe.wait_ge(s_h2, NT * b + t + 1)
                            if t >= 2:
                                pe.wait_ge(s_h2ev, NT * b + t - 1)
                            for k in range(KD):
                                m = pe.transpose(ps[:, 4 + t % 2, k * P:(k + 1) * P], h2p[:, t, k * P:(k + 1) * P], ident[:, :])
                            m.then_inc(s_h2T, 1)

                        turn_h(0)
                        for t in range(NT):
                            if t + 1 < NT:
                                turn_h(t + 1)
                            pe.wait_ge(s_h2ev, NT * b + t + 1)
                            lo = ps[:, 6, t * E:(t + 1) * E]
                            for k in range(KD):
                                pe.matmul(lo, h_t[:, t % 2, k, :], rw_sb[:, k, :], start=k == 0, stop=False)
                            m = pe.matmul(lo, ones_f[0:1, :], rb_sb[:, :], start=False, stop=True)
                        m.then_inc(s_log, 1)
                pe.nop()

            @blk.vector
            def _(dve):
                general = dve.value_load(bad_f[0:1, 0:1])
                with dve.If(general == 1):
                    dve.wait_ge(s_causal, 1)
                    dve.sem_inc(s_x_free, 1)
                    dve.sem_inc(s_xr_free, 1)
                    dve.sem_inc(s_otok, 1)
                    with dve.Fori(0, B) as b:
                        dve.tensor_copy(mod_b[:, :, :], mod_t[:, :, :, bass.ds(b, 1)].rearrange("p j k o -> p j (k o)"))
                        dve.tensor_copy(pick_b[:, :], ident[0:B, bass.ds(b, 1)].to_broadcast([B, P]))
                        dve.drain()
                        for k in range(KD):
                            dve.tensor_scalar(wo_ga[:, k, :], wo_nat[:, k, :], mod_b[:, 2, k:k + 1], None, ALU.mult)
                        dve.drain().then_inc(s_woga, 1)
                        dve.wait_ge(s_x, 16 * (b + 1))
                        for t in range(NT):
                            dve.bn_stats(st[:, t, :], x_in[:, t, :])
                        dve.drain()
                        for t in range(NT):
                            dve.bn_aggr(mv[:, t, :], st[:, t, :])
                        dve.drain()
                        dve.tensor_scalar(var_e[:, :], mv[:, :, 1], EPS, None, ALU.add)
                        dve.drain().then_inc(s_var, 1)
                        dve.wait_ge(s_woT, b + 1)
                        dve.tensor_copy(wo_t[:, :, :], ps[:, 6, :].rearrange("p (k d) -> p k d", k=KD))
                        dve.wait_ge(s_bc, b + 1)
                        dve.tensor_copy(bc[:, :], ps[:, 7, :])
                        dve.wait_ge(s_rstd, b + 1)
                        for t in range(NT):
                            dve.tensor_scalar(x_in[:, t, :], x_in[:, t, :], mv[:, t, 0:1], rstd[:, t:t + 1],
                                              ALU.subtract, ALU.mult).then_inc(s_xhat, 1)
                        for t in range(NT):
                            dve.wait_ge(s_xT, NT * b + t + 1)
                            if t >= 2:
                                dve.wait_ge(s_qkv, NT * b + t - 1)
                            for k in range(KD):
                                m = dve.tensor_scalar(h_t[:, t % 2, k, :], ps[:, t % 2, k * P:(k + 1) * P],
                                                      mod_b[:, 1, k:k + 1], mod_b[:, 0, k:k + 1], ALU.mult, ALU.add)
                            m.then_inc(s_hT, 1)
                            dve.wait_ge(s_yev, NT * b + t + 1)
                            a = y_abs[:, t % 2]
                            dve.tensor_reduce(y_max[:, :], a, AX.X, ALU.max)
                            dve.drain()
                            dve.tensor_tensor(y_eq[:, :, :], a, y_max[:, :].unsqueeze(2).to_broadcast([P, 3 * NH, HD]),
                                              ALU.is_equal)
                            dve.drain()
                            dve.tensor_tensor(y_ord[:, :, :], y_eq[:, :, :], first_of[:, :].unsqueeze(1).to_broadcast([P, 3 * NH, HD]), ALU.mult)
                            dve.drain()
                            dve.tensor_reduce(y_first[:, :], y_ord[:, :, :], AX.X, ALU.max)
                            dve.drain()
                            dve.tensor_tensor(y_one[:, t % 2], y_ord[:, :, :],
                                              y_first[:, :].unsqueeze(2).to_broadcast([P, 3 * NH, HD]),
                                              ALU.is_equal)
                            dve.drain().then_inc(s_one, 1)
                        dve.drain().then_inc(s_x_free, 1)
                        dve.wait_ge(s_keep, NT * (b + 1))
                        dve.memset(stand[:, :], 0.0)
                        with dve.Fori(0, NG) as g:
                            gi = b * NG + g
                            hs = bass.ds(g * HG, HG)
                            dve.tensor_copy(q_st[:, :, :, 0, :], qkv[:, :, 0, hs, :])
                            dve.tensor_scalar(q_st[:, :, :, 1, :], qkv[:, :, 0, hs, :], -1.0, None, ALU.mult)
                            dve.tensor_scalar(k_st[:, :, :, 0, :], qkv[:, :, 1, hs, :], 0.0, None, ALU.max)
                            dve.tensor_scalar(k_st[:, :, :, 1, :], qkv[:, :, 1, hs, :], -1.0, 0.0, ALU.mult, ALU.max)
                            dve.tensor_copy(v_st[:, :, :, 0:HD], qkv[:, :, 2, hs, :])
                            dve.drain().then_inc(s_stage, 1)
                            with dve.Fori(0, NT) as i:
                                dve.wait_ge(s_rows, gi + 1)
                                dve.tensor_copy(q_tile[:, :], q_rows[:, bass.ds(i * P, P)])
                                dve.drain().then_inc(s_qt, 1)
                                for j in range(HG):
                                    u = (gi * NT + i) * HG + j
                                    dve.wait_ge(s_S, u + 1)
                                    dve.memset(stand[:, :], 0.0)
                                    dve.tensor_tensor(sc[:, :], ps[:, 4:6, :].rearrange("p a b -> p (a b)"),
                                                      causal[:, bass.ds((7 - i) * P, T)], ALU.add)
                                    dve.drain()
                                    for r in range(TOPK // 8):
                                        src = sc if r == 0 else work
                                        dve.max(top8[:, 8 * r:8 * r + 8], src[:, :])
                                        dve.drain()
                                        if r == 0:
                                            dve.tensor_scalar(neg_m[:, :], top8[:, 0:1], -0.25, None, ALU.mult)
                                            dve.drain().then_inc(s_m, 1)
                                        dve.match_replace(work[:, :], top8[:, 8 * r:8 * r + 8], src[:, :], TAKEN)
                                        dve.drain()
                                    dve.wait_ge(s_p, u + 1)
                                    dve.scalar_tensor_tensor(prob[:, :], work[:, :], TAKEN, prob[:, :], ALU.is_equal,
                                                             ALU.mult)
                                    dve.drain().then_inc(s_pk, 1)
                                    dve.wait_ge(s_O, u + 1)
                                    dve.reciprocal(z_inv[:, :], ps[:, 0, HD:HD + 1])
                                    dve.drain()
                                    dve.tensor_scalar(o_tok[:, bass.ds(i, 1), bass.ds(g * HG + j, 1), :].rearrange(
                                        "p a b d -> p (a b d)"), ps[:, 0, 0:HD], z_inv[:, :], None, ALU.mult)
                        dve.drain().then_inc(s_otok, 1)
                        dve.wait_ge(s_xr, 16 * (b + 1))
                        for t in range(NT):
                            dve.wait_ge(s_Y, NT * b + t + 1)
                            dve.tensor_tensor(x2[:, t, :], ps[:, 2 + t % 2, 0:D], x_res[:, t, :],
                                              ALU.add).then_inc(s_xr_free, 1)
                        dve.drain().then_inc(s_x2, 1)
                        for t in range(NT):
                            dve.bn_stats(st[:, t, :], x2[:, t, :])
                        dve.drain()
                        for t in range(NT):
                            dve.bn_aggr(mv[:, t, :], st[:, t, :])
                        dve.drain()
                        dve.tensor_scalar(var_e[:, :], mv[:, :, 1], EPS, None, ALU.add)
                        dve.drain().then_inc(s_var2, 1)
                        dve.wait_ge(s_rstd2, b + 1)
                        for t in range(NT):
                            h = h2p[:, t, 0:D]
                            dve.tensor_scalar(h, x2[:, t, :], mv[:, t, 0:1], rstd[:, t:t + 1], ALU.subtract, ALU.mult)
                            dve.drain()
                            dve.tensor_tensor(h, h, bc[:, D:2 * D], ALU.mult)
                            dve.drain()
                            dve.tensor_tensor(h, h, bc[:, 0:D], ALU.add)
                            dve.drain().then_inc(s_h2, 1)
                        dve.wait_ge(s_log, b + 1)
                        lg = ps[:, 6, 0:NT * E].rearrange("p (n e) -> p n e", e=E)
                        dve.tensor_reduce(l_max[:, :], lg, AX.X, ALU.max)
                        dve.drain()
                        dve.tensor_tensor(logit[:, :, :], lg, l_max[:, :].unsqueeze(2).to_broadcast([P, NT, E]), ALU.subtract)
                        dve.drain().then_inc(s_lm, 1)
                        dve.wait_ge(s_lexp, b + 1)
                        dve.tensor_reduce(l_max[:, :], logit[:, :, :], AX.X, ALU.add)
                        dve.drain()
                        dve.reciprocal(l_max[:, :], l_max[:, :])
                        dve.drain()
                        dve.tensor_tensor(h2p[:, :, D:ROW], logit[:, :, :], l_max[:, :].unsqueeze(2).to_broadcast([P, NT, E]),
                                          ALU.mult)
                        dve.drain()
                        dve.tensor_copy(probs[:, bass.ds(b * NT, NT), :], h2p[:, :, D:ROW])
                        dve.drain().then_inc(s_pr, 1)
                        dve.wait_ge(s_out, 32 * (b + 1))
                dve.nop()
        gen.close()

        att.close()
        b2_sb = sb("b2_sb", [1, E, D])
        w1_sb = sb("w1_sb", [P, 2, KD, DFF])
        w2_sb = sb("w2_sb", [P, 2, FO, D])
        sel = ExitStack()

        def sbs(name, shape, dt=F32):
            return sel.enter_context(nc.sbuf_tensor(name, shape, dt))

        gate_q = sbs("gate_q", [P, 2, P])
        junk = sbs("junk", [P, 2 * P], BF16)
        zeros = sbs("zeros", [P, P])
        thr = sbs("thr", [P, 1], U32)
        cand = sbs("cand", [P, 1], U32)
        step_u = sbs("step_u", [P, 1], U32)
        cnt = sbs("cnt", [P, 1])
        cnt2 = sbs("cnt2", [P, 2])
        need = sbs("need", [P, 1])
        start2 = sbs("start2", [P, 2])
        above = sbs("above", [P, 2, P])
        equal = sbs("equal", [P, 2, P])
        rank = sbs("rank", [P, 2, P])
        slot = sbs("slot", [P, NTALL, E])
        slot_i = sbs("slot_i", [P, 2, NTALL, E], I32)
        slot_f = sbs("slot_f", [P, 2, NTALL, E])
        oh_lo = sbs("oh_lo", [P, NTALL, E, 32], BF16)
        oh_hi = sbs("oh_hi", [P, NTALL, E, 2, 16], BF16)
        ids_f = sbs("ids_f", [32, E, 2, 16])
        b1_nat = sbs("b1_nat", [E * FO, P])
        s_gT, s_gq, s_cnt, s_tot = sem("s_gT"), sem("s_gq"), sem("s_cnt"), sem("s_tot")
        s_c2, s_off, s_sel, s_slT, s_oh, s_ids, s_idx = (sem(n) for n in
                                                        ("s_c2", "s_off", "s_sel", "s_slT", "s_oh", "s_ids", "s_idx"))
        s_b, s_b1T, s_b1 = sem("s_b"), sem("s_b1T"), sem("s_b1")

        with nc.Block() as blk:
            @blk.sync
            def _(sp):
                sp.dma_start(b1_nat[:, :], b1.rearrange("e (o p) -> (e o) p", p=P)).then_inc(s_b, 16)
                sp.dma_start(b2_sb[:, :, :], b2.rearrange("(o e) d -> o e d", o=1)).then_inc(s_b, 16)
                sp.wait_ge(s_b, 32)

            @blk.scalar
            def _(act):
                act.wait_ge(s_gT, 1)
                act.activation(gate_q[:, :, :], ps[:, 0, 0:2 * P].rearrange("p (a b) -> p a b", a=2),
                               ACT.Copy).then_inc(s_gq, 1)
                act.wait_ge(s_b1T, 1)
                act.activation(b1_t[:, :], ps[:, 1, 0:E * FO], ACT.Copy).then_inc(s_b1, 1)

            @blk.tensor
            def _(pe):
                flat = probs[:, :, :].rearrange("p n e -> p (n e)")
                for a in range(2):
                    m = pe.transpose(ps[:, 0, a * P:(a + 1) * P], flat[:, a * P:(a + 1) * P], ident[:, :])
                m.then_inc(s_gT, 1)
                pe.wait_ge(s_b, 32)
                pe.transpose(ps[:, 1, 0:E * FO], b1_nat[:, :], ident[0:E * FO, 0:E * FO]).then_inc(s_b1T, 1)
                with pe.Fori(0, 30) as k:
                    pe.wait_ge(s_cnt, k + 1)
                    pe.matmul(ps[:, 2, 0:1], same_e[:, :], cnt[:, :], start=True, stop=True).then_inc(s_tot, 1)
                for r in range(2):
                    pe.wait_ge(s_c2, r + 1)
                    pe.matmul(ps[:, 3, 0:1], same_e[:, :], cnt[:, :], start=True, stop=True)
                    pe.matmul(ps[:, 3, 1:3], before_e[:, :], cnt2[:, :], start=True, stop=True)
                    pe.matmul(ps[:, 3, 3:4], same_e[:, :], cnt2[:, 0:1], start=True, stop=True).then_inc(s_off, 1)
                pe.wait_ge(s_sel, 1)
                for a in range(2):
                    m = pe.transpose(ps[:, 4, a * P:(a + 1) * P], rank[:, a, :], ident[:, :])
                m.then_inc(s_slT, 1)
                pe.wait_ge(s_oh, 1)
                for e in range(E):
                    for n in range(NTALL):
                        m = pe.matmul(ps[0:32, 5, e * 32:(e + 1) * 32], oh_lo[:, n, e, :],
                                      oh_hi[:, n, e].rearrange("p a h -> p (a h)"), start=n == 0, stop=n == NTALL - 1)
                m.then_inc(s_ids, 1)

            @blk.vector
            def _(dve):
                dve.memset(thr[:, :], 0)
                dve.memset(zeros[:, :], 0.0)
                dve.wait_ge(s_gq, 1)
                gates = gate_q[:, :, :].rearrange("p a b -> p (a b)")
                dve.drain()
                with dve.Fori(0, 30) as k:
                    dve.tensor_tensor(cand[:, :], thr[:, :], bit_u[:, bass.ds(k, 1)], ALU.bitwise_or)
                    dve.drain()
                    dve.tensor_scalar(junk[:, :], gates, cand[:, :].bitcast(F32), None, ALU.is_ge, ALU.add,
                                      accum_out=cnt[:, :])
                    dve.drain().then_inc(s_cnt, 1)
                    dve.wait_ge(s_tot, k + 1)
                    dve.tensor_scalar(step_u[:, :], ps[:, 2, 0:1], float(CAP), bit_f[:, bass.ds(k, 1)], ALU.is_ge,
                                      ALU.mult)
                    dve.drain()
                    dve.tensor_tensor(thr[:, :], thr[:, :], step_u[:, :], ALU.bitwise_or)
                    dve.drain()
                t = thr[:, :].bitcast(F32)
                dve.tensor_scalar(above[:, :, :].rearrange("p a b -> p (a b)"), gates, t, None, ALU.is_gt)
                dve.tensor_scalar(equal[:, :, :].rearrange("p a b -> p (a b)"), gates, t, None, ALU.is_equal)
                dve.drain()
                for r, src in ((0, equal), (1, above)):
                    if r == 0:
                        dve.tensor_reduce(cnt[:, :], above[:, :, :], AX.XY, ALU.add)
                    dve.tensor_reduce(cnt2[:, :], src[:, :, :], AX.X, ALU.add)
                    dve.drain().then_inc(s_c2, 1)
                    dve.wait_ge(s_off, r + 1)
                    dve.tensor_copy(start2[:, :], ps[:, 3, 1:3])
                    dve.tensor_scalar(need[:, :], ps[:, 3, 0:1], -1.0, float(CAP), ALU.mult, ALU.add)
                    dve.drain()
                    dve.tensor_tensor(start2[:, 1:2], start2[:, 1:2], ps[:, 3, 3:4], ALU.add)
                    dve.drain()
                    for a in range(2):
                        dve.tensor_tensor_scan(rank[:, a, :], src[:, a, :], zeros[:, :], start2[:, a:a + 1], ALU.add,
                                               ALU.max)
                    dve.drain()
                    if r == 0:
                        dve.scalar_tensor_tensor(equal[:, :, :], rank[:, :, :], need[:, :], equal[:, :, :], ALU.is_le,
                                                 ALU.mult)
                        dve.drain()
                        dve.tensor_tensor(above[:, :, :], above[:, :, :], equal[:, :, :], ALU.add)
                        dve.drain()
                dve.scalar_tensor_tensor(rank[:, :, :], rank[:, :, :], -1025.0, above[:, :, :], ALU.add, ALU.mult)
                dve.drain()
                dve.tensor_scalar(rank[:, :, :], rank[:, :, :], 1024.0, None, ALU.add)
                dve.drain().then_inc(s_sel, 1)
                dve.wait_ge(s_slT, 1)
                dve.tensor_copy(slot_i[:, 0].rearrange("p n e -> p (n e)"), ps[:, 4, 0:2 * P])
                dve.drain()
                dve.tensor_scalar(slot_i[:, 1], slot_i[:, 0], 31, None, ALU.bitwise_and)
                dve.drain()
                dve.tensor_scalar(slot_i[:, 0], slot_i[:, 0], 5, None, ALU.logical_shift_right)
                dve.drain()
                dve.tensor_copy(slot_f[:, :, :, :], slot_i[:, :, :, :])
                dve.drain()
                for e in range(E):
                    dve.tensor_tensor(oh_lo[:, :, e, :], slot_f[:, 1, :, e].unsqueeze(2).to_broadcast([P, NTALL, 32]),
                                      iota_lo[:, :].unsqueeze(1).to_broadcast([P, NTALL, 32]), ALU.is_equal)
                    dve.tensor_tensor(oh_hi[:, :, e, 0, :], slot_f[:, 0, :, e].unsqueeze(2).to_broadcast([P, NTALL, 16]),
                                      iota_hi[:, :].unsqueeze(1).to_broadcast([P, NTALL, 16]), ALU.is_equal)
                dve.drain()
                for e in range(E):
                    dve.tensor_tensor(oh_hi[:, :, e, 1, :], oh_hi[:, :, e, 0, :],
                                      tile_no[:, :].unsqueeze(2).to_broadcast([P, NTALL, 16]), ALU.mult)
                dve.drain()
                for e in range(E):
                    dve.tensor_scalar(oh_hi[:, :, e, 0, :], oh_hi[:, :, e, 0, :], p_col[:, :], None, ALU.mult)
                dve.drain().then_inc(s_oh, 1)
                dve.wait_ge(s_ids, 1)
                dve.tensor_copy(ids_f[:, :, :, :].rearrange("p e a h -> p (e a h)"), ps[0:32, 5, 0:E * 32])
                dve.drain()
                dve.tensor_tensor(ids_f[:, :, 0, :], ids_f[:, :, 0, :], ids_f[:, :, 1, :], ALU.add)
                dve.drain()
                for q in range(CC):
                    dve.tensor_copy(ids[32 * q:32 * q + 32, :, :],
                                    ids_f[:, :, 0, :].rearrange("p e (c q) -> p e c q", q=4)[:, :, :, q])
                dve.drain()
                dve.tensor_scalar(bat[:, :, :], ids[:, :, :], 10, None, ALU.logical_shift_right)
                dve.drain().then_inc(s_idx, 1)

        sel.close()
        idx_e = sb("idx_e", [P, 2, CC], U32)
        bat_e = sb("bat_e", [P, 2, CC], U32)
        tok = sb("tok", [P, 2, CC, ROW])
        gbk = sb("gbk", [P, 2, CC, D])
        tok_t = sb("tok_t", [P, KD, CAP])
        gate = sb("gate", [P, 2, CC])
        b1_e = sb("b1_e", [P, FO])
        b2_e = sb("b2_e", [1, D])
        h1_t = sb("h1_t", [P, FO, CAP])
        ctr = sb("ctr", [P, 2, CC, D])
        s_w12 = [sem("s_w12_0"), sem("s_w12_1")]
        s_ie, s_g0, s_g1, s_tT, s_tt = (sem(n) for n in ("s_ie", "s_g0", "s_g1", "s_tT", "s_tt"))
        s_g = [s_g0, s_g1]
        s_L1, s_h1, s_L2, s_ctr, s_sc, s_be = (sem(n) for n in ("s_L1", "s_h1", "s_L2", "s_ctr", "s_sc", "s_be"))

        with nc.Block() as blk:
            @blk.sync
            def _(sp):
                with sp.Fori(0, E // 2) as ep:
                    for a in range(2):
                        e = 2 * ep + a
                        sp.wait_ge(s_L2, CC * e + 1)
                        sp.dma_start(w1_sb[:, a], w1[bass.ds(e, 1)].rearrange("o (k p) f -> p (o k) f", p=P)).then_inc(s_w12[a], 16)
                        sp.dma_start(w2_sb[:, a], w2[bass.ds(e, 1)].rearrange("o (k p) f -> p (o k) f", p=P)).then_inc(s_w12[a], 16)

            @blk.gpsimd
            def _(pool):
                with pool.Fori(0, E // 2) as ep:
                    for a in range(2):
                        e = 2 * ep + a
                        pool.tensor_copy(idx_e[:, a, :], ids[:, bass.ds(e, 1), :].rearrange("p o c -> p (o c)"))
                        pool.tensor_copy(bat_e[:, a, :], bat[:, bass.ds(e, 1), :].rearrange("p o c -> p (o c)"))
                        pool.drain()
                        for k in range(CC):
                            pool.indirect_dma_start(tok[:, a, k, :], None, h_table,
                                                    bass.IndirectOffsetOnAxis(idx_e[:, a, k:k + 1], 0)).then_inc(s_g[a], 16)
                            pool.indirect_dma_start(gbk[:, a, k, :], None, gb_table,
                                                    bass.IndirectOffsetOnAxis(bat_e[:, a, k:k + 1], 0)).then_inc(s_g[a], 16)
                        for k in range(CC):
                            pool.wait_ge(s_ctr, CC * e + k + 1)
                            pool.tensor_tensor(stand_p[:, :], ones_f[:, 0:1], ones_f[:, 0:1], ALU.add)
                            pool.drain()
                            pool.indirect_dma_start(out_rows, bass.IndirectOffsetOnAxis(idx_e[:, a, k:k + 1], 0),
                                                    ctr[:, a, k, :], None, compute_op=ALU.add).then_inc(s_sc, 16)
                        pool.wait_ge(s_sc, 16 * CC * (e + 1))
                        pool.tensor_tensor(stand_p[:, :], ones_f[:, 0:1], ones_f[:, 0:1], ALU.add)
                        pool.drain()

            @blk.tensor
            def _(pe):
                with pe.Fori(0, E // 2) as ep:
                    for a in range(2):
                        e = 2 * ep + a
                        pe.wait_ge(s_g[a], 32 * CC * (ep + 1))
                        for k in range(KD):
                            for q in range(CC):
                                m = pe.transpose(ps[:, k, q * P:(q + 1) * P], tok[:, a, q, k * P:(k + 1) * P], ident[:, :])
                        m.then_inc(s_tT, 1)
                        pe.wait_ge(s_tt, e + 1)
                        pe.wait_ge(s_w12[a], 32 * (ep + 1))
                        for f in range(FO):
                            if f >= 2:
                                pe.wait_ge(s_h1, FO * e + f - 1)
                            for k in range(KD):
                                m = pe.matmul(ps[:, 2 + f % 2, :], w1_sb[:, a, k, f * P:(f + 1) * P], tok_t[:, k, :],
                                              start=k == 0, stop=k == KD - 1)
                            m.then_inc(s_L1, 1)
                        pe.wait_ge(s_h1, FO * (e + 1))
                        for q in range(CC):
                            if q >= 2:
                                pe.wait_ge(s_ctr, CC * e + q - 1)
                            for f in range(FO):
                                pe.matmul(ps[:, 4 + q % 2, 0:D], h1_t[:, f, q * P:(q + 1) * P], w2_sb[:, a, f, :],
                                          start=f == 0, stop=False)
                            pe.matmul(ps[:, 4 + q % 2, 0:D], ones_f[0:1, :], b2_e[:, :], start=False,
                                      stop=True).then_inc(s_L2, 1)

            @blk.scalar
            def _(act):
                with act.Fori(0, E // 2) as ep:
                    for a in range(2):
                        e = 2 * ep + a
                        act.wait_ge(s_be, e + 1)
                        for f in range(FO):
                            act.wait_ge(s_L1, FO * e + f + 1)
                            act.activation(h1_t[:, f, :], ps[:, 2 + f % 2, :], ACT.Relu,
                                           bias=b1_e[:, f:f + 1]).then_inc(s_h1, 1)

            @blk.vector
            def _(dve):
                dve.drain().then_inc(s_L2, 1)
                with dve.Fori(0, E // 2) as ep:
                    for a in range(2):
                        e = 2 * ep + a
                        dve.wait_ge(s_tT, e + 1)
                        dve.tensor_copy(tok_t[:, :, :], ps[:, 0:2, :]).then_inc(s_tt, 1)
                        dve.tensor_copy(b1_e[:, :], b1_t[:, bass.ds(e * FO, FO)])
                        dve.tensor_copy(b2_e[:, :], b2_sb[:, bass.ds(e, 1), :].rearrange("p o d -> p (o d)"))
                        dve.tensor_copy(gate[:, a, :], tok[:, a, :, bass.ds(D + e, 1)].rearrange("p c o -> p (c o)"))
                        dve.drain().then_inc(s_be, 1)
                        for q in range(CC):
                            dve.wait_ge(s_L2, CC * e + q + 2)
                            dve.scalar_tensor_tensor(ctr[:, a, q, :], ps[:, 4 + q % 2, 0:D], gate[:, a, q:q + 1],
                                                     gbk[:, a, q, :], ALU.mult, ALU.mult).then_inc(s_ctr, 1)


_INS = ["L0_attn_x", "L0_attn_wq", "L0_attn_wk", "L0_attn_wv", "L0_attn_wo", "L0_ffn_router_w", "L0_ffn_router_b",
        "L0_ffn_w1", "L0_ffn_b1", "L0_ffn_w2", "L0_ffn_b2", "L0_c", "L0_wmod"]
_OUTS = [((B, T, D), "float32")]


def kernel(**inputs):
    import numpy as _np
    import concourse.bacc as _bacc
    from concourse import mybir as _mybir
    from concourse.bass_utils import run_bass_kernel_spmd as _run

    nc = _bacc.Bacc("TRN2", target_bir_lowering=False, num_devices=1)
    arrays, args = {}, []
    for name in _INS:
        a = _np.ascontiguousarray(inputs[name])
        arrays[f"in_{name}_dram"] = a
        args.append(nc.dram_tensor(f"in_{name}_dram", a.shape, _mybir.dt.from_np(a.dtype), kind="ExternalInput").ap())
    for i, (shape, dtype) in enumerate(_OUTS):
        dt = _mybir.dt.from_np(_np.dtype(dtype))
        args.append(nc.dram_tensor(f"out_{i}_dram", shape, dt, kind="ExternalOutput").ap())
    build_kernel(nc, *args)
    r = _run(nc, [arrays], core_ids=[0])
    return r.results[0]["out_0_dram"]
```

```python
from contextlib import ExitStack

import concourse.bass as bass
from concourse import mybir

ALU = mybir.AluOpType
ACT = mybir.ActivationFunctionType
AX = mybir.AxisListType
F32 = mybir.dt.float32
BF16 = mybir.dt.bfloat16
I32 = mybir.dt.int32
U32 = mybir.dt.uint32

P = 128
B, T, D = 4, 1024, 256
N = B * T
NT = T // P
NTALL = N // P
KD = D // P
NH, HD = 16, 16
HG = 4
NG = NH // HG
TOPK = 64
E, DFF, CAP = 8, 1024, 512
FO = DFF // P
CC = CAP // P
ROW = D + E
BIG = 1.0e30
TAKEN = -3.0e38
EPS = 1e-5


def build_kernel(nc, x, wq, wk, wv, wo, router_w, router_b, w1, b1, w2, b2, c, wmod, out):
    with ExitStack() as ctx:
        def sb(name, shape, dt=F32):
            return ctx.enter_context(nc.sbuf_tensor(name, shape, dt))

        def sem(name):
            return ctx.enter_context(nc.semaphore(name))

        out_rows = out.rearrange("b t d -> (b t) d")
        h_table = nc.dram_tensor("h_table", [N, ROW], F32, kind="Internal").ap()
        gb_table = nc.dram_tensor("gb_table", [B, D], F32, kind="Internal").ap()

        ps = ctx.enter_context(nc.psum_tensor("ps", [P, 8, 512], F32))

        stand = sb("stand", [P, 1])
        stand_p = sb("stand_p", [P, 1])
        ident = sb("ident", [P, P])
        ones_f = sb("ones_f", [P, P])
        first_of = sb("first_of", [P, HD], BF16)
        same_e = sb("same_e", [P, P])
        before_e = sb("before_e", [P, P])
        e_of_q = sb("e_of_q", [P, E])
        iota_lo = sb("iota_lo", [P, 32], BF16)
        iota_hi = sb("iota_hi", [P, 16], BF16)
        p_col = sb("p_col", [P, 1])
        tile_no = sb("tile_no", [P, NTALL], BF16)
        bit_u = sb("bit_u", [P, 15, 3], U32)
        bit_f = sb("bit_f", [P, 15])

        bad_f = sb("bad_f", [1, 1], I32)
        probs = sb("probs", [P, NTALL, E])
        ids = sb("ids", [P, E, CC], U32)
        of_b = sb("of_b", [P, E, CC, B])
        b1_t = sb("b1_t", [P, E * FO])
        att = ExitStack()

        def sba(name, shape, dt=F32):
            return att.enter_context(nc.sbuf_tensor(name, shape, dt))

        wo_nat = sba("wo_nat", [P, KD, D])
        half_neg = sba("half_neg", [P, NT])
        w_t = sba("w_t", [P, KD, 3 * D])
        wo_t = sba("wo_t", [P, KD, D])
        mod_t = sba("mod_t", [P, 6, KD, B])
        mod_b = sba("mod_b", [P, 6, KD])
        mod_rows = sba("mod_rows", [B, 3 * D])
        pick_b = sba("pick_b", [B, P])
        rw_sb = sba("rw_sb", [P, KD, E])
        rb_sb = sba("rb_sb", [1, E])

        pro = ExitStack()

        def spr(name, shape, dt=F32):
            return pro.enter_context(nc.sbuf_tensor(name, shape, dt))

        w_nat = spr("w_nat", [P, 3, KD, D])
        wmod_sb = spr("wmod_sb", [P, KD, 6 * D])
        c_sb = spr("c_sb", [B, D])
        c_sig = spr("c_sig", [B, D])
        c_t = spr("c_t", [P, KD, B])
        g_abs = spr("g_abs", [P, 2 * KD * B])
        g_row = spr("g_row", [B, D])
        g_row2 = spr("g_row2", [B, D])

        s_const, s_w, s_wload = sem("s_const"), sem("s_w"), sem("s_wload")
        s_cload, s_mload = sem("s_cload"), sem("s_mload")
        s_pe_pro, s_ev_pro, s_tab = sem("s_pe_pro"), sem("s_ev_pro"), sem("s_tab")

        with nc.Block() as blk:
            @blk.sync
            def _(sp):
                sp.dma_start(c_sb[:, :], c).then_inc(s_cload, 16)
                for i, w in enumerate((wq, wk, wv)):
                    sp.dma_start(w_nat[:, i, :, :], w.rearrange("(k p) c -> p k c", p=P)).then_inc(s_wload, 16)
                sp.dma_start(wmod_sb[:, :, :], wmod.rearrange("(k p) m -> p k m", p=P)).then_inc(s_mload, 16)
                sp.dma_start(wo_nat[:, :, :], wo.rearrange("(k p) c -> p k c", p=P)).then_inc(s_mload, 16)
                sp.dma_start(rw_sb[:, :, :], router_w.rearrange("(k p) e -> p k e", p=P)).then_inc(s_mload, 16)
                sp.dma_start(rb_sb[:, :], router_b.rearrange("(o e) -> o e", o=1)).then_inc(s_mload, 16)
                sp.wait_ge(s_mload, 16 * 4)
                sp.wait_ge(s_w, 3)
                sp.dma_start(gb_table, mod_rows[:, 2 * D:3 * D]).then_inc(s_tab, 16)
                sp.wait_ge(s_tab, 16)

            @blk.gpsimd
            def _(pool):
                pool.memset(ones_f[:, :], 1.0)
                pool.memset(ident[:, :], 0.0)
                pool.memset(half_neg[:, :], -0.5)
                pool.iota(first_of[:, :], [[-1, HD]], base=HD, channel_multiplier=0,
                          allow_small_or_imprecise_dtypes=True)
                pool.iota(iota_lo[:, :], [[1, 32]], base=0, channel_multiplier=0,
                          allow_small_or_imprecise_dtypes=True)
                pool.iota(iota_hi[:, :], [[1, 16]], base=0, channel_multiplier=0,
                          allow_small_or_imprecise_dtypes=True)
                pool.iota(p_col[:, :], [[0, 1]], base=0, channel_multiplier=1,
                          allow_small_or_imprecise_dtypes=True)
                pool.iota(tile_no[:, :], [[P, NTALL]], base=0, channel_multiplier=0,
                          allow_small_or_imprecise_dtypes=True)
                for k in range(15):
                    for m in range(3):
                        pool.memset(bit_u[:, k, m:m + 1], (m + 1) << (28 - 2 * k))
                    pool.memset(bit_f[:, k:k + 1], float(1 << (28 - 2 * k)))
                pool.drain()
                pool.affine_select(ident[:, :], ident[:, :], [[-1, P]], ALU.not_equal, 1.0, base=0,
                                   channel_multiplier=1)
                pool.drain().then_inc(s_const, 1)
                pool.wait_ge(s_const, 2)
                pool.affine_select(before_e[:, :], same_e[:, :], [[1, P]], ALU.is_gt, 0.0, base=0,
                                   channel_multiplier=-1)
                pool.drain().then_inc(s_const, 1)

            @blk.vector
            def _(dve):
                dve.wait_ge(s_const, 1)
                dve.tensor_reduce(e_of_q[:, :], ident[:, :].rearrange("p (a e) -> p e a", e=E), AX.X, ALU.add)
                dve.drain()
                dve.tensor_copy(same_e[:, :].rearrange("p (a e) -> p a e", e=E),
                                e_of_q[:, :].unsqueeze(1).to_broadcast([P, P // E, E]))
                dve.drain().then_inc(s_const, 1)
                dve.wait_ge(s_ev_pro, 1)
                dve.tensor_scalar(c_sig[:, :], c_sig[:, :], 1.0, None, ALU.add)
                dve.drain()
                dve.reciprocal(c_sig[:, :], c_sig[:, :])
                dve.drain()
                dve.tensor_tensor(c_sig[:, :], c_sig[:, :], c_sb[:, :], ALU.mult)
                dve.drain().then_inc(s_w, 1)
                dve.wait_ge(s_pe_pro, 1)
                dve.tensor_copy(c_t[:, :, :], ps[:, 0, 0:KD * B].rearrange("p (k b) -> p k b", k=KD))
                dve.drain().then_inc(s_w, 1)
                for w in range(3):
                    dve.wait_ge(s_pe_pro, 2 + w)
                    dve.tensor_copy(w_t[:, :, w * D:(w + 1) * D], ps[:, 1 + w, :].rearrange("p (k d) -> p k d", k=KD))
                dve.wait_ge(s_pe_pro, 5)
                dve.tensor_copy(mod_t[:, :, :, :], ps[:, 4, 0:6 * KD * B].rearrange("p (j k b) -> p j k b", j=6, k=KD))
                dve.tensor_copy(mod_rows[:, 0:2 * D], ps[0:B, 5, :])
                dve.tensor_copy(g_row[:, :], ps[0:B, 6, 0:D])
                dve.drain()
                for g, out_g, tmp in ((mod_t[:, 2, :, :].rearrange("p k b -> p (k b)"), None, g_abs),
                                      (g_row[:, :], mod_rows[:, 2 * D:3 * D], g_row2)):
                    n = KD * B if out_g is None else D
                    a = tmp[:, 0:n]
                    dve.scalar_tensor_tensor(a, g, -1.0, g, ALU.mult, ALU.max)
                    dve.drain()
                    s = tmp[:, n:2 * n] if out_g is None else c_sig[:, :]
                    dve.tensor_scalar(s, g, 0.0, 2.0, ALU.is_ge, ALU.mult)
                    dve.tensor_scalar(a, a, 0.25, None, ALU.max)
                    dve.drain()
                    dve.scalar_tensor_tensor(g if out_g is None else out_g, s, -1.0, a, ALU.add, ALU.mult)
                for j in (1, 4):
                    v = mod_t[:, j, :, :].rearrange("p k b -> p (k b)")
                    dve.tensor_scalar(v, v, 1.0, None, ALU.add)
                dve.tensor_scalar(mod_rows[:, D:2 * D], mod_rows[:, D:2 * D], 1.0, None, ALU.add)
                dve.drain().then_inc(s_w, 1)

            @blk.scalar
            def _(act):
                act.wait_ge(s_cload, 16)
                act.activation(c_sig[:, :], c_sb[:, :], ACT.Exp, scale=-1.0)
                act.drain().then_inc(s_ev_pro, 1)

            @blk.tensor
            def _(pe):
                pe.wait_ge(s_const, 1)
                pe.wait_ge(s_w, 1)
                for k in range(KD):
                    m = pe.transpose(ps[:, 0, k * B:(k + 1) * B], c_sig[:, k * P:(k + 1) * P], ident[0:B, 0:B])
                m.then_inc(s_pe_pro, 1)
                pe.wait_ge(s_wload, 16 * 3)
                for w in range(3):
                    for k in range(KD):
                        for h in range(KD):
                            m = pe.transpose(ps[:, 1 + w, k * D + h * P:k * D + (h + 1) * P],
                                             w_nat[:, w, h, k * P:(k + 1) * P], ident[:, :])
                    m.then_inc(s_pe_pro, 1)
                pe.wait_ge(s_w, 2)
                pe.wait_ge(s_mload, 16 * 4)
                for m6 in range(6 * KD):
                    for k in range(KD):
                        pe.matmul(ps[:, 4, m6 * B:(m6 + 1) * B], wmod_sb[:, k, m6 * P:(m6 + 1) * P], c_t[:, k, :],
                                  start=k == 0, stop=k == KD - 1)
                for bank, lo, n in ((5, 3 * D, 2 * D), (6, 5 * D, D)):
                    for k in range(KD):
                        m = pe.matmul(ps[0:B, bank, 0:n], c_t[:, k, :], wmod_sb[:, k, lo:lo + n],
                                      start=k == 0, stop=k == KD - 1)
                m.then_inc(s_pe_pro, 1)
        pro.close()

        x_v = x.rearrange("b (n p) d -> b p n d", p=P)
        out_v = out.rearrange("b (n p) d -> b p n d", p=P)
        h_v = h_table.rearrange("(b n p) d -> b p n d", b=B, p=P)

        fst = ExitStack()

        def sf(name, shape, dt=F32):
            return fst.enter_context(nc.sbuf_tensor(name, shape, dt))

        st = sf("st", [P, NT, 6])
        mv = sf("mv", [P, NT, 2])
        var_e = sf("var_e", [P, NT])
        rstd = sf("rstd", [P, NT])
        y_mx = sf("y_mx", [P, NT, 3 * NH])
        y_cnt = sf("y_cnt", [P, NT])
        y_ext = sf("y_ext", [P, 3])
        y_hi = sf("y_hi", [P, 1])
        y_lo = sf("y_lo", [P, 1])
        y_most = sf("y_most", [P, 1])
        qkv = sf("qkv", [P, NT, 3, NH, HD])
        q_st = sf("q_st", [P, NT, HG, 2, HD])
        k_st = sf("k_st", [P, NT, HG, 2, HD])
        kn_st = sf("kn_st", [P, HG, 2, HD])
        v_st = sf("v_st", [P, 2, NT, HG, 32])
        vz_r = sf("vz_r", [P, HG, 32])
        vz = sf("vz", [P, 2, 3, HG, 32], BF16)
        kx = sf("kx", [P, T])
        cn = sf("cn", [P, T], BF16)
        x_in = sf("x_in", [P, NT, D])
        mx = x_in[:, 0:NT // 2, :].rearrange("p n d -> p (n d)")
        q1 = x_in[:, NT // 2:NT, :].rearrange("p n d -> p (n d)").bitcast(BF16).rearrange("p (a t) -> p a t", a=2)
        qn = sf("qn", [P, 2, T], BF16)
        parts = sf("parts", [P, 8, T], BF16)
        A1 = sf("A1", [P, 2, HG, T], BF16)
        A2 = sf("A2", [P, 2, HG, T], BF16)
        R1 = sf("R1", [P, 2, HG, T], BF16)
        R2 = sf("R2", [P, 2, HG, T], BF16)
        p_buf = sf("p_buf", [P, 2, HG, 512])
        p_flat = p_buf[:, :, :, :].rearrange("p a h t -> p (a h t)")
        YN = 3 * NH * HD
        y_abs = p_flat[:, 0:2 * YN].rearrange("p (a j d) -> p a j d", a=2, d=HD)
        y_val = p_flat[:, 2 * YN:4 * YN].rearrange("p (a j d) -> p a j d", a=2, d=HD)
        y_one = p_flat[:, 4 * YN:5 * YN].bitcast(BF16).rearrange("p (a j d) -> p a j d", a=2, d=HD)
        y_drop = parts[:, 0, 0:YN]
        h2p = sf("h2p", [P, NT, ROW])
        h_flat = h2p[:, :, :].rearrange("p n r -> p (n r)")
        zm = h_flat[:, 0:2 * 512].bitcast(BF16).rearrange("p (h t) -> p h t", h=HG)
        k1zf = h_flat[:, 1024:1536].rearrange("p (h t) -> p h t", h=HG)
        k0swz = h_flat[:, 1536:1792].bitcast(BF16).rearrange("p (h t) -> p h t", h=HG)
        lw = h_flat[:, 1792:2048].bitcast(BF16).rearrange("p (h t) -> p h t", h=HG)
        em = sf("em", [P, 2, NT, HG])
        gz = sf("gz", [P, 2, HG, P], BF16)
        g_a = sf("g_a", [P, P], BF16)
        k128 = sf("k128", [P, P])
        q128 = sf("q128", [P, P])
        q_first = sf("q_first", [P, 2, P], BF16)

        def q_parts(n):
            if n:
                return parts
            return p_buf[:, :, :, :].rearrange("p a h t -> p (a h t)").bitcast(BF16).rearrange("p (s t) -> p s t", s=8)

        def qx_of(n):
            return kx[:, :] if n else o_sb[:, :, :].rearrange("p a t -> p (a t)")

        kxz = sf("kxz", [P, HG, P])
        k1zb = sf("k1zb", [P, HG, P], BF16)
        nk1f = sf("nk1f", [P, P])
        kb0 = sf("kb0", [P, P], BF16)
        knz = sf("knz", [P, HG, P])
        pn = sf("pn", [P, HG, P])
        wo_ga = pn[:, :, :].rearrange("p h t -> p (h t)").rearrange("p (k d) -> p k d", k=KD)
        o_sb = sf("o_sb", [P, 2, 512])
        h_t = o_sb[:, 0, :].rearrange("p (a k t) -> p a k t", a=2, k=KD)
        o_cmb = sf("o_cmb", [P, 4, HG, HD + 1])
        o_inv = sf("o_inv", [P, 4, HG])
        o_tok = qkv[:, :, 0]
        bc = sf("bc", [P, 2 * D])
        logit = sf("logit", [P, NT, E])
        l_max = sf("l_max", [P, NT])
        n_hi = sf("n_hi", [P, 1])
        z_lo = sf("z_lo", [P, 4, HG])
        good = sf("good", [P, 5])
        onesz = sf("onesz", [P, HG, P], BF16)
        headsel = sf("headsel", [P, HG], BF16)
        identb = sf("identb", [P, P], BF16)
        later_b = sf("later_b", [P, P], BF16)
        late256 = sf("late256", [P, P], BF16)
        upto = sf("upto", [P, P], BF16)
        tie = sf("tie", [P, P])
        partner = sf("partner", [P, P], BF16)
        part_r = nk1f
        t_less = sf("t_less", [P, P])
        z_thr = sf("z_thr", [P, 1])
        TINY = 1e-30
        UP = -(1.0 + 2.0 ** -7)

        f_const, f_ones = sem("f_const"), sem("f_ones")
        f_x, f_xr, f_xrfree = (sem(n) for n in ("f_x", "f_xr", "f_xrfree"))
        f_var, f_rstd, f_xhat, f_hT, f_yev, f_one, f_keep = (sem(n) for n in (
            "f_var", "f_rstd", "f_xhat", "f_hT", "f_yev", "f_one", "f_keep"))
        f_full = [sem(f"f_full{i}") for i in range(3)]
        f_free = [sem(f"f_free{i}") for i in range(3)]
        f_stage, f_kx, f_kp, f_kdma, f_qx, f_qp, f_qdma = (sem(n) for n in (
            "f_stage", "f_kx", "f_kp", "f_kdma", "f_qx", "f_qp", "f_qdma"))
        f_pool, f_pq, f_neg, f_gz, f_em, f_lw, f_nexp, f_pn = (sem(n) for n in (
            "f_pool", "f_pq", "f_neg", "f_gz", "f_em", "f_lw", "f_nexp", "f_pn"))
        f_zm, f_pz, f_p, f_pv, f_O, f_osb = (sem(n) for n in (
            "f_zm", "f_pz", "f_p", "f_pv", "f_O", "f_osb"))
        f_otok, f_oev, f_x2, f_woga, f_h2, f_hev, f_log, f_lm, f_lexp = (sem(n) for n in (
            "f_otok", "f_oev", "f_x2", "f_woga", "f_h2", "f_hev", "f_log", "f_lm", "f_lexp"))
        f_taken, f_good, f_goods, f_flag, f_cnt, f_qp1, f_hout = (sem(n) for n in (
            "f_taken", "f_good", "f_goods", "f_flag", "f_cnt", "f_qp1", "f_hout"))
        f_pr, f_out, f_var2, f_rstd2 = (sem(n) for n in ("f_pr", "f_out", "f_var2", "f_rstd2"))

        def units(c):
            return [(i, c) for i in range(4 * (c + 1))]

        def span(i, c):
            t0 = max(P * i, 512 * c)
            return t0, 512 * (c + 1) - t0

        def group_steps(g):
            n = g + 1
            own = ("stage", "K", "Kd", "Q", "G", "Qd", "D2", "M", "NS", "W")
            last_o = [("O", g - 1, 1)] if g else []
            late = [("D2", 0), ("NS", 0), ("W", 0)] if g == 0 else []
            body = ([("Z", g, 0)] + [("M", 0)] * (g == 0) + [("S", g, 0, 0)] + last_o + [("stage", n)] + late[:1] + [("S", g, 1, 0)] + late[1:] +
                    [("PZ", g, 0), ("Z", g, 1), ("K", n), ("S", g, 2, 0), ("Kd", n), ("S", g, 3, 0), ("PN", g),
                     ("PV", g, 3, 0), ("E", g, 0), ("S", g, 0, 1), ("O", g, 0), ("G", n), ("S", g, 1, 1), ("PZ", g, 1),
                     ("Q", n), ("S", g, 2, 1), ("Qd", n), ("S", g, 3, 1), ("D2", n), ("S", g, 4, 1), ("M", n), ("NS", n),
                     ("S", g, 5, 1), ("W", n), ("S", g, 6, 1), ("S", g, 7, 1), ("PV", g, 7, 1), ("E", g, 1)])
            return [s for s in body if n < NG or s[0] not in own or s[1] == g]

        uses = [("WO",), ("BC",)]
        for t in range(NT):
            if t == 0:
                uses.append(("T", 0))
            if t + 1 < NT:
                uses.append(("T", t + 1))
            uses.append(("Y", t))
        attn = [(k, 0) for k in ("stage", "K", "Q", "Kd", "Qd", "G")]
        attn += [s for g in range(NG) for s in group_steps(g)] + [("O", NG - 1, 1)]
        for s in attn:
            if s[0] in ("K", "Q", "G", "D2", "M", "NS", "W", "O"):
                uses.append(s)
            elif s[0] == "Z":
                uses += [s + (0,), s + (1,)]
            elif s[0] == "S":
                uses += [s + (0,), s + (1,)] if span(s[2], s[3])[1] > 256 else [s + (0,)]
        for t in range(NT):
            if t == 0:
                uses.append(("OT", 0))
            if t + 1 < NT:
                uses.append(("OT", t + 1))
            uses.append(("P", t))
        uses += [("HT", t) for t in range(NT)]
        place = {u: (i % 3, i // 3) for i, u in enumerate(uses)}
        per = [sum(i % 3 == q for i in range(len(uses))) for q in range(3)]

        def buf(u):
            return ps[:, 2 * place[u][0]:2 * place[u][0] + 2, :]

        def buf_of(u):
            return place[u][0]

        def nth(u, b):
            return per[place[u][0]] * b + place[u][1]

        with nc.Block() as blk:
            @blk.sync
            def _(sp):
                def load_x(b):
                    sp.wait_ge(f_out, 16 * b + 1)
                    sp.wait_ge(f_h2, NT * b + 1)
                    sp.dma_start(x_in[:, :, :], x_v[bass.ds(b, 1)].rearrange("o p n d -> (o p) n d")).then_inc(f_x, 16)

                def rest(b, last):
                    for s in attn:
                        if s[0] == "Kd":
                            n = s[1]
                            sp.wait_ge(f_kp, NG * b + n + 1)
                            if n:
                                sp.wait_ge(f_pv, 12 * (NG * b + n - 1) + 2)
                            for h in range(HG):
                                for dst, lo in ((A1, 0), (A2, 2)):
                                    sp.dma_start(dst[:, n % 2, h, :], parts[32 * h:32 * h + 32, lo:lo + 4, :]).then_inc(f_kdma, 16)
                        if s[0] == "Qd":
                            n = s[1]
                            sp.wait_ge(f_qp1, NG * b + n + 1)
                            for h in range(HG):
                                sp.dma_start(R1[:, n % 2, h, :], q_parts(n)[32 * h:32 * h + 32, 0:4, :]).then_inc(f_qdma, 16)
                            sp.wait_ge(f_qp, NG * b + n + 1)
                            for h in range(HG):
                                sp.dma_start(R2[:, n % 2, h, :], q_parts(n)[32 * h:32 * h + 32, 4:8, :]).then_inc(f_qdma, 16)
                    sp.wait_ge(f_xrfree, b + 1)
                    sp.dma_start(x_in[:, :, :], x_v[bass.ds(b, 1)].rearrange("o p n d -> (o p) n d")).then_inc(f_xr, 16)
                    sp.wait_ge(f_x2, b + 1)
                    sp.dma_start(out_v[bass.ds(b, 1)].rearrange("o p n d -> (o p) n d"), x_in[:, :, :]).then_inc(f_out, 16)
                    if not last:
                        load_x(b + 1)
                    sp.wait_ge(f_pr, b + 1)
                    sp.dma_start(h_v[bass.ds(b, 1)].rearrange("o p n d -> (o p) n d"), h2p[:, :, :]).then_inc(f_hout, 16)

                load_x(0)
                with sp.Fori(0, B - 1) as b:
                    rest(b, False)
                rest(B - 1, True)
                sp.wait_ge(f_out, 16 * B + 1)
                sp.wait_ge(f_hout, 16 * B + 1)

            @blk.gpsimd
            def _(pool):
                pool.memset(vz_r[:, :, :], 0.0)
                pool.memset(headsel[:, :], 0.0)
                pool.memset(later_b[:, :], 0.0)
                pool.memset(late256[:, :], 0.0)
                pool.memset(upto[:, :], 1.0)
                pool.memset(tie[:, :], 0.0)
                pool.memset(part_r[:, :], 0.0)
                pool.memset(half_neg[:, :], -0.5)
                pool.memset(y_hi[:, :], 0.0)
                pool.memset(y_lo[:, :], 1.0)
                pool.memset(y_most[:, :], 0.0)
                pool.memset(n_hi[:, :], 0.0)
                pool.memset(z_lo[:, :, :], 1.0)
                pool.iota(t_less[:, :], [[1, P]], base=1 - TOPK, channel_multiplier=0,
                          allow_small_or_imprecise_dtypes=True)
                pool.iota(z_thr[:, :], [[0, 1]], base=TOPK, channel_multiplier=-1,
                          allow_small_or_imprecise_dtypes=True)
                pool.tensor_copy(identb[:, :], ident[:, :])
                pool.drain()
                for h in range(HG):
                    pool.memset(headsel[32 * h:32 * h + 32, h:h + 1], 1.0)
                    pool.drain()
                pool.affine_select(later_b[:, :], later_b[:, :], [[1, P]], ALU.is_ge, -BIG, base=0, channel_multiplier=-1)
                pool.affine_select(late256[:, :], late256[:, :], [[1, P]], ALU.is_ge, 256.0, base=0, channel_multiplier=-1)
                pool.affine_select(upto[:, :], upto[:, :], [[1, P]], ALU.is_ge, 0.0, base=0, channel_multiplier=-1)
                pool.affine_select(tie[:, :], tie[:, :], [[1, P]], ALU.is_ge, TINY, base=0, channel_multiplier=-1)
                for h in range(HG):
                    lo = 32 * h
                    pool.affine_select(part_r[:, lo + HD:lo + 32], part_r[:, lo + HD:lo + 32], [[-1, HD]],
                                       ALU.not_equal, 1.0, base=-lo, channel_multiplier=1)
                    pool.affine_select(part_r[:, lo:lo + HD], part_r[:, lo:lo + HD], [[-1, HD]],
                                       ALU.not_equal, 1.0, base=-lo - HD, channel_multiplier=1)
                pool.drain()
                pool.tensor_tensor(partner[:, :], part_r[:, :], ident[:, :], ALU.add)
                pool.drain().then_inc(f_const, 1)
                with pool.Fori(0, B) as b:
                    pool.wait_ge(f_var, b + 1)
                    pool.tensor_tensor(rstd[:, :], var_e[:, :], half_neg[:, :], ALU.pow)
                    pool.drain().then_inc(f_rstd, 1)
                    for t in range(NT):
                        pool.wait_ge(f_one, NT * b + t + 1)
                        pool.tensor_tensor(qkv[:, t].rearrange("p j h d -> p (j h) d"), y_val[:, t % 2],
                                           y_one[:, t % 2], ALU.mult).then_inc(f_keep, 1)
                    for s in attn:
                        if s[0] == "Qd":
                            pool.wait_ge(f_pool, NG * b + s[1] + 1)
                            pool.tensor_tensor(qn[:, s[1] % 2, :], q1[:, s[1] % 2, :], cn[:, :], ALU.mult)
                            pool.drain().then_inc(f_pq, 1)
                    pool.wait_ge(f_var2, b + 1)
                    pool.tensor_tensor(rstd[:, :], var_e[:, :], half_neg[:, :], ALU.pow)
                    pool.drain().then_inc(f_rstd2, 1)

            @blk.scalar
            def _(act):
                with act.Fori(0, B) as b:
                    def count_kept(t):
                        act.wait_ge(f_one, NT * b + t + 1)
                        act.activation(y_drop, y_one[:, t % 2].rearrange("p j d -> p (j d)"), ACT.Copy,
                                       accum_out=y_cnt[:, t:t + 1])
                        act.drain().then_inc(f_cnt, 1)

                    for t in range(NT):
                        u = ("Y", t)
                        act.wait_ge(f_full[buf_of(u)], nth(u, b) + 1)
                        y = buf(u).rearrange("p a b -> p (a b)")[:, 0:3 * D]
                        if t >= 2:
                            act.wait_ge(f_one, NT * b + t - 1)
                            act.wait_ge(f_keep, NT * b + t - 1)
                        act.activation(y_abs[:, t % 2].rearrange("p h d -> p (h d)"), y, ACT.Abs)
                        act.activation(y_val[:, t % 2].rearrange("p h d -> p (h d)"), y, ACT.Copy)
                        act.drain().then_inc(f_free[buf_of(u)], 1)
                        act.nop().then_inc(f_yev, 1)
                        if t >= 1:
                            count_kept(t - 1)
                    count_kept(NT - 1)
                    for s in attn:
                        kind = s[0]
                        gi = NG * b + s[1]
                        if kind in ("K", "Q", "M", "NS"):
                            u = s
                            act.wait_ge(f_full[buf_of(u)], nth(u, b) + 1)
                        if kind == "K":
                            if s[1]:
                                act.wait_ge(f_qdma, 128 * gi)
                            flat = buf(u).rearrange("p a b -> p (a b)")
                            act.activation(kx[:, :], flat, ACT.Copy)
                            act.activation(parts[:, 2, :], flat, ACT.Copy)
                            act.drain().then_inc(f_free[buf_of(u)], 1)
                            act.nop().then_inc(f_kx, 1)
                        if kind == "Q":
                            if s[1]:
                                act.wait_ge(f_kdma, 128 * (gi + 1))
                            flat = buf(u).rearrange("p a b -> p (a b)")
                            act.activation(qx_of(s[1]), flat, ACT.Copy)
                            act.activation(q_parts(s[1])[:, 0, :], flat, ACT.Copy)
                            act.drain().then_inc(f_free[buf_of(u)], 1)
                            act.nop().then_inc(f_qx, 1)
                        if kind == "M":
                            act.activation(em[:, s[1] % 2, :, :].rearrange("p n h -> p (n h)"), buf(u)[:, 0, 0:NT * HG],
                                           ACT.Exp, scale=0.25)
                            act.drain().then_inc(f_free[buf_of(u)], 1)
                            act.nop().then_inc(f_em, 1)
                        if kind == "NS":
                            act.activation(pn[:, :, :].rearrange("p h t -> p (h t)"), buf(u)[:, 0, :], ACT.Exp,
                                           scale=0.25)
                            act.drain().then_inc(f_free[buf_of(u)], 1)
                            act.nop().then_inc(f_nexp, 1)
                        if kind == "S":
                            _, g, i, c = s
                            w = span(i, c)[1]
                            k = (12 * gi + (i if c == 0 else 4 + i))
                            act.wait_ge(f_pv, k + 1)
                            pb = p_buf[:, (i if c == 0 else 4 + i) % 2]
                            if w > 256:
                                for a in range(2):
                                    u = s + (a,)
                                    act.wait_ge(f_full[buf_of(u)], nth(u, b) + 1)
                                    act.activation(pb[:, 2 * a:2 * a + 2, 0:w], buf(u)[:, :, 0:w], ACT.Exp, scale=0.25)
                                    act.drain().then_inc(f_free[buf_of(u)], 1)
                            else:
                                u = s + (0,)
                                act.wait_ge(f_full[buf_of(u)], nth(u, b) + 1)
                                act.activation(pb[:, :, 0:w], buf(u).rearrange("p a (h t) -> p (a h) t", h=2)[:, :, 0:w],
                                               ACT.Exp, scale=0.25)
                                act.drain().then_inc(f_free[buf_of(u)], 1)
                            act.nop().then_inc(f_p, 1)
                        if kind == "E":
                            c = s[2]
                            if s[1] or c:
                                act.wait_ge(f_taken, 2 * gi + c)
                            act.wait_ge(f_O, 2 * gi + c + 1)
                            act.activation(o_sb[:, :, :], ps[:, 6:8, :], ACT.Copy)
                            act.drain().then_inc(f_osb, 1)
                    for t in range(NT):
                        u = ("OT", t)
                        act.wait_ge(f_full[buf_of(u)], nth(u, b) + 1)
                        act.activation(h_t[:, t % 2].rearrange("p k t -> p (k t)"), buf(u)[:, 0, 0:KD * P], ACT.Copy)
                        act.drain().then_inc(f_free[buf_of(u)], 1)
                        act.nop().then_inc(f_oev, 1)
                    for t in range(NT):
                        u = ("HT", t)
                        act.wait_ge(f_full[buf_of(u)], nth(u, b) + 1)
                        if t >= 2:
                            act.wait_ge(f_log, NT * b + t - 1)
                        act.activation(h_t[:, t % 2].rearrange("p k t -> p (k t)"), buf(u)[:, 0, 0:KD * P], ACT.Copy)
                        act.drain().then_inc(f_free[buf_of(u)], 1)
                        act.nop().then_inc(f_hev, 1)
                    act.wait_ge(f_lm, b + 1)
                    act.activation(logit[:, :, :], logit[:, :, :], ACT.Exp)
                    act.drain().then_inc(f_lexp, 1)

            @blk.tensor
            def _(pe):
                for q in range(3):
                    pe.drain().then_inc(f_free[q], 1)
                pe.drain().then_inc(f_pv, 2)
                pe.drain().then_inc(f_pz, 1)
                pe.wait_ge(f_const, 1)
                pe.wait_ge(f_ones, 1)
                with pe.Fori(0, B) as b:
                    def begin(u):
                        pe.wait_ge(f_free[buf_of(u)], nth(u, b) + 1)

                    u = ("WO",)
                    begin(u)
                    pe.wait_ge(f_woga, b + 1)
                    for k in range(KD):
                        for h in range(KD):
                            m = pe.transpose(buf(u)[:, 0, k * D + h * P:k * D + (h + 1) * P],
                                             wo_ga[:, h, k * P:(k + 1) * P], ident[:, :])
                    m.then_inc(f_full[buf_of(u)], 1)
                    u = ("BC",)
                    begin(u)
                    pe.matmul(buf(u)[:, 0, :], pick_b[:, :], mod_rows[:, 0:2 * D], start=True,
                              stop=True).then_inc(f_full[buf_of(u)], 1)

                    def turn(t):
                        u = ("T", t)
                        begin(u)
                        pe.wait_ge(f_xhat, NT * b + t + 1)
                        for k in range(KD):
                            m = pe.transpose(buf(u)[:, 0, k * P:(k + 1) * P], x_in[:, t, k * P:(k + 1) * P], ident[:, :])
                        m.then_inc(f_full[buf_of(u)], 1)

                    turn(0)
                    for t in range(NT):
                        if t + 1 < NT:
                            turn(t + 1)
                        u = ("Y", t)
                        begin(u)
                        pe.wait_ge(f_hT, NT * b + t + 1)
                        for bank, lo, n in ((0, 0, 2 * D), (1, 2 * D, D)):
                            for k in range(KD):
                                m = pe.matmul(buf(u)[:, bank, 0:n], h_t[:, t % 2, k, :], w_t[:, k, lo:lo + n],
                                              start=k == 0, stop=k == KD - 1)
                        m.then_inc(f_full[buf_of(u)], 1)

                    def pv(g, i, c):
                        gi = NG * b + g
                        k = i if c == 0 else 4 + i
                        pe.wait_ge(f_p, 12 * gi + k + 1)
                        t0, w = span(i, c)
                        o = t0 - 512 * c
                        if i == 0:
                            pe.wait_ge(f_osb, 2 * gi + c + 1)
                        for h in range(HG):
                            m = pe.matmul(ps[32 * h:32 * h + 32, 6, o:o + w], v_st[:, g % 2, i, h, :],
                                          p_buf[:, k % 2, h, 0:w], start=i == 0, stop=False, skip_group_check=True)
                        m.then_inc(f_pv, 1)

                    for s in attn:
                        kind = s[0]
                        n = s[1]
                        gi = NG * b + n
                        par = n % 2
                        if kind in ("K", "Q", "G", "D2", "M", "NS", "W", "O"):
                            u = s
                            if kind != "O":
                                begin(u)
                        if kind in ("K", "Q"):
                            pe.wait_ge(f_stage, gi + 1)
                            src = k_st if kind == "K" else q_st
                            for t in range(NT):
                                m = pe.transpose(buf(u)[:, t // 4, (t % 4) * P:(t % 4 + 1) * P],
                                                 src[:, t].rearrange("p h s d -> p (h s d)"), ident[:, :])
                            m.then_inc(f_full[buf_of(u)], 1)
                        if kind == "G":
                            pe.wait_ge(f_neg, gi + 1)
                            pe.matmul(buf(u)[:, 0, 0:P], partner[:, :], g_a[:, :], start=True, stop=True)
                            pe.transpose(buf(u)[:, 1, 0:P], kn_st[:, :, :, :].rearrange("p h s d -> p (h s d)"),
                                         ident[:, :]).then_inc(f_full[buf_of(u)], 1)
                        if kind == "D2":
                            pe.wait_ge(f_gz, gi + 1)
                            for h in range(HG):
                                o = buf(u)[:, 0, h * P:(h + 1) * P]
                                pe.matmul(o, k1zb[:, h, :], kb0[:, :], start=True, stop=False)
                                pe.matmul(o, k1zf[:, h, :], k128[:, :], start=False, stop=False)
                                m = pe.matmul(o, kxz[:, h, :], nk1f[:, :], start=False, stop=True)
                            m.then_inc(f_full[buf_of(u)], 1)
                        if kind == "M":
                            pe.wait_ge(f_qp, gi + 1)
                            for t in range(NT):
                                m = pe.matmul(buf(u)[:, 0, t * HG:(t + 1) * HG], q_parts(n)[:, 1, t * P:(t + 1) * P],
                                              headsel[:, :], start=True, stop=True)
                            m.then_inc(f_full[buf_of(u)], 1)
                        if kind == "NS":
                            for h in range(HG):
                                o = buf(u)[:, 0, h * P:(h + 1) * P]
                                pe.matmul(o, k0swz[:, h, :], q_first[:, 1, :], start=True, stop=False)
                                pe.matmul(o, identb[:, :], later_b[:, :], start=False, stop=False)
                                pe.matmul(o, onesz[:, h, :], q_first[:, 0, :], start=False, stop=False)
                                m = pe.matmul(o, knz[:, h, :], q128[:, :], start=False, stop=True)
                            m.then_inc(f_full[buf_of(u)], 1)
                        if kind == "W":
                            pe.wait_ge(f_lw, gi + 1)
                            for h in range(HG):
                                m = pe.matmul(buf(u)[:, 0, h * P:(h + 1) * P], lw[:, h, :], upto[:, :], start=True, stop=True)
                            m.then_inc(f_full[buf_of(u)], 1)
                        if kind == "Z":
                            c = s[2]
                            if c == 0:
                                pe.wait_ge(f_gz, gi + 1)
                                pe.wait_ge(f_pq, gi + 1)
                            for a in range(2):
                                u = s + (a,)
                                begin(u)
                                for h in (2 * a, 2 * a + 1):
                                    o = buf(u)[:, h % 2, :]
                                    pe.matmul(o, gz[:, par, h, :], q1[:, par, 512 * c:512 * c + 512], start=True, stop=False)
                                    m = pe.matmul(o, onesz[:, h, :], qn[:, par, 512 * c:512 * c + 512], start=False,
                                                  stop=c == 1)
                                    if c == 0:
                                        m = pe.matmul(o[:, 0:P], identb[:, :], late256[:, :], start=False, stop=True)
                                m.then_inc(f_full[buf_of(u)], 1)
                        if kind == "PZ":
                            c = s[2]
                            pe.wait_ge(f_zm, 2 * gi + c + 1)
                            pe.wait_ge(f_osb, 2 * gi + c + 1)
                            for q in range(3):
                                for h in range(HG):
                                    m = pe.matmul(ps[32 * h:32 * h + 32, 7, :], vz[:, par, q, h, :], zm[:, h, :],
                                                  start=q == 0, stop=q == 2, skip_group_check=True)
                            m.then_inc(f_pz, 1)
                        if kind == "PN":
                            pe.wait_ge(f_pn, gi + 1)
                            for h in range(HG):
                                m = pe.matmul(ps[32 * h:32 * h + 32, 6, 0:P], v_st[:, par, 0, h, :], pn[:, h, :],
                                              start=False, stop=False, skip_group_check=True)
                        if kind == "S":
                            _, g, i, c = s
                            t0, w = span(i, c)
                            if i == 0 and c == 0:
                                pe.wait_ge(f_kdma, 128 * (gi + 1))
                                pe.wait_ge(f_qdma, 128 * (gi + 1))
                            for a in range(2 if w > 256 else 1):
                                u = s + (a,)
                                begin(u)
                                for h in ((2 * a, 2 * a + 1) if w > 256 else range(HG)):
                                    o = buf(u)[:, h % 2, 0:w] if w > 256 else buf(u)[:, h // 2, 256 * (h % 2):256 * (h % 2) + w]
                                    ks, ts = slice(P * i, P * i + P), slice(t0, t0 + w)
                                    pe.matmul(o, A1[:, par, h, ks], R1[:, par, h, ts], start=True, stop=False)
                                    m = pe.matmul(o, A2[:, par, h, ks], R2[:, par, h, ts], start=False, stop=t0 != P * i)
                                    if t0 == P * i:
                                        m = pe.matmul(o[:, 0:P], identb[:, :], later_b[:, :], start=False, stop=True)
                                m.then_inc(f_full[buf_of(u)], 1)
                            if i:
                                pv(g, i - 1, c)
                        if kind == "PV":
                            _, g, i, c = s
                            pv(g, i, c)
                            pe.drain().then_inc(f_O, 1)
                        if kind == "O":
                            c = s[2]
                            begin(u)
                            pe.wait_ge(f_osb, 2 * gi + c + 2)
                            for q in range(4):
                                for a in range(2):
                                    m = pe.transpose(buf(u)[:, a, q * P:(q + 1) * P], o_sb[:, a, q * P:(q + 1) * P], ident[:, :])
                            m.then_inc(f_full[buf_of(u)], 1)
                            pe.drain().then_inc(f_taken, 1)

                    def turn_o(t):
                        u = ("OT", t)
                        begin(u)
                        if t == 0:
                            pe.wait_ge(f_otok, b + 1)
                        for k in range(KD):
                            m = pe.transpose(buf(u)[:, 0, k * P:(k + 1) * P],
                                             o_tok[:, t].rearrange("p h d -> p (h d)")[:, k * P:(k + 1) * P], ident[:, :])
                        m.then_inc(f_full[buf_of(u)], 1)

                    turn_o(0)
                    for t in range(NT):
                        if t + 1 < NT:
                            turn_o(t + 1)
                        u = ("P", t)
                        begin(u)
                        pe.wait_ge(f_oev, NT * b + t + 1)
                        for k in range(KD):
                            m = pe.matmul(buf(u)[:, 0, 0:D], h_t[:, t % 2, k, :], wo_t[:, k, :],
                                          start=k == 0, stop=k == KD - 1)
                        m.then_inc(f_full[buf_of(u)], 1)

                    def turn_h(t):
                        u = ("HT", t)
                        begin(u)
                        pe.wait_ge(f_h2, NT * b + t + 2)
                        for k in range(KD):
                            m = pe.transpose(buf(u)[:, 0, k * P:(k + 1) * P], h2p[:, t, k * P:(k + 1) * P], ident[:, :])
                        m.then_inc(f_full[buf_of(u)], 1)

                    turn_h(0)
                    for t in range(NT):
                        if t + 1 < NT:
                            turn_h(t + 1)
                        pe.wait_ge(f_hev, NT * b + t + 1)
                        lo = ps[:, 6, t * E:(t + 1) * E]
                        for k in range(KD):
                            pe.matmul(lo, h_t[:, t % 2, k, :], rw_sb[:, k, :], start=k == 0, stop=False)
                        pe.matmul(lo, ones_f[0:1, :], rb_sb[:, :], start=False, stop=True).then_inc(f_log, 1)
                pe.wait_ge(f_good, 1)
                pe.matmul(ps[0:1, 7, 0:5], ones_f[:, 0:1], good[:, :], start=True, stop=True).then_inc(f_goods, 1)

            @blk.vector
            def _(dve):
                dve.drain().then_inc(f_out, 1)
                dve.drain().then_inc(f_hout, 1)
                dve.drain().then_inc(f_h2, 1)
                dve.drain().then_inc(f_osb, 1)
                dve.memset(onesz[:, :, :], 0.0)
                dve.memset(gz[:, :, :, :], 0.0)
                dve.memset(kxz[:, :, :], 0.0)
                dve.memset(knz[:, :, :], 0.0)
                dve.memset(v_st[:, :, :, :, :], 0.0)
                dve.drain()
                dve.memset(v_st[:, :, :, :, HD:HD + 1], 1.0)
                for h in range(HG):
                    dve.memset(onesz[32 * h:32 * h + 32, h, :], 1.0)
                dve.drain().then_inc(f_ones, 1)
                with dve.Fori(0, B) as b:
                    def full(u):
                        dve.wait_ge(f_full[buf_of(u)], nth(u, b) + 1)

                    def release(u):
                        dve.drain().then_inc(f_free[buf_of(u)], 1)

                    dve.tensor_copy(mod_b[:, :, :], mod_t[:, :, :, bass.ds(b, 1)].rearrange("p j k o -> p j (k o)"))
                    dve.tensor_copy(pick_b[:, :], ident[0:B, bass.ds(b, 1)].to_broadcast([B, P]))
                    dve.drain()
                    for k in range(KD):
                        dve.tensor_scalar(wo_ga[:, k, :], wo_nat[:, k, :], mod_b[:, 2, k:k + 1], None, ALU.mult)
                    dve.drain().then_inc(f_woga, 1)
                    dve.wait_ge(f_x, 16 * (b + 1))
                    for t in range(NT):
                        dve.bn_stats(st[:, t, :], x_in[:, t, :])
                    dve.drain()
                    for t in range(NT):
                        dve.bn_aggr(mv[:, t, :], st[:, t, :])
                    dve.drain()
                    dve.tensor_scalar(var_e[:, :], mv[:, :, 1], EPS, None, ALU.add)
                    dve.drain().then_inc(f_var, 1)
                    full(("WO",))
                    dve.tensor_copy(wo_t[:, :, :], buf(("WO",))[:, 0, :].rearrange("p (k d) -> p k d", k=KD))
                    release(("WO",))
                    full(("BC",))
                    dve.tensor_copy(bc[:, :], buf(("BC",))[:, 0, :])
                    release(("BC",))
                    dve.wait_ge(f_rstd, b + 1)
                    for t in range(NT):
                        dve.tensor_scalar(x_in[:, t, :], x_in[:, t, :], mv[:, t, 0:1], rstd[:, t:t + 1],
                                          ALU.subtract, ALU.mult).then_inc(f_xhat, 1)

                    def modulate(t):
                        u = ("T", t)
                        full(u)
                        if t >= 2:
                            v = ("Y", t - 2)
                            dve.wait_ge(f_full[buf_of(v)], nth(v, b) + 1)
                        for k in range(KD):
                            dve.tensor_scalar(h_t[:, t % 2, k, :], buf(u)[:, 0, k * P:(k + 1) * P],
                                              mod_b[:, 1, k:k + 1], mod_b[:, 0, k:k + 1], ALU.mult, ALU.add)
                        release(u)
                        dve.nop().then_inc(f_hT, 1)

                    modulate(0)
                    dve.wait_ge(f_const, 1)
                    for t in range(-1, NT):
                        if t + 2 < NT:
                            modulate(t + 2)
                        if t < 0:
                            continue
                        dve.wait_ge(f_yev, NT * b + t + 1)
                        one = y_one[:, t % 2]
                        if t >= 2:
                            dve.wait_ge(f_keep, NT * b + t - 1)
                            dve.wait_ge(f_cnt, NT * b + t - 1)
                        dve.tensor_reduce(y_mx[:, t, :], y_abs[:, t % 2], AX.X, ALU.max)
                        dve.drain()
                        dve.tensor_tensor(one, y_abs[:, t % 2],
                                          y_mx[:, t, :].unsqueeze(2).to_broadcast([P, 3 * NH, HD]), ALU.is_equal)
                        dve.drain().then_inc(f_one, 1)
                    dve.tensor_reduce(y_ext[:, 0:1], y_mx[:, :, 0:2 * NH], AX.XY, ALU.max)
                    dve.tensor_reduce(y_ext[:, 1:2], y_mx[:, :, 0:2 * NH], AX.XY, ALU.min)
                    dve.drain()
                    dve.tensor_tensor(y_hi[:, :], y_hi[:, :], y_ext[:, 0:1], ALU.max)
                    dve.tensor_tensor(y_lo[:, :], y_lo[:, :], y_ext[:, 1:2], ALU.min)
                    dve.wait_ge(f_cnt, NT * (b + 1))
                    dve.tensor_reduce(y_ext[:, 2:3], y_cnt[:, :], AX.X, ALU.max)
                    dve.drain()
                    dve.tensor_tensor(y_most[:, :], y_most[:, :], y_ext[:, 2:3], ALU.max)

                    for s in attn:
                        kind = s[0]
                        n = s[1]
                        gi = NG * b + n
                        par = n % 2
                        hs = slice(HG * n, HG * n + HG)
                        if kind == "stage":
                            if n == 0:
                                dve.wait_ge(f_keep, NT * (b + 1))
                            else:
                                dve.wait_ge(f_pv, 12 * (gi - 1) + 2)
                            for sg, mul in ((0, 1.0), (1, -1.0)):
                                dve.tensor_scalar(k_st[:, :, :, sg, :], qkv[:, :, 1, hs, :], mul, 0.0, ALU.mult, ALU.max)
                                dve.tensor_scalar(q_st[:, :, :, sg, :], qkv[:, :, 0, hs, :], mul, 0.0, ALU.mult, ALU.max)
                                dve.tensor_scalar(kn_st[:, :, sg, :], qkv[:, 0, 1, hs, :], mul, 0.0, ALU.mult, ALU.min)
                            dve.drain().then_inc(f_stage, 1)
                            dve.tensor_copy(v_st[:, par, :, :, 0:HD], qkv[:, :, 2, hs, :])
                            dve.drain()
                            v0 = v_st[:, par, 0, :, :]
                            dve.tensor_copy(vz[:, par, 0], v0)
                            dve.drain()
                            dve.tensor_tensor(vz_r[:, :, :], v0, vz[:, par, 0], ALU.subtract)
                            dve.drain()
                            dve.tensor_copy(vz[:, par, 1], vz_r[:, :, :])
                            dve.drain()
                            dve.tensor_tensor(vz[:, par, 2], vz_r[:, :, :], vz[:, par, 1], ALU.subtract)
                        if kind == "Kd":
                            if n == 0:
                                dve.wait_ge(f_hout, 16 * b + 1)
                            dve.wait_ge(f_kx, gi + 1)
                            dve.tensor_scalar(parts[:, 1, :], kx[:, :], 0.0, None, ALU.is_gt)
                            dve.tensor_scalar(parts[:, 5, :], kx[:, :], 0.0, None, ALU.is_le)
                            dve.tensor_copy(parts[:, 4, :], parts[:, 2, :])
                            dve.drain()
                            dve.tensor_tensor_scan(mx[:, :], kx[:, :], kx[:, :], 0.0, ALU.max, ALU.max)
                            dve.tensor_copy(k128[:, :], kx[:, 0:P])
                            for h in range(HG):
                                r = slice(32 * h, 32 * h + 32)
                                dve.tensor_copy(kxz[r, h, :], kx[r, 0:P])
                            dve.drain()
                            dve.tensor_tensor(kx[:, :], kx[:, :], parts[:, 2, :], ALU.subtract)
                            dve.drain()
                            dve.tensor_copy(parts[:, 3, :], kx[:, :])
                            dve.drain()
                            dve.tensor_tensor(parts[:, 0, :], kx[:, :], parts[:, 3, :], ALU.subtract)
                            dve.drain().then_inc(f_kp, 1)
                            dve.tensor_tensor_scan(cn[:, :], parts[:, 1, :], parts[:, 1, :], 0.0, ALU.add, ALU.max)
                            dve.drain()
                            dve.tensor_scalar(k1zf[:, :, :], kxz[:, :, :], 0.0, None, ALU.is_gt)
                            dve.tensor_scalar(k1zb[:, :, :], kxz[:, :, :], 0.0, None, ALU.is_gt)
                            dve.tensor_scalar(nk1f[:, :], k128[:, :], 0.0, -1.0, ALU.is_gt, ALU.mult)
                            dve.tensor_scalar(kb0[:, :], k128[:, :], 0.0, BIG, ALU.is_le, ALU.mult)
                            dve.scalar_tensor_tensor(g_a[:, :], parts[:, 1, 0:P], 257.0, cn[:, 0:P], ALU.mult, ALU.subtract)
                            dve.tensor_tensor(n_hi[:, :], n_hi[:, :], cn[:, T - 1:T], ALU.max)
                            dve.drain().then_inc(f_neg, 1)
                        if kind == "G":
                            full(s)
                            for h in range(HG):
                                r = slice(32 * h, 32 * h + 32)
                                dve.tensor_copy(gz[r, par, h, :], buf(s)[r, 0, 0:P])
                                dve.tensor_copy(knz[r, h, :], buf(s)[r, 1, 0:P])
                            release(s)
                            dve.scalar_tensor_tensor(k0swz[:, :, :], knz[:, :, :], 0.0, onesz[:, :, :], ALU.is_ge, ALU.mult)
                            dve.drain().then_inc(f_gz, 1)
                        if kind == "Qd":
                            dve.wait_ge(f_qx, gi + 1)
                            qx, qp = qx_of(n), q_parts(n)
                            dve.tensor_scalar(q1[:, par, :], qx, 0.0, None, ALU.is_gt)
                            dve.drain().then_inc(f_pool, 1)
                            dve.scalar_tensor_tensor(qp[:, 1, :], qx, UP, mx[:, :], ALU.mult, ALU.mult)
                            dve.tensor_copy(qp[:, 2, :], qp[:, 0, :])
                            dve.tensor_copy(qp[:, 3, :], qp[:, 0, :])
                            dve.drain().then_inc(f_qp1, 1)
                            dve.tensor_scalar(qp[:, 7, :], qx, 0.0, -BIG, ALU.is_gt, ALU.mult)
                            dve.tensor_copy(q128[:, :], qx[:, 0:P])
                            dve.tensor_copy(q_first[:, 0, :], qp[:, 1, 0:P])
                            dve.drain()
                            dve.tensor_tensor(qx, qx, qp[:, 0, :], ALU.subtract)
                            dve.tensor_copy(q_first[:, 1, :], qp[:, 7, 0:P])
                            dve.drain()
                            dve.tensor_copy(qp[:, 4, :], qx)
                            dve.drain()
                            dve.tensor_copy(qp[:, 5, :], qp[:, 4, :])
                            dve.tensor_tensor(qp[:, 6, :], qx, qp[:, 4, :], ALU.subtract)
                            dve.drain().then_inc(f_qp, 1)
                        if kind == "D2":
                            full(s)
                            dve.tensor_tensor(lw[:, :, :], buf(s)[:, 0, :].rearrange("p (h t) -> p h t", h=HG),
                                              tie[:, :].unsqueeze(1).to_broadcast([P, HG, P]), ALU.is_lt)
                            release(s)
                            dve.nop().then_inc(f_lw, 1)
                        if kind == "W":
                            full(s)
                            dve.tensor_tensor(k1zf[:, :, :], buf(s)[:, 0, :].rearrange("p (h t) -> p h t", h=HG),
                                              t_less[:, :].unsqueeze(1).to_broadcast([P, HG, P]), ALU.is_ge)
                            release(s)
                            dve.wait_ge(f_nexp, gi + 1)
                            dve.tensor_tensor(pn[:, :, :], pn[:, :, :], k1zf[:, :, :], ALU.mult)
                            dve.drain().then_inc(f_pn, 1)
                        if kind == "Z":
                            c = s[2]
                            for a in range(2):
                                u = s + (a,)
                                full(u)
                                if a == 0:
                                    dve.wait_ge(f_pz, 2 * gi + c + 1)
                                dve.tensor_scalar(zm[:, 2 * a:2 * a + 2, :], buf(u), z_thr[:, :], None, ALU.is_lt)
                                release(u)
                            dve.nop().then_inc(f_zm, 1)
                            if n == NG - 1 and c == 1:
                                dve.drain().then_inc(f_xrfree, 1)
                        if kind == "O":
                            c = s[2]
                            full(s)
                            if c == 0:
                                dve.wait_ge(f_em, gi + 1)
                            o4 = buf(s)[:, 1, :].rearrange("p (q h d) -> p q h d", q=4, h=HG)[:, :, :, 0:HD + 1]
                            p4 = buf(s)[:, 0, :].rearrange("p (q h d) -> p q h d", q=4, h=HG)[:, :, :, 0:HD + 1]
                            dve.tensor_tensor(o_cmb[:, :, :, :], o4,
                                              em[:, par, 4 * c:4 * c + 4, :].unsqueeze(3).to_broadcast([P, 4, HG, HD + 1]),
                                              ALU.mult)
                            dve.drain()
                            dve.tensor_tensor(o_cmb[:, :, :, :], o_cmb[:, :, :, :], p4, ALU.add)
                            release(s)
                            dve.drain()
                            dve.tensor_tensor(z_lo[:, :, :], z_lo[:, :, :], o_cmb[:, :, :, HD], ALU.min)
                            dve.reciprocal(o_inv[:, :, :], o_cmb[:, :, :, HD])
                            dve.drain()
                            dve.tensor_tensor(o_tok[:, 4 * c:4 * c + 4, hs, :], o_cmb[:, :, :, 0:HD],
                                              o_inv[:, :, :].unsqueeze(3).to_broadcast([P, 4, HG, HD]), ALU.mult)
                            dve.drain()
                    dve.drain().then_inc(f_otok, 1)
                    dve.wait_ge(f_xr, 16 * (b + 1))
                    for t in range(NT):
                        u = ("P", t)
                        full(u)
                        dve.tensor_tensor(x_in[:, t, :], buf(u)[:, 0, 0:D], x_in[:, t, :], ALU.add)
                        release(u)
                        dve.bn_stats(st[:, t, :], x_in[:, t, :])
                    dve.drain().then_inc(f_x2, 1)
                    for t in range(NT):
                        dve.bn_aggr(mv[:, t, :], st[:, t, :])
                    dve.drain()
                    dve.tensor_scalar(var_e[:, :], mv[:, :, 1], EPS, None, ALU.add)
                    dve.drain().then_inc(f_var2, 1)
                    dve.wait_ge(f_rstd2, b + 1)
                    for t in range(NT):
                        h = h2p[:, t, 0:D]
                        dve.scalar_tensor_tensor(h, x_in[:, t, :], mv[:, t, 0:1], bc[:, D:2 * D], ALU.subtract, ALU.mult)
                        dve.drain()
                        dve.scalar_tensor_tensor(h, h, rstd[:, t:t + 1], bc[:, 0:D], ALU.mult, ALU.add)
                        dve.drain().then_inc(f_h2, 1)
                    dve.wait_ge(f_log, NT * (b + 1))
                    lg = ps[:, 6, 0:NT * E].rearrange("p (n e) -> p n e", e=E)
                    dve.tensor_reduce(l_max[:, :], lg, AX.X, ALU.max)
                    dve.drain()
                    dve.tensor_tensor(logit[:, :, :], lg, l_max[:, :].unsqueeze(2).to_broadcast([P, NT, E]), ALU.subtract)
                    dve.drain().then_inc(f_lm, 1)
                    dve.wait_ge(f_lexp, b + 1)
                    dve.tensor_reduce(l_max[:, :], logit[:, :, :], AX.X, ALU.add)
                    dve.drain()
                    dve.reciprocal(l_max[:, :], l_max[:, :])
                    dve.drain()
                    dve.tensor_tensor(h2p[:, :, D:ROW], logit[:, :, :], l_max[:, :].unsqueeze(2).to_broadcast([P, NT, E]),
                                      ALU.mult)
                    dve.drain()
                    dve.tensor_copy(probs[:, bass.ds(b * NT, NT), :], h2p[:, :, D:ROW])
                    dve.drain().then_inc(f_pr, 1)
                dve.tensor_reduce(y_ext[:, 0:1], z_lo[:, :, :], AX.XY, ALU.min)
                dve.drain()
                dve.tensor_scalar(good[:, 0:1], n_hi[:, :], float(TOPK), None, ALU.is_le)
                dve.tensor_scalar(good[:, 1:2], y_hi[:, :], 1e12, None, ALU.is_le)
                dve.tensor_scalar(good[:, 2:3], y_lo[:, :], 1e-12, None, ALU.is_ge)
                dve.tensor_scalar(good[:, 3:4], y_ext[:, 0:1], 1e-30, None, ALU.is_ge)
                dve.tensor_scalar(good[:, 4:5], y_most[:, :], 3.0 * NH, None, ALU.is_le)
                dve.drain().then_inc(f_good, 1)
                dve.wait_ge(f_goods, 1)
                dve.tensor_reduce(good[0:1, 0:1], ps[0:1, 7, 0:5], AX.X, ALU.add)
                dve.drain()
                dve.tensor_scalar(bad_f[:, :], good[0:1, 0:1], 5.0 * P, None, ALU.is_lt)
                dve.drain().then_inc(f_flag, 1)
        fst.close()

        gen = ExitStack()

        def sg(name, shape, dt=F32):
            return gen.enter_context(nc.sbuf_tensor("gen_" + name, shape, dt))

        x_in = sg("x_in", [P, NT, D])
        x_res = sg("x_res", [P, NT, D])
        st = sg("st", [P, NT, 6])
        mv = sg("mv", [P, NT, 2])
        var_e = sg("var_e", [P, NT])
        rstd = sg("rstd", [P, NT])
        h_t = sg("h_t", [P, 2, KD, P])
        y_abs = sg("y_abs", [P, 2, 3 * NH, HD])
        y_val = sg("y_val", [P, 2, 3 * NH, HD])
        y_max = sg("y_max", [P, 3 * NH])
        y_eq = sg("y_eq", [P, 3 * NH, HD], BF16)
        y_ord = sg("y_ord", [P, 3 * NH, HD], BF16)
        y_first = sg("y_first", [P, 3 * NH], BF16)
        y_one = sg("y_one", [P, 2, 3 * NH, HD], BF16)
        qkv = sg("qkv", [P, NT, 3, NH, HD])
        q_st = sg("q_st", [P, NT, HG, 2, HD])
        k_st = sg("k_st", [P, NT, HG, 2, HD])
        v_st = sg("v_st", [P, NT, HG, HD + 1])
        q_rows = sg("q_rows", [P, T])
        k_rows = sg("k_rows", [P, T])
        q_tile = sg("q_tile", [P, P])
        sc = sg("sc", [P, T])
        work = sg("work", [P, T])
        top8 = sg("top8", [P, TOPK])
        neg_m = sg("neg_m", [P, 1])
        prob = sg("prob", [P, T])
        prob_t = sg("prob_t", [P, NT, P])
        z_inv = sg("z_inv", [P, 1])
        o_tok = sg("o_tok", [P, NT, NH, HD])
        o_t = sg("o_t", [P, 2, KD, P])
        x2 = sg("x2", [P, NT, D])
        bc = sg("bc", [P, 2 * D])
        h2p = sg("h2p", [P, NT, ROW])
        logit = sg("logit", [P, NT, E])
        l_max = sg("l_max", [P, NT])
        wo_ga = sg("wo_ga", [P, KD, D])
        causal = sg("causal", [P, 15 * P])
        s_causal = sem("s_causal")
        s_x, s_xr = sem("s_x"), sem("s_xr")
        s_x_free, s_xr_free = sem("s_x_free"), sem("s_xr_free")
        s_var, s_rstd = sem("s_var"), sem("s_rstd")
        s_xhat, s_xT, s_hT, s_qkv = sem("s_xhat"), sem("s_xT"), sem("s_hT"), sem("s_qkv")
        s_yev, s_one, s_keep = sem("s_yev"), sem("s_one"), sem("s_keep")
        s_stage, s_rT, s_rows, s_qt = sem("s_stage"), sem("s_rT"), sem("s_rows"), sem("s_qt")
        s_S, s_m, s_p, s_pk, s_pT, s_pts, s_O = (sem(n) for n in
                                                ("s_S", "s_m", "s_p", "s_pk", "s_pT", "s_pts", "s_O"))
        s_otok, s_oT, s_oev, s_Y, s_x2 = (sem(n) for n in ("s_otok", "s_oT", "s_oev", "s_Y", "s_x2"))
        s_woga, s_woT, s_bc = (sem(n) for n in ("s_woga", "s_woT", "s_bc"))
        s_h2, s_h2T, s_h2ev, s_log, s_lm, s_lexp = (sem(n) for n in
                                                    ("s_h2", "s_h2T", "s_h2ev", "s_log", "s_lm", "s_lexp"))
        s_pr, s_out, s_var2, s_rstd2 = (sem(n) for n in ("s_pr", "s_out", "s_var2", "s_rstd2"))

        with nc.Block() as blk:
            @blk.sync
            def _(sp):
                general = sp.value_load(bad_f[0:1, 0:1])
                with sp.If(general == 1):
                    with sp.Fori(0, B) as b:
                        sp.wait_ge(s_x_free, b + 1)
                        sp.dma_start(x_in[:, :, :], x_v[bass.ds(b, 1)].rearrange("o p n d -> (o p) n d")).then_inc(s_x, 16)
                        sp.wait_ge(s_xr_free, NT * b + 1)
                        sp.dma_start(x_res[:, :, :], x_v[bass.ds(b, 1)].rearrange("o p n d -> (o p) n d")).then_inc(s_xr, 16)
                        sp.wait_ge(s_x2, b + 1)
                        sp.dma_start(out_v[bass.ds(b, 1)].rearrange("o p n d -> (o p) n d"), x2[:, :, :]).then_inc(s_out, 16)
                        sp.wait_ge(s_pr, b + 1)
                        sp.dma_start(h_v[bass.ds(b, 1)].rearrange("o p n d -> (o p) n d"), h2p[:, :, :]).then_inc(s_out, 16)
                    sp.wait_ge(s_out, 32 * B)
                sp.nop()

            @blk.gpsimd
            def _(pool):
                general = pool.value_load(bad_f[0:1, 0:1])
                with pool.If(general == 1):
                    pool.memset(causal[:, :], 0.0)
                    pool.memset(v_st[:, :, :, :], 1.0)
                    pool.drain()
                    pool.affine_select(causal[:, :], causal[:, :], [[-1, 15 * P]], ALU.is_ge, -BIG, base=7 * P,
                                       channel_multiplier=1)
                    pool.drain().then_inc(s_causal, 1)
                    with pool.Fori(0, B) as b:
                        pool.wait_ge(s_var, b + 1)
                        pool.tensor_tensor(rstd[:, :], var_e[:, :], half_neg[:, :], ALU.pow)
                        pool.drain().then_inc(s_rstd, 1)
                        for t in range(NT):
                            pool.wait_ge(s_one, NT * b + t + 1)
                            if t == 0:
                                pool.wait_ge(s_otok, b + 1)
                            pool.tensor_tensor(qkv[:, t].rearrange("p j h d -> p (j h) d"), y_val[:, t % 2],
                                               y_one[:, t % 2], ALU.mult).then_inc(s_keep, 1)
                        pool.wait_ge(s_var2, b + 1)
                        pool.tensor_tensor(rstd[:, :], var_e[:, :], half_neg[:, :], ALU.pow)
                        pool.drain().then_inc(s_rstd2, 1)
                pool.nop()

            @blk.scalar
            def _(act):
                general = act.value_load(bad_f[0:1, 0:1])
                with act.If(general == 1):
                    with act.Fori(0, B) as b:
                        for t in range(NT):
                            act.wait_ge(s_qkv, NT * b + t + 1)
                            y = ps[:, 2 + 2 * (t % 2):4 + 2 * (t % 2), :].rearrange("p a b -> p (a b)")[:, 0:3 * D]
                            if t >= 2:
                                act.wait_ge(s_keep, NT * b + t - 1)
                            act.activation(y_abs[:, t % 2].rearrange("p h d -> p (h d)"), y, ACT.Abs)
                            act.activation(y_val[:, t % 2].rearrange("p h d -> p (h d)"), y, ACT.Copy).then_inc(s_yev, 1)
                        with act.Fori(0, NG) as g:
                            gi = b * NG + g
                            act.wait_ge(s_rT, gi + 1)
                            act.activation(q_rows[:, :], ps[:, 0:2, :].rearrange("p a b -> p (a b)"), ACT.Copy)
                            act.activation(k_rows[:, :], ps[:, 2:4, :].rearrange("p a b -> p (a b)"),
                                           ACT.Copy).then_inc(s_rows, 1)
                            with act.Fori(0, NT) as i:
                                for j in range(HG):
                                    u = (gi * NT + i) * HG + j
                                    act.wait_ge(s_m, u + 1)
                                    act.activation(prob[:, :], sc[:, :], ACT.Exp, scale=0.25,
                                                   bias=neg_m[:, :]).then_inc(s_p, 1)
                                    act.wait_ge(s_pT, u + 1)
                                    act.activation(prob_t[:, :, :].rearrange("p a b -> p (a b)"),
                                                   ps[:, 6:8, :].rearrange("p a b -> p (a b)"), ACT.Copy).then_inc(s_pts, 1)
                        for t in range(NT):
                            act.wait_ge(s_oT, NT * b + t + 1)
                            act.activation(o_t[:, t % 2].rearrange("p k t -> p (k t)"), ps[:, t % 2, 0:KD * P],
                                           ACT.Copy).then_inc(s_oev, 1)
                        for t in range(NT):
                            act.wait_ge(s_h2T, NT * b + t + 1)
                            act.activation(h_t[:, t % 2].rearrange("p k t -> p (k t)"), ps[:, 4 + t % 2, 0:KD * P],
                                           ACT.Copy).then_inc(s_h2ev, 1)
                        act.wait_ge(s_lm, b + 1)
                        act.activation(logit[:, :, :], logit[:, :, :], ACT.Exp).then_inc(s_lexp, 1)
                act.nop()

            @blk.tensor
            def _(pe):
                general = pe.value_load(bad_f[0:1, 0:1])
                with pe.If(general == 1):
                    with pe.Fori(0, B) as b:
                        pe.wait_ge(s_woga, b + 1)
                        for k in range(KD):
                            for h in range(KD):
                                m = pe.transpose(ps[:, 6, k * D + h * P:k * D + (h + 1) * P],
                                                 wo_ga[:, h, k * P:(k + 1) * P], ident[:, :])
                        m.then_inc(s_woT, 1)
                        pe.matmul(ps[:, 7, :], pick_b[:, :], mod_rows[:, 0:2 * D], start=True, stop=True).then_inc(s_bc, 1)

                        def turn(t):
                            pe.wait_ge(s_xhat, NT * b + t + 1)
                            for k in range(KD):
                                m = pe.transpose(ps[:, t % 2, k * P:(k + 1) * P], x_in[:, t, k * P:(k + 1) * P], ident[:, :])
                            m.then_inc(s_xT, 1)

                        turn(0)
                        for t in range(NT):
                            if t + 1 < NT:
                                turn(t + 1)
                            pe.wait_ge(s_hT, NT * b + t + 1)
                            if t >= 2:
                                pe.wait_ge(s_yev, NT * b + t - 1)
                            for bank, lo, n in ((0, 0, 2 * D), (1, 2 * D, D)):
                                for k in range(KD):
                                    m = pe.matmul(ps[:, 2 + 2 * (t % 2) + bank, 0:n], h_t[:, t % 2, k, :],
                                                  w_t[:, k, lo:lo + n], start=k == 0, stop=k == KD - 1)
                            m.then_inc(s_qkv, 1)
                        with pe.Fori(0, NG) as g:
                            gi = b * NG + g
                            pe.wait_ge(s_stage, gi + 1)
                            for bank, src in ((0, q_st), (2, k_st)):
                                for t in range(NT):
                                    m = pe.transpose(ps[:, bank + t // 4, (t % 4) * P:(t % 4 + 1) * P],
                                                     src[:, t].rearrange("p h s d -> p (h s d)"), ident[:, :])
                            m.then_inc(s_rT, 1)
                            with pe.Fori(0, NT) as i:
                                pe.wait_ge(s_qt, gi * NT + i + 1)
                                for j in range(HG):
                                    u = (gi * NT + i) * HG + j
                                    r = slice(32 * j, 32 * j + 32)
                                    for half in range(2):
                                        m = pe.matmul(ps[:, 4 + half, :], q_tile[r, :], k_rows[r, 512 * half:512 * half + 512],
                                                      start=True, stop=True)
                                    m.then_inc(s_S, 1)
                                    pe.wait_ge(s_pk, u + 1)
                                    for t in range(NT):
                                        m = pe.transpose(ps[:, 6 + t // 4, (t % 4) * P:(t % 4 + 1) * P],
                                                         prob[:, t * P:(t + 1) * P], ident[:, :])
                                    m.then_inc(s_pT, 1)
                                    pe.wait_ge(s_pts, u + 1)
                                    for t in range(NT):
                                        m = pe.matmul(ps[:, 0, 0:HD + 1], prob_t[:, t, :], v_st[:, t, j, :],
                                                      start=t == 0, stop=t == NT - 1)
                                    m.then_inc(s_O, 1)

                        def turn_o(t):
                            if t == 0:
                                pe.wait_ge(s_otok, b + 2)
                            if t >= 2:
                                pe.wait_ge(s_oev, NT * b + t - 1)
                            for k in range(KD):
                                m = pe.transpose(ps[:, t % 2, k * P:(k + 1) * P],
                                                 o_tok[:, t].rearrange("p h d -> p (h d)")[:, k * P:(k + 1) * P], ident[:, :])
                            m.then_inc(s_oT, 1)

                        turn_o(0)
                        for t in range(NT):
                            if t + 1 < NT:
                                turn_o(t + 1)
                            pe.wait_ge(s_oev, NT * b + t + 1)
                            if t >= 2:
                                pe.wait_ge(s_xr_free, NT * b + t)
                            for k in range(KD):
                                m = pe.matmul(ps[:, 2 + t % 2, 0:D], o_t[:, t % 2, k, :], wo_t[:, k, :],
                                              start=k == 0, stop=k == KD - 1)
                            m.then_inc(s_Y, 1)

                        def turn_h(t):
                            pe.wait_ge(s_h2, NT * b + t + 1)
                            if t >= 2:
                                pe.wait_ge(s_h2ev, NT * b + t - 1)
                            for k in range(KD):
                                m = pe.transpose(ps[:, 4 + t % 2, k * P:(k + 1) * P], h2p[:, t, k * P:(k + 1) * P], ident[:, :])
                            m.then_inc(s_h2T, 1)

                        turn_h(0)
                        for t in range(NT):
                            if t + 1 < NT:
                                turn_h(t + 1)
                            pe.wait_ge(s_h2ev, NT * b + t + 1)
                            lo = ps[:, 6, t * E:(t + 1) * E]
                            for k in range(KD):
                                pe.matmul(lo, h_t[:, t % 2, k, :], rw_sb[:, k, :], start=k == 0, stop=False)
                            m = pe.matmul(lo, ones_f[0:1, :], rb_sb[:, :], start=False, stop=True)
                        m.then_inc(s_log, 1)
                pe.nop()

            @blk.vector
            def _(dve):
                general = dve.value_load(bad_f[0:1, 0:1])
                with dve.If(general == 1):
                    dve.wait_ge(s_causal, 1)
                    dve.sem_inc(s_x_free, 1)
                    dve.sem_inc(s_xr_free, 1)
                    dve.sem_inc(s_otok, 1)
                    with dve.Fori(0, B) as b:
                        dve.tensor_copy(mod_b[:, :, :], mod_t[:, :, :, bass.ds(b, 1)].rearrange("p j k o -> p j (k o)"))
                        dve.tensor_copy(pick_b[:, :], ident[0:B, bass.ds(b, 1)].to_broadcast([B, P]))
                        dve.drain()
                        for k in range(KD):
                            dve.tensor_scalar(wo_ga[:, k, :], wo_nat[:, k, :], mod_b[:, 2, k:k + 1], None, ALU.mult)
                        dve.drain().then_inc(s_woga, 1)
                        dve.wait_ge(s_x, 16 * (b + 1))
                        for t in range(NT):
                            dve.bn_stats(st[:, t, :], x_in[:, t, :])
                        dve.drain()
                        for t in range(NT):
                            dve.bn_aggr(mv[:, t, :], st[:, t, :])
                        dve.drain()
                        dve.tensor_scalar(var_e[:, :], mv[:, :, 1], EPS, None, ALU.add)
                        dve.drain().then_inc(s_var, 1)
                        dve.wait_ge(s_woT, b + 1)
                        dve.tensor_copy(wo_t[:, :, :], ps[:, 6, :].rearrange("p (k d) -> p k d", k=KD))
                        dve.wait_ge(s_bc, b + 1)
                        dve.tensor_copy(bc[:, :], ps[:, 7, :])
                        dve.wait_ge(s_rstd, b + 1)
                        for t in range(NT):
                            dve.tensor_scalar(x_in[:, t, :], x_in[:, t, :], mv[:, t, 0:1], rstd[:, t:t + 1],
                                              ALU.subtract, ALU.mult).then_inc(s_xhat, 1)
                        for t in range(NT):
                            dve.wait_ge(s_xT, NT * b + t + 1)
                            if t >= 2:
                                dve.wait_ge(s_qkv, NT * b + t - 1)
                            for k in range(KD):
                                m = dve.tensor_scalar(h_t[:, t % 2, k, :], ps[:, t % 2, k * P:(k + 1) * P],
                                                      mod_b[:, 1, k:k + 1], mod_b[:, 0, k:k + 1], ALU.mult, ALU.add)
                            m.then_inc(s_hT, 1)
                            dve.wait_ge(s_yev, NT * b + t + 1)
                            a = y_abs[:, t % 2]
                            dve.tensor_reduce(y_max[:, :], a, AX.X, ALU.max)
                            dve.drain()
                            dve.tensor_tensor(y_eq[:, :, :], a, y_max[:, :].unsqueeze(2).to_broadcast([P, 3 * NH, HD]),
                                              ALU.is_equal)
                            dve.drain()
                            dve.tensor_tensor(y_ord[:, :, :], y_eq[:, :, :], first_of[:, :].unsqueeze(1).to_broadcast([P, 3 * NH, HD]), ALU.mult)
                            dve.drain()
                            dve.tensor_reduce(y_first[:, :], y_ord[:, :, :], AX.X, ALU.max)
                            dve.drain()
                            dve.tensor_tensor(y_one[:, t % 2], y_ord[:, :, :],
                                              y_first[:, :].unsqueeze(2).to_broadcast([P, 3 * NH, HD]),
                                              ALU.is_equal)
                            dve.drain().then_inc(s_one, 1)
                        dve.drain().then_inc(s_x_free, 1)
                        dve.wait_ge(s_keep, NT * (b + 1))
                        dve.memset(stand[:, :], 0.0)
                        with dve.Fori(0, NG) as g:
                            gi = b * NG + g
                            hs = bass.ds(g * HG, HG)
                            dve.tensor_copy(q_st[:, :, :, 0, :], qkv[:, :, 0, hs, :])
                            dve.tensor_scalar(q_st[:, :, :, 1, :], qkv[:, :, 0, hs, :], -1.0, None, ALU.mult)
                            dve.tensor_scalar(k_st[:, :, :, 0, :], qkv[:, :, 1, hs, :], 0.0, None, ALU.max)
                            dve.tensor_scalar(k_st[:, :, :, 1, :], qkv[:, :, 1, hs, :], -1.0, 0.0, ALU.mult, ALU.max)
                            dve.tensor_copy(v_st[:, :, :, 0:HD], qkv[:, :, 2, hs, :])
                            dve.drain().then_inc(s_stage, 1)
                            with dve.Fori(0, NT) as i:
                                dve.wait_ge(s_rows, gi + 1)
                                dve.tensor_copy(q_tile[:, :], q_rows[:, bass.ds(i * P, P)])
                                dve.drain().then_inc(s_qt, 1)
                                for j in range(HG):
                                    u = (gi * NT + i) * HG + j
                                    dve.wait_ge(s_S, u + 1)
                                    dve.memset(stand[:, :], 0.0)
                                    dve.tensor_tensor(sc[:, :], ps[:, 4:6, :].rearrange("p a b -> p (a b)"),
                                                      causal[:, bass.ds((7 - i) * P, T)], ALU.add)
                                    dve.drain()
                                    for r in range(TOPK // 8):
                                        src = sc if r == 0 else work
                                        dve.max(top8[:, 8 * r:8 * r + 8], src[:, :])
                                        dve.drain()
                                        if r == 0:
                                            dve.tensor_scalar(neg_m[:, :], top8[:, 0:1], -0.25, None, ALU.mult)
                                            dve.drain().then_inc(s_m, 1)
                                        dve.match_replace(work[:, :], top8[:, 8 * r:8 * r + 8], src[:, :], TAKEN)
                                        dve.drain()
                                    dve.wait_ge(s_p, u + 1)
                                    dve.scalar_tensor_tensor(prob[:, :], work[:, :], TAKEN, prob[:, :], ALU.is_equal,
                                                             ALU.mult)
                                    dve.drain().then_inc(s_pk, 1)
                                    dve.wait_ge(s_O, u + 1)
                                    dve.reciprocal(z_inv[:, :], ps[:, 0, HD:HD + 1])
                                    dve.drain()
                                    dve.tensor_scalar(o_tok[:, bass.ds(i, 1), bass.ds(g * HG + j, 1), :].rearrange(
                                        "p a b d -> p (a b d)"), ps[:, 0, 0:HD], z_inv[:, :], None, ALU.mult)
                        dve.drain().then_inc(s_otok, 1)
                        dve.wait_ge(s_xr, 16 * (b + 1))
                        for t in range(NT):
                            dve.wait_ge(s_Y, NT * b + t + 1)
                            dve.tensor_tensor(x2[:, t, :], ps[:, 2 + t % 2, 0:D], x_res[:, t, :],
                                              ALU.add).then_inc(s_xr_free, 1)
                        dve.drain().then_inc(s_x2, 1)
                        for t in range(NT):
                            dve.bn_stats(st[:, t, :], x2[:, t, :])
                        dve.drain()
                        for t in range(NT):
                            dve.bn_aggr(mv[:, t, :], st[:, t, :])
                        dve.drain()
                        dve.tensor_scalar(var_e[:, :], mv[:, :, 1], EPS, None, ALU.add)
                        dve.drain().then_inc(s_var2, 1)
                        dve.wait_ge(s_rstd2, b + 1)
                        for t in range(NT):
                            h = h2p[:, t, 0:D]
                            dve.tensor_scalar(h, x2[:, t, :], mv[:, t, 0:1], rstd[:, t:t + 1], ALU.subtract, ALU.mult)
                            dve.drain()
                            dve.tensor_tensor(h, h, bc[:, D:2 * D], ALU.mult)
                            dve.drain()
                            dve.tensor_tensor(h, h, bc[:, 0:D], ALU.add)
                            dve.drain().then_inc(s_h2, 1)
                        dve.wait_ge(s_log, b + 1)
                        lg = ps[:, 6, 0:NT * E].rearrange("p (n e) -> p n e", e=E)
                        dve.tensor_reduce(l_max[:, :], lg, AX.X, ALU.max)
                        dve.drain()
                        dve.tensor_tensor(logit[:, :, :], lg, l_max[:, :].unsqueeze(2).to_broadcast([P, NT, E]), ALU.subtract)
                        dve.drain().then_inc(s_lm, 1)
                        dve.wait_ge(s_lexp, b + 1)
                        dve.tensor_reduce(l_max[:, :], logit[:, :, :], AX.X, ALU.add)
                        dve.drain()
                        dve.reciprocal(l_max[:, :], l_max[:, :])
                        dve.drain()
                        dve.tensor_tensor(h2p[:, :, D:ROW], logit[:, :, :], l_max[:, :].unsqueeze(2).to_broadcast([P, NT, E]),
                                          ALU.mult)
                        dve.drain()
                        dve.tensor_copy(probs[:, bass.ds(b * NT, NT), :], h2p[:, :, D:ROW])
                        dve.drain().then_inc(s_pr, 1)
                        dve.wait_ge(s_out, 32 * (b + 1))
                dve.nop()
        gen.close()

        att.close()
        b2_sb = sb("b2_sb", [P, E, D])
        gb_sb = sb("gb_sb", [P, B, D])
        w1_sb = sb("w1_sb", [P, 2, KD, DFF])
        w2_sb = sb("w2_sb", [P, 2, FO, D])
        sel = ExitStack()

        def sbs(name, shape, dt=F32):
            return sel.enter_context(nc.sbuf_tensor(name, shape, dt))

        bat_u = sbs("bat_u", [P, E, CC], U32)
        bat = sbs("bat", [P, E, CC])
        gate_q = sbs("gate_q", [P, 2, P])
        junk = sbs("junk", [P, 3, 2 * P], BF16)
        reach = sbs("reach", [P, 3])
        reached = sbs("reached", [P, 1])
        zeros = sbs("zeros", [P, P])
        thr = sbs("thr", [P, 1], U32)
        cand = sbs("cand", [P, 3], U32)
        step_u = sbs("step_u", [P, 1], U32)
        cnt = sbs("cnt", [P, 3])
        cnt2 = sbs("cnt2", [P, 2])
        need = sbs("need", [P, 1])
        start2 = sbs("start2", [P, 2])
        above = sbs("above", [P, 2, P])
        equal = sbs("equal", [P, 2, P])
        rank = sbs("rank", [P, 2, P])
        slot = sbs("slot", [P, NTALL, E])
        slot_i = sbs("slot_i", [P, 2, NTALL, E], I32)
        slot_f = sbs("slot_f", [P, 2, NTALL, E], BF16)
        oh_lo = sbs("oh_lo", [P, NTALL, E, 32], BF16)
        oh_hi = sbs("oh_hi", [P, NTALL, E, 2, 16], BF16)
        ids_f = sbs("ids_f", [32, E, 2, 16])
        b1_nat = sbs("b1_nat", [E * FO, P])
        s_gT, s_gq, s_cnt, s_tot = sem("s_gT"), sem("s_gq"), sem("s_cnt"), sem("s_tot")
        s_c2, s_off, s_sel, s_slT, s_oh, s_ids, s_idx = (sem(n) for n in
                                                        ("s_c2", "s_off", "s_sel", "s_slT", "s_oh", "s_ids", "s_idx"))
        s_b1in = sem("s_b1in")
        s_b, s_b1T, s_b1 = sem("s_b"), sem("s_b1T"), sem("s_b1")

        with nc.Block() as blk:
            @blk.sync
            def _(sp):
                sp.dma_start(b1_nat[:, :], b1.rearrange("e (o p) -> (e o) p", p=P)).then_inc(s_b1in, 16)
                sp.dma_start(b2_sb[:, :, :].rearrange("p e d -> p (e d)"),
                             b2.rearrange("(o e) d -> o (e d)", o=1).to_broadcast([P, E * D])).then_inc(s_b, 16)
                sp.dma_start(gb_sb[:, :, :].rearrange("p b d -> p (b d)"),
                             gb_table.rearrange("(o b) d -> o (b d)", o=1).to_broadcast([P, B * D])).then_inc(s_b, 16)
                for e in range(2):
                    sp.dma_start(w1_sb[:, e], w1[e].rearrange("(k p) f -> p k f", p=P)).then_inc(s_b, 16)
                    sp.dma_start(w2_sb[:, e], w2[e].rearrange("(k p) f -> p k f", p=P)).then_inc(s_b, 16)
                sp.wait_ge(s_b, 16 * 6)

            @blk.scalar
            def _(act):
                act.wait_ge(s_gT, 1)
                act.activation(gate_q[:, :, :], ps[:, 0, 0:2 * P].rearrange("p (a b) -> p a b", a=2),
                               ACT.Copy).then_inc(s_gq, 1)
                act.wait_ge(s_b1T, 1)
                act.activation(b1_t[:, :], ps[:, 1, 0:E * FO], ACT.Copy).then_inc(s_b1, 1)

            @blk.tensor
            def _(pe):
                flat = probs[:, :, :].rearrange("p n e -> p (n e)")
                for a in range(2):
                    m = pe.transpose(ps[:, 0, a * P:(a + 1) * P], flat[:, a * P:(a + 1) * P], ident[:, :])
                m.then_inc(s_gT, 1)
                pe.wait_ge(s_b1in, 16)
                pe.transpose(ps[:, 1, 0:E * FO], b1_nat[:, :], ident[0:E * FO, 0:E * FO]).then_inc(s_b1T, 1)
                with pe.Fori(0, 5) as k3:
                    for j in range(3):
                        pe.wait_ge(s_cnt, 3 * k3 + j + 1)
                        pe.matmul(ps[:, 2, 0:3], same_e[:, :], cnt[:, :], start=True, stop=True).then_inc(s_tot, 1)
                for r in range(2):
                    pe.wait_ge(s_c2, r + 1)
                    pe.matmul(ps[:, 3, 0:1], same_e[:, :], cnt[:, 0:1], start=True, stop=True)
                    pe.matmul(ps[:, 3, 1:3], before_e[:, :], cnt2[:, :], start=True, stop=True)
                    pe.matmul(ps[:, 3, 3:4], same_e[:, :], cnt2[:, 0:1], start=True, stop=True).then_inc(s_off, 1)
                pe.wait_ge(s_sel, 1)
                for a in range(2):
                    m = pe.transpose(ps[:, 4, a * P:(a + 1) * P], rank[:, a, :], ident[:, :])
                m.then_inc(s_slT, 1)
                for e in range(E):
                    pe.wait_ge(s_oh, e + 1)
                    for n in range(NTALL):
                        m = pe.matmul(ps[0:32, 5, e * 32:(e + 1) * 32], oh_lo[:, n, e, :],
                                      oh_hi[:, n, e].rearrange("p a h -> p (a h)"), start=n == 0, stop=n == NTALL - 1)
                m.then_inc(s_ids, 1)

            @blk.vector
            def _(dve):
                dve.memset(thr[:, :], 0)
                dve.memset(zeros[:, :], 0.0)
                dve.wait_ge(s_gq, 1)
                gates = gate_q[:, :, :].rearrange("p a b -> p (a b)")
                dve.drain()
                with dve.Fori(0, 5) as k3:
                    for j in range(3):
                        k = 3 * k3 + j
                        dve.tensor_tensor(cand[:, :], thr[:, :].to_broadcast([P, 3]),
                                          bit_u[:, bass.ds(k, 1), :].rearrange("p o m -> p (o m)"), ALU.bitwise_or)
                        dve.drain()
                        for m in range(3):
                            dve.tensor_scalar(junk[:, m, :], gates, cand[:, m:m + 1].bitcast(F32), None, ALU.is_ge,
                                              ALU.add, accum_out=cnt[:, m:m + 1])
                        dve.drain().then_inc(s_cnt, 1)
                        dve.wait_ge(s_tot, k + 1)
                        dve.tensor_scalar(reach[:, :], ps[:, 2, 0:3], float(CAP), None, ALU.is_ge, ALU.add,
                                          accum_out=reached[:, :])
                        dve.drain()
                        dve.tensor_scalar(step_u[:, :], reached[:, :], bit_f[:, bass.ds(k, 1)], None, ALU.mult)
                        dve.drain()
                        dve.tensor_tensor(thr[:, :], thr[:, :], step_u[:, :], ALU.bitwise_or)
                        dve.drain()
                t = thr[:, :].bitcast(F32)
                dve.tensor_scalar(above[:, :, :].rearrange("p a b -> p (a b)"), gates, t, None, ALU.is_gt)
                dve.tensor_scalar(equal[:, :, :].rearrange("p a b -> p (a b)"), gates, t, None, ALU.is_equal)
                dve.drain()
                for r, src in ((0, equal), (1, above)):
                    if r == 0:
                        dve.tensor_reduce(cnt[:, 0:1], above[:, :, :], AX.XY, ALU.add)
                    dve.tensor_reduce(cnt2[:, :], src[:, :, :], AX.X, ALU.add)
                    dve.drain().then_inc(s_c2, 1)
                    dve.wait_ge(s_off, r + 1)
                    dve.tensor_copy(start2[:, :], ps[:, 3, 1:3])
                    dve.tensor_scalar(need[:, :], ps[:, 3, 0:1], -1.0, float(CAP), ALU.mult, ALU.add)
                    dve.drain()
                    dve.tensor_tensor(start2[:, 1:2], start2[:, 1:2], ps[:, 3, 3:4], ALU.add)
                    dve.drain()
                    for a in range(2):
                        dve.tensor_tensor_scan(rank[:, a, :], src[:, a, :], zeros[:, :], start2[:, a:a + 1], ALU.add,
                                               ALU.max)
                    dve.drain()
                    if r == 0:
                        dve.scalar_tensor_tensor(equal[:, :, :], rank[:, :, :], need[:, :], equal[:, :, :], ALU.is_le,
                                                 ALU.mult)
                        dve.drain()
                        dve.tensor_tensor(above[:, :, :], above[:, :, :], equal[:, :, :], ALU.add)
                        dve.drain()
                dve.scalar_tensor_tensor(rank[:, :, :], rank[:, :, :], -1025.0, above[:, :, :], ALU.add, ALU.mult)
                dve.drain()
                dve.tensor_scalar(rank[:, :, :], rank[:, :, :], 1024.0, None, ALU.add)
                dve.drain().then_inc(s_sel, 1)
                dve.wait_ge(s_slT, 1)
                dve.tensor_copy(slot_i[:, 0].rearrange("p n e -> p (n e)"), ps[:, 4, 0:2 * P])
                dve.drain()
                dve.tensor_scalar(slot_i[:, 1], slot_i[:, 0], 31, None, ALU.bitwise_and)
                dve.drain()
                dve.tensor_scalar(slot_i[:, 0], slot_i[:, 0], 5, None, ALU.logical_shift_right)
                dve.drain()
                dve.tensor_copy(slot_f[:, :, :, :], slot_i[:, :, :, :])
                dve.drain()
                def one_hots(e):
                    dve.tensor_tensor(oh_lo[:, :, e, :], slot_f[:, 1, :, e].unsqueeze(2).to_broadcast([P, NTALL, 32]),
                                      iota_lo[:, :].unsqueeze(1).to_broadcast([P, NTALL, 32]), ALU.is_equal)
                    dve.tensor_tensor(oh_hi[:, :, e, 0, :], slot_f[:, 0, :, e].unsqueeze(2).to_broadcast([P, NTALL, 16]),
                                      iota_hi[:, :].unsqueeze(1).to_broadcast([P, NTALL, 16]), ALU.is_equal)

                def weigh(e):
                    dve.tensor_tensor(oh_hi[:, :, e, 1, :], oh_hi[:, :, e, 0, :],
                                      tile_no[:, :].unsqueeze(2).to_broadcast([P, NTALL, 16]), ALU.mult)
                    dve.drain()
                    dve.tensor_scalar(oh_hi[:, :, e, 0, :], oh_hi[:, :, e, 0, :], p_col[:, :], None, ALU.mult)
                    dve.drain().then_inc(s_oh, 1)

                one_hots(0)
                for e in range(E):
                    dve.drain()
                    if e + 1 < E:
                        one_hots(e + 1)
                    weigh(e)
                dve.wait_ge(s_ids, 1)
                dve.tensor_copy(ids_f[:, :, :, :].rearrange("p e a h -> p (e a h)"), ps[0:32, 5, 0:E * 32])
                dve.drain()
                dve.tensor_tensor(ids_f[:, :, 0, :], ids_f[:, :, 0, :], ids_f[:, :, 1, :], ALU.add)
                dve.drain()
                for q in range(CC):
                    dve.tensor_copy(ids[32 * q:32 * q + 32, :, :],
                                    ids_f[:, :, 0, :].rearrange("p e (c q) -> p e c q", q=4)[:, :, :, q])
                dve.drain()
                dve.tensor_scalar(bat_u[:, :, :], ids[:, :, :], 10, None, ALU.logical_shift_right)
                dve.drain()
                dve.tensor_copy(bat[:, :, :], bat_u[:, :, :])
                dve.drain()
                dve.tensor_tensor(of_b[:, :, :, :], bat[:, :, :].unsqueeze(3).to_broadcast([P, E, CC, B]),
                                  iota_hi[:, 0:B].unsqueeze(1).unsqueeze(1).to_broadcast([P, E, CC, B]), ALU.is_equal)
                dve.drain().then_inc(s_idx, 1)

        sel.close()
        idx_e = sb("idx_e", [P, 2, CC], U32)
        ofb_e = sb("ofb_e", [P, 2, CC, B])
        tok = sb("tok", [P, 2, CC, ROW])
        gbk = sb("gbk", [P, 2, CC, D])
        tok_t = sb("tok_t", [P, 2, KD, CAP])
        gate = sb("gate", [P, 2, CC])
        b1_e = sb("b1_e", [P, 2, FO])
        b2_e = sb("b2_e", [P, 2, D])
        h1_t = sb("h1_t", [P, FO, CAP])
        eo = sb("eo", [P, 2, D])
        ctr = sb("ctr", [P, 2, CC, D])
        s_w12 = [sem("s_w12_0"), sem("s_w12_1")]
        s_g = [sem("s_g0"), sem("s_g1")]
        s_sc = [sem("s_sc0"), sem("s_sc1")]
        s_tT, s_tt, s_L1, s_h1, s_L2, s_ctr, s_be = (sem(n) for n in (
            "s_tT", "s_tt", "s_L1", "s_h1", "s_L2", "s_ctr", "s_be"))
        s_L2free, s_done = sem("s_L2free"), sem("s_done")

        with nc.Block() as blk:
            @blk.sync
            def _(sp):
                with sp.Fori(0, E // 2 - 1) as ep:
                    for a in range(2):
                        e = 2 * ep + a
                        sp.wait_ge(s_L2, CC * (e + 1))
                        sp.dma_start(w1_sb[:, a], w1[bass.ds(e + 2, 1)].rearrange("o (k p) f -> p (o k) f", p=P)).then_inc(s_w12[a], 16)
                        sp.dma_start(w2_sb[:, a], w2[bass.ds(e + 2, 1)].rearrange("o (k p) f -> p (o k) f", p=P)).then_inc(s_w12[a], 16)

            @blk.gpsimd
            def _(pool):
                def gather(e, a):
                    pool.tensor_copy(idx_e[:, a, :], ids[:, bass.ds(e, 1), :].rearrange("p o c -> p (o c)"))
                    pool.drain()
                    for k in range(CC):
                        pool.indirect_dma_start(tok[:, a, k, :], None, h_table,
                                                bass.IndirectOffsetOnAxis(idx_e[:, a, k:k + 1], 0)).then_inc(s_g[a], 16)

                def scatter(e, a):
                    for k in range(CC):
                        pool.wait_ge(s_ctr, CC * e + k + 1)
                        pool.tensor_tensor(stand_p[:, :], ones_f[:, 0:1], ones_f[:, 0:1], ALU.add)
                        pool.drain()
                        pool.indirect_dma_start(out_rows, bass.IndirectOffsetOnAxis(idx_e[:, a, k:k + 1], 0),
                                                ctr[:, a, k, :], None, compute_op=ALU.add).then_inc(s_sc[a], 16)

                def scattered(ep, a):
                    pool.wait_ge(s_sc[a], 16 * CC * (ep + 1))
                    pool.tensor_tensor(stand_p[:, :], ones_f[:, 0:1], ones_f[:, 0:1], ALU.add)
                    pool.drain().then_inc(s_done, 1)

                for a in range(2):
                    gather(a, a)
                with pool.Fori(0, E // 2 - 1) as ep:
                    for a in range(2):
                        e = 2 * ep + a
                        scatter(e, a)
                        scattered(ep, a)
                        gather(e + 2, a)
                for a in range(2):
                    scatter(E - 2 + a, a)
                    scattered(E // 2 - 1, a)

            @blk.tensor
            def _(pe):
                def turn(e, a, nth):
                    pe.wait_ge(s_g[a], 16 * CC * nth)
                    for k in range(KD):
                        for q in range(CC):
                            m = pe.transpose(ps[:, k, q * P:(q + 1) * P], tok[:, a, q, k * P:(k + 1) * P], ident[:, :])
                    m.then_inc(s_tT, 1)

                def layer1(e, a):
                    pe.wait_ge(s_tt, e + 1)
                    for f in range(FO):
                        if f >= 2:
                            pe.wait_ge(s_h1, FO * e + f - 1)
                        for k in range(KD):
                            m = pe.matmul(ps[:, 2 + f % 2, :], w1_sb[:, a, k, f * P:(f + 1) * P], tok_t[:, a, k, :],
                                          start=k == 0, stop=k == KD - 1)
                        m.then_inc(s_L1, 1)

                def layer2(e, a):
                    pe.wait_ge(s_h1, FO * (e + 1))
                    for q in range(CC):
                        pe.wait_ge(s_L2free, CC * e + q + 1)
                        for f in range(FO):
                            m = pe.matmul(ps[:, 4 + q % 2, 0:D], h1_t[:, f, q * P:(q + 1) * P], w2_sb[:, a, f, :],
                                          start=f == 0, stop=f == FO - 1)
                        m.then_inc(s_L2, 1)

                turn(0, 0, 1)
                with pe.Fori(0, E // 2 - 1) as ep:
                    for a in range(2):
                        e = 2 * ep + a
                        pe.wait_ge(s_w12[a], 32 * ep + 1)
                        layer1(e, a)
                        turn(e + 1, 1 - a, ep + 1 + a)
                        layer2(e, a)
                for a in range(2):
                    pe.wait_ge(s_w12[a], 32 * (E // 2 - 1) + 1)
                    layer1(E - 2 + a, a)
                    if a == 0:
                        turn(E - 1, 1, E // 2)
                    layer2(E - 2 + a, a)

            @blk.scalar
            def _(act):
                act.drain().then_inc(s_w12[0], 1)
                act.drain().then_inc(s_w12[1], 1)
                with act.Fori(0, E // 2) as ep:
                    for a in range(2):
                        e = 2 * ep + a
                        act.wait_ge(s_be, e + 1)
                        for f in range(FO):
                            act.wait_ge(s_L1, FO * e + f + 1)
                            act.activation(h1_t[:, f, :], ps[:, 2 + f % 2, :], ACT.Relu,
                                           bias=b1_e[:, a, f:f + 1]).then_inc(s_h1, 1)

            @blk.vector
            def _(dve):
                dve.drain().then_inc(s_L2free, 2)
                dve.drain().then_inc(s_done, 2)

                def prepare(e, a):
                    dve.tensor_copy(b1_e[:, a, :], b1_t[:, bass.ds(e * FO, FO)])
                    dve.tensor_copy(b2_e[:, a, :], b2_sb[:, bass.ds(e, 1), :].rearrange("p o d -> p (o d)"))
                    dve.tensor_copy(ofb_e[:, a], of_b[:, bass.ds(e, 1)].rearrange("p o c b -> p (o c) b"))
                    dve.wait_ge(s_tT, e + 1)
                    dve.tensor_copy(tok_t[:, a], ps[:, 0:2, :])
                    dve.drain().then_inc(s_tt, 1)
                    dve.tensor_copy(gate[:, a, :], tok[:, a, :, bass.ds(D + e, 1)].rearrange("p c o -> p (c o)"))
                    dve.drain().then_inc(s_be, 1)

                def spread_gb(a):
                    for q in range(CC):
                        dve.tensor_scalar(gbk[:, a, q, :], gb_sb[:, 0, :], ofb_e[:, a, q, 0:1], None, ALU.mult)
                        for b in range(1, B):
                            dve.drain()
                            dve.scalar_tensor_tensor(gbk[:, a, q, :], gb_sb[:, b, :], ofb_e[:, a, q, b:b + 1],
                                                     gbk[:, a, q, :], ALU.mult, ALU.add)

                def finish(e, a):
                    dve.wait_ge(s_done, e + 1)
                    for q in range(CC):
                        dve.wait_ge(s_L2, CC * e + q + 1)
                        dve.tensor_tensor(eo[:, q % 2, :], ps[:, 4 + q % 2, 0:D], b2_e[:, a, :], ALU.add)
                        dve.drain().then_inc(s_L2free, 1)
                        dve.scalar_tensor_tensor(ctr[:, a, q, :], eo[:, q % 2, :], gate[:, a, q:q + 1],
                                                 gbk[:, a, q, :], ALU.mult, ALU.mult).then_inc(s_ctr, 1)

                prepare(0, 0)
                spread_gb(0)
                with dve.Fori(0, E // 2 - 1) as ep:
                    for a in range(2):
                        e = 2 * ep + a
                        prepare(e + 1, 1 - a)
                        finish(e, a)
                        spread_gb(1 - a)
                prepare(E - 1, 1)
                finish(E - 2, 0)
                spread_gb(1)
                finish(E - 1, 1)


_INS = ["L0_attn_x", "L0_attn_wq", "L0_attn_wk", "L0_attn_wv", "L0_attn_wo", "L0_ffn_router_w", "L0_ffn_router_b",
        "L0_ffn_w1", "L0_ffn_b1", "L0_ffn_w2", "L0_ffn_b2", "L0_c", "L0_wmod"]
_OUTS = [((B, T, D), "float32")]


def kernel(**inputs):
    import numpy as _np
    import concourse.bacc as _bacc
    from concourse import mybir as _mybir
    from concourse.bass_utils import run_bass_kernel_spmd as _run

    nc = _bacc.Bacc("TRN2", target_bir_lowering=False, num_devices=1)
    arrays, args = {}, []
    for name in _INS:
        a = _np.ascontiguousarray(inputs[name])
        arrays[f"in_{name}_dram"] = a
        args.append(nc.dram_tensor(f"in_{name}_dram", a.shape, _mybir.dt.from_np(a.dtype), kind="ExternalInput").ap())
    for i, (shape, dtype) in enumerate(_OUTS):
        dt = _mybir.dt.from_np(_np.dtype(dtype))
        args.append(nc.dram_tensor(f"out_{i}_dram", shape, dt, kind="ExternalOutput").ap())
    build_kernel(nc, *args)
    r = _run(nc, [arrays], core_ids=[0])
    return r.results[0]["out_0_dram"]
```
